# Optimizing a Trainium2 kernel written in Bass

```python
import numpy as np
import jax
import jax.numpy as jnp

def _softmax(x, axis=-1):
    return jax.nn.softmax(x, axis=axis)

def _gelu(x):
    return jax.nn.gelu(x, approximate=True)

def _silu(x):
    return jax.nn.silu(x)

def _sigmoid(x):
    return jax.nn.sigmoid(x)

def _layernorm(x, axis=-1, eps=1e-05):
    m = jnp.mean(x, axis=axis, keepdims=True)
    v = jnp.var(x, axis=axis, keepdims=True)
    return (x - m) / jnp.sqrt(v + eps)

def _scatter_add(tgt, idx, src, axis=0):
    return tgt.at[idx].add(src)

def _segment_sum(src, seg, n):
    return jax.ops.segment_sum(src, seg, n)
kernel_name = 'mk_decoder_preln_d2_seqx_r8_a91ad9'

def setup_inputs(seed: int=0):
    np.random.seed(seed)
    _w = jnp.asarray

    def _rec_inputs():
        import jax
        import jax.numpy as jnp
        _rk = jax.random.key(seed)
        x = -0.000125 + 0.9999 * jax.random.normal(jax.random.fold_in(_rk, 1), (4, 256, 256), jnp.float32)
        _lenS = 256 - jax.random.randint(jax.random.fold_in(_rk, 7), (4,), 0, max(1, 256 // 4) + 1, jnp.int32)
        _lenS2 = 256 - jax.random.randint(jax.random.fold_in(_rk, 8), (4,), 0, max(1, 256 // 4) + 1, jnp.int32)
        itok_BxS_13_99985 = jax.random.randint(jax.random.fold_in(_rk, 11), (4, 256), 13, 99986, jnp.int32)
        _ctx_2048P = jax.random.normal(jax.random.fold_in(_rk, 12), (4, 16, 256), jnp.float32)
        _ctx_2048c = jax.random.dirichlet(jax.random.fold_in(_rk, 512), 0.3 * jnp.ones((16,), jnp.float32), (4, 256))
        _ctx_2048t = jnp.einsum('bsk,bkd->bsd', _ctx_2048c, _ctx_2048P)
        _ctx_2048t = _ctx_2048t * jax.lax.rsqrt(jnp.mean(jnp.square(_ctx_2048t)) + 1e-12) * 0.953939
        ctx_2048 = 6.82029e-06 + 0.0200006 * (_ctx_2048t + 0.3 * jax.random.normal(jax.random.fold_in(_rk, 612), (4, 256, 256), jnp.float32))
        return (x, itok_BxS_13_99985, ctx_2048)
    x, itok_BxS_13_99985, ctx_2048 = _rec_inputs()

    def _L0_attn_setup():
        import jax, jax.numpy as jnp
        import numpy as np
        N_EMBD = 256
        Q_HEAD = 16
        KV_HEAD = 4
        HEAD_DIM = N_EMBD // Q_HEAD
        ROPE_BASE = 10000.0

        def _rope(Y, d_rope, base=ROPE_BASE):
            b, h, t, d = Y.shape
            mid = d_rope // 2
            Y1 = Y[:, :mid]
            Y2 = Y[:, mid:]
            Ym1 = jnp.concatenate([Y1, Y2], axis=1)
            Ym2 = jnp.concatenate([-Y2, Y1], axis=1)
            inv = base ** (-2.0 * jnp.arange(d // 2, dtype=jnp.float32) / d)
            theta = jnp.arange(t, dtype=jnp.float32)[:, None] * inv[None, :]
            cos2 = jnp.concatenate([jnp.cos(theta), jnp.cos(theta)], axis=1)
            sin2 = jnp.concatenate([jnp.sin(theta), jnp.sin(theta)], axis=1)
            return Ym1 * cos2 + Ym2 * sin2

        def _attention(x, Wq, bq, Wk, bk, Wv, bv, Wo, bo):
            b, t, n = x.shape
            hd = n // Q_HEAD
            q = x @ Wq.T + bq
            k = x @ Wk.T + bk
            v = x @ Wv.T + bv
            q = q.reshape(b, t, Q_HEAD, hd).transpose(0, 2, 1, 3)
            k = k.reshape(b, t, KV_HEAD, hd).transpose(0, 2, 1, 3)
            v = v.reshape(b, t, KV_HEAD, hd).transpose(0, 2, 1, 3)
            q = _rope(q, N_EMBD)
            k = _rope(k, N_EMBD)
            rep = Q_HEAD // KV_HEAD
            k = jnp.repeat(k, rep, axis=1)
            v = jnp.repeat(v, rep, axis=1)
            scale = jnp.sqrt(jnp.float32(hd))
            att = jnp.einsum('bhqd,bhkd->bhqk', q, k) / scale
            causal = jnp.tril(jnp.ones((t, t), dtype=bool))
            att = jnp.where(causal[None, None], att, -jnp.inf)
            att = jax.nn.softmax(att, axis=-1)
            y = jnp.einsum('bhqt,bhtd->bhqd', att, v)
            y = y.transpose(0, 2, 1, 3).reshape(b, t, n)
            return y @ Wo.T + bo
        key = jax.random.key(seed)
        ks = jax.random.split(key, 9)
        kv_dim = HEAD_DIM * KV_HEAD
        s = 1.0 / np.sqrt(N_EMBD)
        return {'x': jax.random.normal(ks[0], (4, 128, N_EMBD), jnp.float32), 'Wq': jax.random.normal(ks[1], (N_EMBD, N_EMBD), jnp.float32) * s, 'bq': jax.random.normal(ks[2], (N_EMBD,), jnp.float32) * 0.01, 'Wk': jax.random.normal(ks[3], (kv_dim, N_EMBD), jnp.float32) * s, 'bk': jax.random.normal(ks[4], (kv_dim,), jnp.float32) * 0.01, 'Wv': jax.random.normal(ks[5], (kv_dim, N_EMBD), jnp.float32) * s, 'bv': jax.random.normal(ks[6], (kv_dim,), jnp.float32) * 0.01, 'Wo': jax.random.normal(ks[7], (N_EMBD, N_EMBD), jnp.float32) * s, 'bo': jax.random.normal(ks[8], (N_EMBD,), jnp.float32) * 0.01}
    _L0_attn_all = _L0_attn_setup()
    _L0_attn_in = {k: v for k, v in _L0_attn_all.items() if k in ('Wq', 'bq', 'Wk', 'bk', 'Wv', 'bv', 'Wo', 'bo')}
    del _L0_attn_all

    def _L0_xattn_setup():
        import jax, jax.numpy as jnp
        import numpy as np
        B, S, D = (4, 512, 256)
        E = 4
        F = 1024 // E
        VOCAB = 12500
        key = jax.random.key(seed)
        k1, k2, k3, k4, k5 = jax.random.split(key, 5)
        hidden_states = jax.random.normal(k1, (B, S, D), dtype=jnp.float32)
        token_ids = jax.random.randint(k2, (B, S), 0, VOCAB, dtype=jnp.int64)
        Wg = jax.random.normal(k3, (E, F, D), dtype=jnp.float32) * 0.02
        Wu = jax.random.normal(k4, (E, F, D), dtype=jnp.float32) * 0.02
        Wd = jax.random.normal(k5, (E, D, F), dtype=jnp.float32) * 0.02
        return {'hidden_states': hidden_states, 'token_ids': token_ids, 'Wg': Wg, 'Wu': Wu, 'Wd': Wd}
    _L0_xattn_all = _L0_xattn_setup()
    _L0_xattn_in = {k: v for k, v in _L0_xattn_all.items() if k in ()}
    del _L0_xattn_all

    def _L0_ffn_setup():
        import jax, jax.numpy as jnp
        import numpy as np
        from jax import lax
        TOP_K = 2
        N_EXPERTS = 8
        key = jax.random.key(seed)
        ks = jax.random.split(key, 7)
        B, S, H, I, E = (4, 256, 256, 176, N_EXPERTS)
        s_h = 1.0 / np.sqrt(H)
        s_i = 1.0 / np.sqrt(I)
        return {'hidden_states': jax.random.normal(ks[0], (B, S, H), jnp.float32), 'gate_w': jax.random.normal(ks[1], (E, H), jnp.float32) * s_h, 'w1': jax.random.normal(ks[2], (E, H, 2 * I), jnp.float32) * s_h, 'w2': jax.random.normal(ks[3], (E, I, H), jnp.float32) * s_i, 'sw1': jax.random.normal(ks[4], (I, H), jnp.float32) * s_h, 'sw2': jax.random.normal(ks[5], (I, H), jnp.float32) * s_h, 'sw3': jax.random.normal(ks[6], (H, I), jnp.float32) * s_i}
    _L0_ffn_all = _L0_ffn_setup()
    _L0_ffn_in = {k: v for k, v in _L0_ffn_all.items() if k in ('gate_w', 'w1', 'w2', 'sw1', 'sw2', 'sw3')}
    del _L0_ffn_all

    def _L1_attn_setup():
        import jax, jax.numpy as jnp
        import numpy as np
        D_MODEL = 256
        D_INNER = 512
        D_STATE = 64
        N_QK_HEADS = 8
        N_V_HEADS = 64
        CHUNK = 128
        KSIZE = 4
        CONV_DIM = D_INNER + 2 * N_QK_HEADS * D_STATE
        PROJ_DIM = CONV_DIM + D_INNER + N_V_HEADS

        def segsum(x):
            T = x.shape[-1]
            xe = jnp.broadcast_to(x[..., None], x.shape + (T,))
            strict_lower = jnp.tril(jnp.ones((T, T), dtype=bool), -1)
            xe = jnp.where(strict_lower, xe, 0.0)
            s = jnp.cumsum(xe, axis=-2)
            lower = jnp.tril(jnp.ones((T, T), dtype=bool), 0)
            return jnp.where(lower, s, -jnp.inf)

        def ssd_chunk_scan(X, dA, Bm, Cm, chunk):
            b, l, h, p = X.shape
            g = Bm.shape[2]
            rep = h // g
            Bm = jnp.repeat(Bm, rep, axis=2)
            Cm = jnp.repeat(Cm, rep, axis=2)
            c = l // chunk
            X = X.reshape(b, c, chunk, h, p)
            Bm = Bm.reshape(b, c, chunk, h, -1)
            Cm = Cm.reshape(b, c, chunk, h, -1)
            A = jnp.transpose(dA.reshape(b, c, chunk, h), (0, 3, 1, 2))
            A_cum = jnp.cumsum(A, axis=-1)
            Lm = jnp.exp(segsum(A))
            Y_diag = jnp.einsum('bcshn,bczhn,bhcsz,bczhp->bcshp', Cm, Bm, Lm, X)
            decay_states = jnp.exp(A_cum[..., -1:] - A_cum)
            states = jnp.einsum('bcshn,bhcs,bcshp->bchpn', Bm, decay_states, X)
            states = jnp.concatenate([jnp.zeros_like(states[:, :1]), states], axis=1)
            chunk_sums = jnp.pad(A_cum[..., -1], ((0, 0), (0, 0), (1, 0)))
            decay_chunk = jnp.exp(segsum(chunk_sums))
            new_states = jnp.einsum('bhzc,bchpn->bzhpn', decay_chunk, states)
            states = new_states[:, :-1]
            state_decay_out = jnp.exp(A_cum)
            Y_off = jnp.einsum('bcshn,bchpn,bhcs->bcshp', Cm, states, state_decay_out)
            return (Y_diag + Y_off).reshape(b, l, h, p)
        key = jax.random.key(seed)
        ks = jax.random.split(key, 6)
        input_ = jax.random.normal(ks[0], (2, 512, D_MODEL), dtype=jnp.float32)
        in_proj_w = jax.random.normal(ks[1], (PROJ_DIM, D_MODEL), dtype=jnp.float32) * (2.0 / D_MODEL) ** 0.5
        cb = (CONV_DIM * KSIZE) ** (-0.5)
        conv1d_weight = jax.random.uniform(ks[2], (CONV_DIM, 1, KSIZE), dtype=jnp.float32, minval=-cb, maxval=cb)
        conv1d_bias = jax.random.uniform(ks[3], (CONV_DIM,), dtype=jnp.float32, minval=-0.5, maxval=0.5)
        z_bias = jnp.zeros((D_INNER,), dtype=jnp.float32)
        D = jnp.ones((N_V_HEADS,), dtype=jnp.float32)
        out_proj_w = jax.random.normal(ks[4], (D_MODEL, D_INNER), dtype=jnp.float32) * (2.0 / D_INNER) ** 0.5
        return {'input_': input_, 'in_proj_w': in_proj_w, 'conv1d_weight': conv1d_weight, 'conv1d_bias': conv1d_bias, 'z_bias': z_bias, 'D': D, 'out_proj_w': out_proj_w}
    _L1_attn_all = _L1_attn_setup()
    _L1_attn_in = {k: v for k, v in _L1_attn_all.items() if k in ('in_proj_w', 'conv1d_weight', 'conv1d_bias', 'z_bias', 'D', 'out_proj_w')}
    del _L1_attn_all

    def _L1_xattn_setup():
        import jax, jax.numpy as jnp
        import numpy as np
        HIDDEN = 256
        NUM_HEADS = 16
        HEAD_DIM = HIDDEN // NUM_HEADS
        CHUNK = 128
        SCALE = HEAD_DIM ** (-0.5)

        def _chunked_causal_attention(q, k, v):
            B, H, S, D = q.shape
            n_chunks = S // CHUNK
            kc = k.reshape(B, H, n_chunks, CHUNK, D).transpose(2, 0, 1, 3, 4)
            vc = v.reshape(B, H, n_chunks, CHUNK, D).transpose(2, 0, 1, 3, 4)
            j0s = jnp.arange(n_chunks) * CHUNK
            q_idx = jnp.arange(S)[:, None]
            k_off = jnp.arange(CHUNK)[None, :]
            out0 = jnp.zeros_like(q)
            m0 = jnp.full((B, H, S, 1), -jnp.inf, dtype=q.dtype)
            s0 = jnp.zeros((B, H, S, 1), dtype=q.dtype)

            def step(carry, inputs):
                out, m, s = carry
                kj, vj, j0 = inputs
                scores = jnp.einsum('bhqd,bhkd->bhqk', q, kj) * SCALE
                causal = j0 + k_off > q_idx
                scores = jnp.where(causal[None, None], -jnp.inf, scores)
                chunk_max = scores.max(axis=-1, keepdims=True)
                new_m = jnp.maximum(m, chunk_max)
                exp_old = jnp.exp(m - new_m)
                exp_c = jnp.exp(scores - new_m)
                new_s = s * exp_old + exp_c.sum(axis=-1, keepdims=True)
                out = out * (s / new_s) * exp_old + jnp.einsum('bhqk,bhkd->bhqd', exp_c / new_s, vj)
                return ((out, new_m, new_s), None)
            (out, _, _), _ = jax.lax.scan(step, (out0, m0, s0), (kc, vc, j0s))
            return out
        key = jax.random.key(seed)
        kq, kk, kv = jax.random.split(key, 3)
        B, S = (2, 512)
        return {'query': jax.random.normal(kq, (B, S, HIDDEN), dtype=jnp.float32), 'key': jax.random.normal(kk, (B, S, HIDDEN), dtype=jnp.float32), 'value': jax.random.normal(kv, (B, S, HIDDEN), dtype=jnp.float32)}
    _L1_xattn_all = _L1_xattn_setup()
    _L1_xattn_in = {k: v for k, v in _L1_xattn_all.items() if k in ()}
    del _L1_xattn_all

    def _L1_ffn_setup():
        import jax, jax.numpy as jnp
        import numpy as np
        TOP_K = 2
        key = jax.random.key(seed)
        ks = jax.random.split(key, 6)
        B, S, H, F, E = (1, 256, 256, 176, 8)
        Fs = 2 * F
        std = jnp.float32(0.02)
        return {'hidden_states': jax.random.normal(ks[0], (B, S, H), jnp.float32), 'gate_weight': jax.random.normal(ks[1], (E, H), jnp.float32) * std, 'gate_up_weights': jax.random.normal(ks[2], (E, 2 * F, H), jnp.float32) * std, 'down_weights': jax.random.normal(ks[3], (E, H, F), jnp.float32) * std, 'shared_gate_up': jax.random.normal(ks[4], (2 * Fs, H), jnp.float32) * std, 'shared_down': jax.random.normal(ks[5], (H, Fs), jnp.float32) * std}
    _L1_ffn_all = _L1_ffn_setup()
    _L1_ffn_in = {k: v for k, v in _L1_ffn_all.items() if k in ('gate_weight', 'gate_up_weights', 'down_weights', 'shared_gate_up', 'shared_down')}
    del _L1_ffn_all
    return {'x': x, 'itok_BxS_13_99985': itok_BxS_13_99985, 'ctx_2048': ctx_2048, 'L0_attn_Wq': _L0_attn_in['Wq'], 'L0_attn_bq': _L0_attn_in['bq'], 'L0_attn_Wk': _L0_attn_in['Wk'], 'L0_attn_bk': _L0_attn_in['bk'], 'L0_attn_Wv': _L0_attn_in['Wv'], 'L0_attn_bv': _L0_attn_in['bv'], 'L0_attn_Wo': _L0_attn_in['Wo'], 'L0_attn_bo': _L0_attn_in['bo'], 'L0_ffn_gate_w': _L0_ffn_in['gate_w'], 'L0_ffn_w1': _L0_ffn_in['w1'], 'L0_ffn_w2': _L0_ffn_in['w2'], 'L0_ffn_sw1': _L0_ffn_in['sw1'], 'L0_ffn_sw2': _L0_ffn_in['sw2'], 'L0_ffn_sw3': _L0_ffn_in['sw3'], 'L1_attn_in_proj_w': _L1_attn_in['in_proj_w'], 'L1_attn_conv1d_weight': _L1_attn_in['conv1d_weight'], 'L1_attn_conv1d_bias': _L1_attn_in['conv1d_bias'], 'L1_attn_z_bias': _L1_attn_in['z_bias'], 'L1_attn_D': _L1_attn_in['D'], 'L1_attn_out_proj_w': _L1_attn_in['out_proj_w'], 'L1_ffn_gate_weight': _L1_ffn_in['gate_weight'], 'L1_ffn_gate_up_weights': _L1_ffn_in['gate_up_weights'], 'L1_ffn_down_weights': _L1_ffn_in['down_weights'], 'L1_ffn_shared_gate_up': _L1_ffn_in['shared_gate_up'], 'L1_ffn_shared_down': _L1_ffn_in['shared_down']}

def reference(x, itok_BxS_13_99985, ctx_2048, L0_attn_Wq, L0_attn_bq, L0_attn_Wk, L0_attn_bk, L0_attn_Wv, L0_attn_bv, L0_attn_Wo, L0_attn_bo, L0_ffn_gate_w, L0_ffn_w1, L0_ffn_w2, L0_ffn_sw1, L0_ffn_sw2, L0_ffn_sw3, L1_attn_in_proj_w, L1_attn_conv1d_weight, L1_attn_conv1d_bias, L1_attn_z_bias, L1_attn_D, L1_attn_out_proj_w, L1_ffn_gate_weight, L1_ffn_gate_up_weights, L1_ffn_down_weights, L1_ffn_shared_gate_up, L1_ffn_shared_down):
    import jax
    import jax.numpy as jnp

    def _L0_attn_ref(x, Wq, bq, Wk, bk, Wv, bv, Wo, bo):
        import jax, jax.numpy as jnp
        import numpy as np
        N_EMBD = 256
        Q_HEAD = 16
        KV_HEAD = 4
        HEAD_DIM = N_EMBD // Q_HEAD
        ROPE_BASE = 10000.0

        def _rope(Y, d_rope, base=ROPE_BASE):
            b, h, t, d = Y.shape
            mid = d_rope // 2
            Y1 = Y[:, :mid]
            Y2 = Y[:, mid:]
            Ym1 = jnp.concatenate([Y1, Y2], axis=1)
            Ym2 = jnp.concatenate([-Y2, Y1], axis=1)
            inv = base ** (-2.0 * jnp.arange(d // 2, dtype=jnp.float32) / d)
            theta = jnp.arange(t, dtype=jnp.float32)[:, None] * inv[None, :]
            cos2 = jnp.concatenate([jnp.cos(theta), jnp.cos(theta)], axis=1)
            sin2 = jnp.concatenate([jnp.sin(theta), jnp.sin(theta)], axis=1)
            return Ym1 * cos2 + Ym2 * sin2

        def _attention(x, Wq, bq, Wk, bk, Wv, bv, Wo, bo):
            b, t, n = x.shape
            hd = n // Q_HEAD
            q = x @ Wq.T + bq
            k = x @ Wk.T + bk
            v = x @ Wv.T + bv
            q = q.reshape(b, t, Q_HEAD, hd).transpose(0, 2, 1, 3)
            k = k.reshape(b, t, KV_HEAD, hd).transpose(0, 2, 1, 3)
            v = v.reshape(b, t, KV_HEAD, hd).transpose(0, 2, 1, 3)
            q = _rope(q, N_EMBD)
            k = _rope(k, N_EMBD)
            rep = Q_HEAD // KV_HEAD
            k = jnp.repeat(k, rep, axis=1)
            v = jnp.repeat(v, rep, axis=1)
            scale = jnp.sqrt(jnp.float32(hd))
            att = jnp.einsum('bhqd,bhkd->bhqk', q, k) / scale
            causal = jnp.tril(jnp.ones((t, t), dtype=bool))
            att = jnp.where(causal[None, None], att, -jnp.inf)
            att = jax.nn.softmax(att, axis=-1)
            y = jnp.einsum('bhqt,bhtd->bhqd', att, v)
            y = y.transpose(0, 2, 1, 3).reshape(b, t, n)
            return y @ Wo.T + bo
        return _attention(x, Wq, bq, Wk, bk, Wv, bv, Wo, bo)

    def _L0_xattn_ref(hidden_states, token_ids, Wg, Wu, Wd):
        import jax, jax.numpy as jnp
        import numpy as np
        B, S, D = (4, 512, 256)
        E = 4
        F = 1024 // E
        VOCAB = 12500
        tokens_per_expert = VOCAB // E
        tid = jnp.clip(token_ids, 0, VOCAB - 1)
        expert_ids = jnp.minimum(tid // tokens_per_expert, E - 1)
        out = jnp.zeros_like(hidden_states)
        for e in range(E):
            g = jax.nn.silu(jnp.einsum('bsd,fd->bsf', hidden_states, Wg[e]))
            u = jnp.einsum('bsd,fd->bsf', hidden_states, Wu[e])
            y = jnp.einsum('bsf,df->bsd', g * u, Wd[e])
            out = jnp.where((expert_ids == e)[..., None], y, out)
        return out

    def _L0_ffn_ref(hidden_states, gate_w, w1, w2, sw1, sw2, sw3):
        import jax, jax.numpy as jnp
        import numpy as np
        from jax import lax
        TOP_K = 2
        N_EXPERTS = 8
        B, S, H = hidden_states.shape
        x = hidden_states.reshape(-1, H)
        T = x.shape[0]
        logits = jnp.einsum('th,eh->te', x.astype(jnp.float32), gate_w.astype(jnp.float32))
        scores = jax.nn.softmax(logits, axis=-1)
        topk_w, topk_idx = lax.top_k(scores, TOP_K)
        topk_w = topk_w / (topk_w.sum(-1, keepdims=True) + 1e-20)
        topk_w = topk_w.astype(hidden_states.dtype)
        cw = jnp.zeros((T, N_EXPERTS), hidden_states.dtype).at[jnp.arange(T)[:, None], topk_idx].add(topk_w)

        def body(acc, ew):
            w1e, w2e, cwe = ew
            h = x @ w1e
            g, u = jnp.split(h, 2, axis=-1)
            y = jax.nn.silu(g) * u @ w2e
            return (acc + cwe[:, None] * y, None)
        moe, _ = lax.scan(body, jnp.zeros_like(x), (w1, w2, cw.T))
        moe = moe.reshape(B, S, H)
        shared = jnp.einsum('bsi,hi->bsh', jax.nn.silu(jnp.einsum('bsh,ih->bsi', hidden_states, sw1)) * jnp.einsum('bsh,ih->bsi', hidden_states, sw2), sw3)
        return moe + shared

    def _L1_attn_ref(input_, in_proj_w, conv1d_weight, conv1d_bias, z_bias, D, out_proj_w):
        import jax, jax.numpy as jnp
        import numpy as np
        D_MODEL = 256
        D_INNER = 512
        D_STATE = 64
        N_QK_HEADS = 8
        N_V_HEADS = 64
        CHUNK = 128
        KSIZE = 4
        CONV_DIM = D_INNER + 2 * N_QK_HEADS * D_STATE
        PROJ_DIM = CONV_DIM + D_INNER + N_V_HEADS

        def segsum(x):
            T = x.shape[-1]
            xe = jnp.broadcast_to(x[..., None], x.shape + (T,))
            strict_lower = jnp.tril(jnp.ones((T, T), dtype=bool), -1)
            xe = jnp.where(strict_lower, xe, 0.0)
            s = jnp.cumsum(xe, axis=-2)
            lower = jnp.tril(jnp.ones((T, T), dtype=bool), 0)
            return jnp.where(lower, s, -jnp.inf)

        def ssd_chunk_scan(X, dA, Bm, Cm, chunk):
            b, l, h, p = X.shape
            g = Bm.shape[2]
            rep = h // g
            Bm = jnp.repeat(Bm, rep, axis=2)
            Cm = jnp.repeat(Cm, rep, axis=2)
            c = l // chunk
            X = X.reshape(b, c, chunk, h, p)
            Bm = Bm.reshape(b, c, chunk, h, -1)
            Cm = Cm.reshape(b, c, chunk, h, -1)
            A = jnp.transpose(dA.reshape(b, c, chunk, h), (0, 3, 1, 2))
            A_cum = jnp.cumsum(A, axis=-1)
            Lm = jnp.exp(segsum(A))
            Y_diag = jnp.einsum('bcshn,bczhn,bhcsz,bczhp->bcshp', Cm, Bm, Lm, X)
            decay_states = jnp.exp(A_cum[..., -1:] - A_cum)
            states = jnp.einsum('bcshn,bhcs,bcshp->bchpn', Bm, decay_states, X)
            states = jnp.concatenate([jnp.zeros_like(states[:, :1]), states], axis=1)
            chunk_sums = jnp.pad(A_cum[..., -1], ((0, 0), (0, 0), (1, 0)))
            decay_chunk = jnp.exp(segsum(chunk_sums))
            new_states = jnp.einsum('bhzc,bchpn->bzhpn', decay_chunk, states)
            states = new_states[:, :-1]
            state_decay_out = jnp.exp(A_cum)
            Y_off = jnp.einsum('bcshn,bchpn,bhcs->bcshp', Cm, states, state_decay_out)
            return (Y_diag + Y_off).reshape(b, l, h, p)
        b, L, _ = input_.shape
        xBCzA = jnp.einsum('bld,ed->ble', input_, in_proj_w)
        xBC = xBCzA[..., :CONV_DIM]
        z = xBCzA[..., CONV_DIM:CONV_DIM + D_INNER]
        A_log = xBCzA[..., CONV_DIM + D_INNER:]
        xt = jnp.transpose(xBC, (0, 2, 1))
        y = jax.lax.conv_general_dilated(xt, conv1d_weight, (1,), [(KSIZE - 1, 0)], feature_group_count=CONV_DIM, dimension_numbers=('NCH', 'OIH', 'NCH'))
        xBC = jax.nn.silu(jnp.transpose(y + conv1d_bias[None, :, None], (0, 2, 1)))
        x = xBC[..., :D_INNER].reshape(b, L, N_V_HEADS, D_INNER // N_V_HEADS)
        Bm = xBC[..., D_INNER:D_INNER + N_QK_HEADS * D_STATE].reshape(b, L, N_QK_HEADS, D_STATE)
        Cm = xBC[..., D_INNER + N_QK_HEADS * D_STATE:].reshape(b, L, N_QK_HEADS, D_STATE)
        dt = jax.nn.softplus(A_log)
        x_in = x / dt[..., None]
        y_ssm = ssd_chunk_scan(x_in * dt[..., None], -dt, Bm, Cm, CHUNK)
        Du = D[None, None, :, None] * x_in
        yf = (y_ssm + Du).reshape(b, L, D_INNER)
        out = jnp.einsum('bld,ed->ble', yf * jax.nn.silu(z + z_bias), out_proj_w)
        return out

    def _L1_xattn_ref(query, key, value):
        import jax, jax.numpy as jnp
        import numpy as np
        HIDDEN = 256
        NUM_HEADS = 16
        HEAD_DIM = HIDDEN // NUM_HEADS
        CHUNK = 128
        SCALE = HEAD_DIM ** (-0.5)

        def _chunked_causal_attention(q, k, v):
            B, H, S, D = q.shape
            n_chunks = S // CHUNK
            kc = k.reshape(B, H, n_chunks, CHUNK, D).transpose(2, 0, 1, 3, 4)
            vc = v.reshape(B, H, n_chunks, CHUNK, D).transpose(2, 0, 1, 3, 4)
            j0s = jnp.arange(n_chunks) * CHUNK
            q_idx = jnp.arange(S)[:, None]
            k_off = jnp.arange(CHUNK)[None, :]
            out0 = jnp.zeros_like(q)
            m0 = jnp.full((B, H, S, 1), -jnp.inf, dtype=q.dtype)
            s0 = jnp.zeros((B, H, S, 1), dtype=q.dtype)

            def step(carry, inputs):
                out, m, s = carry
                kj, vj, j0 = inputs
                scores = jnp.einsum('bhqd,bhkd->bhqk', q, kj) * SCALE
                causal = j0 + k_off > q_idx
                scores = jnp.where(causal[None, None], -jnp.inf, scores)
                chunk_max = scores.max(axis=-1, keepdims=True)
                new_m = jnp.maximum(m, chunk_max)
                exp_old = jnp.exp(m - new_m)
                exp_c = jnp.exp(scores - new_m)
                new_s = s * exp_old + exp_c.sum(axis=-1, keepdims=True)
                out = out * (s / new_s) * exp_old + jnp.einsum('bhqk,bhkd->bhqd', exp_c / new_s, vj)
                return ((out, new_m, new_s), None)
            (out, _, _), _ = jax.lax.scan(step, (out0, m0, s0), (kc, vc, j0s))
            return out
        B, S, _ = query.shape
        q = query.reshape(B, S, NUM_HEADS, HEAD_DIM).transpose(0, 2, 1, 3)
        k = key.reshape(B, S, NUM_HEADS, HEAD_DIM).transpose(0, 2, 1, 3)
        v = value.reshape(B, S, NUM_HEADS, HEAD_DIM).transpose(0, 2, 1, 3)
        out = _chunked_causal_attention(q, k, v)
        return out.transpose(0, 2, 1, 3).reshape(B, S, HIDDEN)

    def _L1_ffn_ref(hidden_states, gate_weight, gate_up_weights, down_weights, shared_gate_up, shared_down):
        import jax, jax.numpy as jnp
        import numpy as np
        TOP_K = 2
        B, S, H = hidden_states.shape
        E, twoF, _ = gate_up_weights.shape
        F = twoF // 2
        T = B * S
        x = hidden_states.reshape(T, H)
        logits = x @ gate_weight.T
        scores = jax.nn.softmax(logits, axis=-1)
        topk_w, topk_idx = jax.lax.top_k(scores, TOP_K)
        combine = jnp.zeros((T, E), x.dtype).at[jnp.arange(T)[:, None], topk_idx].add(topk_w)
        gu = jnp.einsum('th,efh->tef', x, gate_up_weights)
        act = jax.nn.silu(gu[..., :F]) * gu[..., F:]
        y = jnp.einsum('tef,te,ehf->th', act, combine, down_weights)
        Fs = shared_gate_up.shape[0] // 2
        sgu = x @ shared_gate_up.T
        sact = jax.nn.silu(sgu[:, :Fs]) * sgu[:, Fs:]
        y = y + sact @ shared_down.T
        return y.reshape(B, S, H)
    x = x + _L0_attn_ref(_layernorm(x, axis=-1), L0_attn_Wq, L0_attn_bq, L0_attn_Wk, L0_attn_bk, L0_attn_Wv, L0_attn_bv, L0_attn_Wo, L0_attn_bo)
    x = x + _L0_xattn_ref(_layernorm(x, axis=-1), itok_BxS_13_99985, ctx_2048, ctx_2048, ctx_2048)
    x = x + _L0_ffn_ref(_layernorm(x, axis=-1), L0_ffn_gate_w, L0_ffn_w1, L0_ffn_w2, L0_ffn_sw1, L0_ffn_sw2, L0_ffn_sw3)
    x = x + _L1_attn_ref(_layernorm(x, axis=-1), L1_attn_in_proj_w, L1_attn_conv1d_weight, L1_attn_conv1d_bias, L1_attn_z_bias, L1_attn_D, L1_attn_out_proj_w)
    x = x + _L1_xattn_ref(_layernorm(x, axis=-1), ctx_2048, ctx_2048)
    x = x + _L1_ffn_ref(_layernorm(x, axis=-1), L1_ffn_gate_weight, L1_ffn_gate_up_weights, L1_ffn_down_weights, L1_ffn_shared_gate_up, L1_ffn_shared_down)
    return x

_drawn_inputs = setup_inputs


def setup_inputs(seed=0):
    import zlib

    import numpy as np

    out = dict(_drawn_inputs(seed))
    spreads = {'L1_attn_z_bias': (0.0, 0.1), 'L1_attn_D': (1.0, 0.2)}
    factors = {'L0_attn_bq': 5.818,
     'L0_attn_bk': 3.277,
     'L1_ffn_gate_weight': 8.0,
     'L1_ffn_gate_up_weights': 8.0,
     'L1_ffn_down_weights': 8.0,
     'L1_ffn_shared_gate_up': 5.314,
     'L1_ffn_shared_down': 5.314}
    for name, (base, spread) in spreads.items():
        noise = np.random.default_rng([zlib.crc32(name.encode()), seed]).standard_normal(out[name].shape)
        drawn = base * np.exp(spread * noise) if base else spread * noise
        out[name] = jnp.asarray(drawn.astype(out[name].dtype))
    for name, factor in factors.items():
        out[name] = (out[name] * factor).astype(out[name].dtype)
    return out
```

```python
from contextlib import ExitStack

import numpy as np

import concourse.bass as bass
from concourse import mybir

ALU = mybir.AluOpType
ACT = mybir.ActivationFunctionType
AX = mybir.AxisListType
F32 = mybir.dt.float32
BF16 = mybir.dt.bfloat16
I32 = mybir.dt.int32
U32 = mybir.dt.uint32

P = 128
B, L, D = 4, 256, 256
TOK = B * L
NT = L // P
KD = D // P
EPS = 1e-5
NH, HD = 16, 16
NKV = 4
QSCALE = HD ** -0.5
NEG = -1e30
SLOTS = 6
KQ = SLOTS * HD
VW = HD + 1
VOCAB, E0 = 12500, 4
PER_EXPERT = VOCAB // E0
NE, FE = 8, 176
HALF = TOK // 2
TH = HALF // P
ROUTED = NE * FE // P
SHARED = {"C": 2, "F": 3}
WCOLS = KD * 2 * P + D
DI, NS, NG, NV = 512, 64, 8, 64
PV = DI // NV
CONV = DI + 2 * NG * NS
CT = CONV // P
KS = 4
HG = 4
NHG = NV // HG
RR = 3 + 3 * HG
RA = HG // 2 * 3 * NHG


def schedule(stages):
    steps = []
    after = {s: stages[i + 1] if i + 1 < len(stages) else None for i, s in enumerate(stages)}

    def norm(s, b):
        if after[s] is not None:
            steps.append(("ln", after[s], b))

    def turn(s, b):
        if s is not None and s != "E":
            steps.append(("lt", s, b))

    for b in range(B):
        steps.append(("ln", stages[0], b))
        turn(stages[0], b)
    late = []
    for s in stages:
        steps.append(("switch", s, 0))
        nxt = after[s]
        if s in "AE":
            def front(b):
                steps.append(("qkv_mm", s, b))
                steps.append(("qkv_split", s, b))
                steps.append(("stack_t", s, b))
            front(0)
            while late:
                turn(*late.pop(0))
            steps.append(("s", s, 0))
            steps.append(("m_split", s, 0))
            steps.append(("m_t", s, 0))
            front(1)
            for b in range(B):
                if b + 1 < B:
                    steps.append(("s", s, b + 1))
                    steps.append(("m_split", s, b + 1))
                    if b + 2 < B:
                        steps.append(("qkv_mm", s, b + 2))
                    steps.append(("m_t", s, b + 1))
                    if b + 2 < B:
                        steps.append(("qkv_split", s, b + 2))
                steps.append(("pv", s, b))
                if b + 2 < B:
                    steps.append(("stack_t", s, b + 2))
                steps.append(("o", s, b))
                norm(s, b)
                if b:
                    turn(nxt, b - 1)
            late.append((nxt, B - 1))
        elif s == "B":
            for hf in range(2):
                steps.append(("b_mask", s, hf))
                steps.append(("b_h", s, hf))
                while late:
                    turn(*late.pop(0))
                steps.append(("b_y", s, hf))
                for b in (2 * hf, 2 * hf + 1):
                    norm(s, b)
                    late.append((nxt, b))
        elif s in "CF":
            for hf in range(2):
                steps.append(("gate", s, hf))
                n = SHARED[s] + ROUTED
                for j in range(n + 1):
                    if j == 1:
                        steps.append(("cw_t", s, hf))
                    if j == 3:
                        while late:
                            turn(*late.pop(0))
                    steps.append(("moe", s, (hf, j)))
                steps.append(("moe_y", s, hf))
                for b in (2 * hf, 2 * hf + 1):
                    norm(s, b)
                    late.append((nxt, b))
        elif s == "D":
            def prep(u):
                return [("dz", s, u), ("dt", s, u), ("acum", s, u), ("at", s, u), ("xt", s, u)]
            for i in range(CT // 2):
                steps.append(("din", s, (0, i)))
            steps.extend(prep(0))
            steps.append(("cb", s, 0))
            while late:
                turn(*late.pop(0))
            for u in range(B * NT):
                b, c = divmod(u, NT)
                ahead = []
                if b + 1 < B:
                    ahead += [("din", s, (b + 1, 3 * c + i)) for i in range(3)]
                if u + 1 < B * NT:
                    ahead += prep(u + 1)
                cut = -(-len(ahead) // 4)
                for q in range(4):
                    steps.append(("ssd", s, (u, q)))
                    steps.extend(ahead[q * cut:(q + 1) * cut])
                if u + 1 < B * NT:
                    steps.append(("cb", s, u + 1))
                steps.append(("state", s, u))
                steps.append(("dy", s, u))
                if c == NT - 1:
                    norm(s, b)
                    if b:
                        turn(nxt, b - 1)
            late.append((nxt, B - 1))
    return steps



def number(steps):
    at = {r: {} for r in "TVAOGWY"}

    def fill(ring, *key):
        at[ring][key] = len(at[ring])

    for kind, s, i in steps:
        if kind in ("lt", "m_t", "gate", "cw_t", "acum", "at", "dy"):
            fill("T", kind, s, i)
        if kind == "dz":
            fill("V", kind, s, i)
            fill("T", kind, s, i)
        if kind == "qkv_mm" and s == "A":
            for t in range(NT):
                fill("V", kind, s, i, t)
        if kind == "s":
            for k in range(12):
                fill("V", kind, s, i, k)
        if kind == "stack_t":
            for t in range(NT):
                for k in range(3 if s == "A" else 4):
                    fill("A", kind, s, i, t, k)
        if kind == "pv":
            for k in range(12):
                fill("A", kind, s, i, k)
            for q in range(NT):
                fill("O", kind, s, i, q)
        if kind == "o" and s == "A":
            fill("T", kind, s, i)
            fill("V", kind, s, i)
        if kind == "b_h":
            for f in range(KD):
                fill("G", kind, s, i, f)
        if kind == "moe" and i[1] < SHARED[s] + ROUTED:
            fill("G", kind, s, *i)
            if i[1] >= SHARED[s]:
                fill("W", kind, s, *i)
        if kind in ("b_y", "moe_y"):
            for b in (2 * i, 2 * i + 1):
                fill("Y", s, b)
        if kind == "din":
            fill("A", kind, s, *i)
        if kind == "xt":
            fill("A", kind, s, i, 0)
            if i % 2 == 0:
                fill("A", kind, s, i, 1)
        if kind == "cb":
            for par in range(2):
                fill("V", kind, s, i, par)
        if kind == "ssd":
            for k in range(4):
                fill("A", kind, s, i[0], 4 * i[1] + k)
            if i[1] == 0:
                fill("O", kind, s, i[0])
        if kind == "state" and i % 2 == 0:
            fill("T", kind, s, i)
        if kind == "state" and i % 2 == 1:
            for par in range(2):
                fill("V", kind, s, i, par)
        if kind == "dy":
            fill("V", kind, s, i)
    return at


def decoder(nc, A, out, stages="ABCDEF"):
    steps = schedule(stages)
    at = number(steps)
    with ExitStack() as ctx:
        def sb(name, shape, dt=F32):
            return ctx.enter_context(nc.sbuf_tensor("s_" + name, shape, dt))

        def ps(name):
            return ctx.enter_context(nc.psum_tensor(name, [P, 512], F32))

        def sem(name):
            return ctx.enter_context(nc.semaphore(name))

        bank = [ps(f"bank{i}") for i in range(8)]
        V = bank[0:2]
        AR = [bank[2], bank[3], bank[6]]
        O = bank[4:6]
        T = bank[7]
        G = bank[0:4]
        CW = bank[4]
        Y = bank[5:7]

        x = sb("x", [P, B * NT, D])
        xn = sb("xn", [P, 2, NT, D])
        xnT = sb("xnT", [P, 2, KD, TOK])
        stats = sb("stats", [P, 2, NT, 6])
        mv = sb("mv", [P, 2, NT, 2])
        ve = sb("ve", [P, 2, NT])
        rstd = sb("rstd", [P, 2, NT])
        mhalf = sb("mhalf", [P, NT])
        ident = sb("ident", [P, P])
        identb = sb("identb", [P, P], BF16)
        masks = sb("masks", [P, 2 * P], BF16)
        maskt = sb("maskt", [P, P], BF16)
        ctxn = sb("ctxn", [P, B * NT, D])

        wqkv = sb("wqkv", [P, KD, 384])
        wo = sb("wo", [P, KD, D])
        bqkv = sb("bqkv", [P, 384])
        bo = sb("bo", [P, D])
        rope = sb("rope", [P, NT, 320])

        ctxT = sb("ctxT", [P, E0, KD, D])
        mask = sb("mask", [P, E0, TOK], BF16)

        NW = 3
        wmoe = sb("wmoe", [P, NW, WCOLS])
        gatew = sb("gatew", [P, 2, KD, NE])
        iota = sb("iota", [P, NE])
        sel = sb("sel", [3 * NE, ROUTED, P], BF16)
        lg = sb("lg", [P, TH, NE])
        g1 = sb("g1", [P, TH, NE])
        g2 = sb("g2", [P, TH, NE])
        gs = sb("gs", [P, TH])
        top = sb("top", [P, TH, NE])
        topi = sb("topi", [P, TH, NE], U32)
        topf = sb("topf", [P, TH, 2])
        cwp = sb("cwp", [P, TH, 3, NE], BF16)
        cwT = sb("cwT", [3 * NE, HALF], BF16)

        win = sb("win", [P, KD, CONV + DI + NV])
        wout = sb("wout", [P, DI // P, D])
        convw = sb("convw", [P, CT, KS + 1])
        zb = sb("zb", [P, DI])
        dskip = sb("dskip", [P, NV])
        tri = sb("tri", [P, 2, P])

        ARENA = 23600
        arena = sb("arena", [P, ARENA])
        at_ = [0]

        def cut(words, dt=F32, parts=P):
            a = arena[0:parts, at_[0]:at_[0] + words]
            at_[0] += words
            assert at_[0] <= ARENA, at_
            return a if dt is F32 else a.bitcast(dt)

        QT = cut(2 * NH * L // 2, BF16).rearrange("p (c h q) -> p c h q", c=2, h=NH)
        KT = cut(2 * NH * L // 2, BF16).rearrange("p (c h q) -> p c h q", c=2, h=NH)
        qf = cut(2 * 512).rearrange("p (c n) -> p c n", c=2)
        r1 = cut(512)
        stk = cut(2 * 32 * KQ // 2, BF16).rearrange("p (c h s d) -> p c h s d", c=2, h=32, s=SLOTS)
        vaug = cut(3 * NT * NH * VW).rearrange("p (c t g w) -> p c t g w", c=3, t=NT, g=NH)
        nM = cut(NT * NH).rearrange("p (t h) -> p t h", t=NT)
        mp = cut(NT * 2 * NH // 2, BF16).rearrange("p (t m h) -> p t m h", t=NT, m=2)
        MT = cut(L // 2, BF16, 2 * NH)
        NPT = 4
        PT = cut(NPT * 512).rearrange("p (c n) -> p c n", c=NPT)
        rs = cut(NT * NH).rearrange("p (t h) -> p t h", t=NT)
        y = cut(2 * NT * D).rearrange("p (c t d) -> p c t d", c=2, t=NT)
        yT = cut(KD * L).rearrange("p (k q) -> p k q", k=KD)
        attn_words = at_[0]

        at_[0] = 0
        xm = cut(E0 * KD * HALF).rearrange("p (e k t) -> p e k t", e=E0, k=KD)
        hb = cut(KD * HALF).rearrange("p (k t) -> p k t", k=KD)
        sg = cut(2 * HALF).rearrange("p (c t) -> p c t", c=2)
        NA = 3
        act_ = cut(NA * HALF).rearrange("p (c t) -> p c t", c=NA)
        tok32 = cut(TOK, I32)
        tokf = cut(TOK)
        gef = cut(3 * TOK // 2, BF16).rearrange("p (e t) -> p e t", e=3)

        at_[0] = 0
        NRAW = 2
        raw = cut(NRAW * 2 * (KS - 1 + L)).rearrange("p (c i t) -> p c i t", c=NRAW, i=2)
        xs = cut(2 * CT * L).rearrange("p (c i t) -> p c i t", c=2, i=CT)
        zt = cut(DI)
        zs = cut(2 * DI).rearrange("p (c n) -> p c n", c=2)
        dtb = cut(2 * 8 * NV).rearrange("p (c i h) -> p c i h", c=2, i=8)
        acs = cut(2 * 2 * NV).rearrange("p (c i h) -> p c i h", c=2, i=2)
        dec = cut(2 * NV).rearrange("p (c h) -> p c h", c=2)
        ap_ = cut(3 * NV // 2, BF16).rearrange("p (j m g) -> p j m g", j=HG, m=3)
        AT = cut(2 * P // 2, BF16, RA).rearrange("p (i s) -> p i s", i=2)
        nAT = cut(2 * P // 2, BF16, RA).rearrange("p (i s) -> p i s", i=2)
        rows_s = cut(NHG * HG * P // 2, BF16, RR).rearrange("p (j g s) -> p j g s", j=HG, g=NHG)
        rows_z = cut(NHG * P // 2, BF16, RR).rearrange("p (g z) -> p g z", g=NHG)
        Xt = cut(2 * DI).rearrange("p (c n) -> p c n", c=2)
        Bt = cut(DI)
        XD = cut(DI)
        Du = cut(2 * DI).rearrange("p (c n) -> p c n", c=2)
        CBs = cut(NG * P).rearrange("p (g s) -> p g s", g=NG)
        NM = 3
        M = cut(NM * 512).rearrange("p (c n) -> p c n", c=NM)
        stt = cut(NG // 2 * NS).rearrange("p (g n) -> p g n", g=NG // 2)
        yo = cut(DI)
        yf = cut(DI)
        yfT = cut(DI).rearrange("p (k q) -> p k q", k=DI // P)

        def sems(names):
            return [sem(n) for n in names.split()]

        x_in, const_in, attn_in, ctx_in, tok_in, gate_in, mix_in, hot_in = sems(
            "x_in const_in attn_in ctx_in tok_in gate_in mix_in hot_in")
        w_in = [sem(f"w_in{i}") for i in range(NW)]
        w_used, stored, init = sems("w_used stored init")
        dv, ac, pl = sems("dv ac pl")
        t_full, t_read, v_full, v_read, a_full, a_read, o_read = sems(
            "t_full t_read v_full v_read a_full a_read o_read")
        g_full, u_full, g_read, cw_full, cw_read, y_full, y_read = sems("g_full u_full g_read cw_full cw_read y_full y_read")
        ve_ready, rstd_ready, xn_ready = sems("ve_ready rstd_ready xn_ready")
        qk_ready, v_copied, parts_ready, stack_ready = sems("qk_ready v_copied parts_ready stack_ready")
        mp_ready, m_landed, pv_used, y_ready, attn_added = sems(
            "mp_ready m_landed pv_used y_ready attn_added")
        mask_ready, xm_ready, hb_ready, hm_ready, s_ready = sems("mask_ready xm_ready hb_ready hm_ready s_ready")
        gsub_ready, gexp_ready, cwp_ready = sems("gsub_ready gexp_ready cwp_ready")
        raw_cleared, conv_dve, conv_pool, xs_ready = sems("raw_cleared conv_dve conv_pool xs_ready")
        zs_ready, nab_ready, u_ready, w_ready, ln_ready, dt_ready = sems(
            "zs_ready nab_ready u_ready w_ready ln_ready dt_ready")
        ap_ready, decin_ready, dec_ready, rows_landed = sems("ap_ready decin_ready dec_ready rows_landed")
        du_ready, xd_ready, m_ready, m_used, yf_ready = sems("du_ready xd_ready m_ready m_used yf_ready")

        first = {s: i for i, s in enumerate(stages)}
        turned = [s for s in stages if s != "E"]
        attns = [s for s in stages if s in "AE"]

        def ln_index(s, b):
            return first[s] * B + b

        def attn_index(s, b):
            return attns.index(s) * B + b

        def xn_of(s, b):
            if s == "E":
                k = sum(t < s for t in turned) % 2
                return xnT[:, k].rearrange("p k t -> p (k t)").rearrange("p (n d) -> p n d", d=D)[:, NT * b:NT * b + NT, :]
            return xn[:, ln_index(s, b) % 2]

        def xnT_of(s):
            return xnT[:, turned.index(s) % 2]

        def added(s, b):
            if s in "AE":
                return attn_added, attn_index(s, b) + 1
            if s in "BCF":
                return y_read, at["Y"][s, b] + 1
            return v_read, at["V"]["dy", s, NT * b + 1] + 1

        def previous(s):
            return added(stages[first[s] - 1], B - 1)

        def on_pool(pair):
            return False

        def ssd_on_pool(hg):
            return hg % 4 == 3

        out_v = out.rearrange("b (t p) d -> p (b t) d", p=P)
        x_v = A["x"].rearrange("b (t p) d -> p (b t) d", p=P)
        ctx_v = A["ctx"].rearrange("b (t p) d -> p (b t) d", p=P)

        def row(name, n):
            return A[name].rearrange("(a n) -> a n", a=1).to_broadcast([P, n])

        block = ctx.enter_context(nc.Block())

        m_pool = sem("m_pool")

        def g_other(s):
            return sum(k[0] == "b_h" for k in at["G"])

        def conv(eng, e, s, i, ready):
            b, j = i
            n = b * (CT // 2) + j
            r = raw[:, n % NRAW]
            eng.wait_ge(a_read, at["A"]["din", s, b, j] + 1)
            if b >= 2:
                eng.wait_ge(v_read, at["V"]["dy", s, NT * (b - 2) + 1] + 1)
            for k in range(KS):
                for h in range(2):
                    ct = 2 * j + h
                    o = xs[:, b % 2, ct, :]
                    w = convw[:, ct, KS - 1 - k:KS - k]
                    src = r[:, h, KS - 1 - k:KS - 1 - k + L]
                    if k == 0:
                        ins = e.tensor_scalar(o, src, w, convw[:, ct, KS:KS + 1], ALU.mult, ALU.add)
                    else:
                        ins = e.scalar_tensor_tensor(o, src, w, o, ALU.mult, ALU.add)
                ins.then_inc(ready, 1)
                if k < KS - 1:
                    eng.wait_ge(ready, KS * conv_index(i) + k + 1)

        def conv_index(i):
            b, j = i
            mine = [on_pool(q) == on_pool(j) for q in range(CT // 2)]
            return b * sum(mine) + sum(mine[:j])

        def decayed(eng, e, s, i, mine):
            u, q = i
            for hg in range(4 * q, 4 * q + 4):
                if ssd_on_pool(hg) != mine:
                    continue
                k = NHG * u + hg
                if hg < 4:
                    eng.wait_ge(v_read, at["V"]["cb", s, u, 1] + 1)
                eng.wait_ge(a_read, at["A"]["ssd", s, u, hg] + 1)
                m = M[:, k % NM, :].rearrange("p (h z) -> p h z", h=HG)
                e.tensor_tensor(m, m, CBs[:, hg // (NV // NG):NG:NG // HG, :],
                                ALU.mult).then_inc(m_sem(hg), 1)

        def m_sem(hg):
            return m_pool if ssd_on_pool(hg) else m_ready

        def m_value(u, hg):
            mine = [ssd_on_pool(q) == ssd_on_pool(hg) for q in range(NHG)]
            return u * sum(mine) + sum(mine[:hg + 1])

        def silu(act, a, s, m):
            b, j = divmod(m, CT // 2)
            act.wait_ge(conv_pool if on_pool(j) else conv_dve, KS * (conv_index((b, j)) + 1))
            v = xs[:, b % 2, 2 * j:2 * j + 2, :]
            a.activation(v, v, ACT.Silu).then_inc(xs_ready, 1)

        def moe_half(s, hf):
            return 2 * (s == "F" and "C" in first) + hf

        def stage_of(ring, key):
            return key[0] if ring == "Y" else key[1]

        def w_all(s):
            return 2 * (SHARED[s] + ROUTED)

        def stack_end(k, t):
            s = attns[k // B]
            return at["A"]["stack_t", s, k % B, t, 2 if s == "A" else 3]

        @block.sync
        def _(sp):
            for b in range(B):
                sp.dma_start(x[:, NT * b:NT * b + NT, :], x_v[:, NT * b:NT * b + NT, :]).then_inc(x_in, 16)
            for dst, name in ((ident, "ident"), (identb, "identb"), (masks, "masks"), (maskt, "maskt")):
                sp.dma_start(dst[:, :], A[name]).then_inc(const_in, 16)
            for dst, name in ((wqkv, "wqkv"), (wo, "wo"), (rope, "rope")):
                sp.dma_start(dst[:, :, :], A[name]).then_inc(attn_in, 16)
            sp.dma_start(bqkv[:, :], row("bqkv", 384)).then_inc(attn_in, 16)
            sp.dma_start(bo[:, :], row("bo", D)).then_inc(attn_in, 16)
            sp.dma_start(ctxT[:, :, :, :], A["ctxT"]).then_inc(ctx_in, 16)
            sp.dma_start(ctxn[:, :, :], ctx_v).then_inc(ctx_in, 16)
            sp.dma_start(gatew[:, :, :, :], A["gatew"]).then_inc(gate_in, 16)
            sp.dma_start(iota[:, :], A["iota"]).then_inc(gate_in, 16)
            sp.dma_start(sel[:, :, :], A["sel"]).then_inc(gate_in, 16)
            sp.dma_start(win[:, :, :], A["win"]).then_inc(mix_in, 16)
            sp.dma_start(wout[:, :, :], A["wout"]).then_inc(mix_in, 16)
            sp.dma_start(convw[:, :, :], A["convw"]).then_inc(mix_in, 16)
            sp.dma_start(zb[:, :], row("zb", DI)).then_inc(mix_in, 16)
            sp.dma_start(dskip[:, :], row("dskip", NV)).then_inc(mix_in, 16)
            sp.dma_start(tri[:, :, :], A["tri"]).then_inc(mix_in, 16)
            for kind, s, i in steps:
                if kind == "m_t":
                    k = attn_index(s, i)
                    sp.wait_ge(t_read, at["T"]["m_t", s, i] + 1)
                    if k >= 2:
                        sp.wait_ge(pv_used, 8 * (k - 1))
                    for m in range(2):
                        sp.dma_start(QT[KQ + m:KQ + m + 1, k % 2, :, :],
                                     MT[m * NH:(m + 1) * NH, :]).then_inc(m_landed, 16)
                elif kind == "switch" and s == "B":
                    if first[s]:
                        sp.wait_ge(*previous(s))
                    sp.dma_start(tok32, row("tok", TOK)).then_inc(tok_in, 16)
                elif kind == "switch" and s == "D":
                    if first[s]:
                        sp.wait_ge(*previous(s))
                    sp.dma_start(rows_s[3:RR, :, :, :], A["onehot"]).then_inc(hot_in, 16)
                    sp.dma_start(rows_z[0:3, :, :], A["ones3"]).then_inc(hot_in, 16)
                elif kind == "moe" and i[1] < SHARED[s] + ROUTED:
                    k = at["G"]["moe", s, i[0], i[1]] - g_other(s)
                    if k >= NW:
                        sp.wait_ge(w_used, k - NW + 1)
                    sp.dma_start(wmoe[:, k % NW, :], A["w" + s][i[1]]).then_inc(w_in[k % NW], 16)
                elif kind == "at":
                    sp.wait_ge(t_read, at["T"]["at", s, i] + 1)
                    if i:
                        sp.wait_ge(a_full, at["A"]["ssd", s, i - 1, NHG - 1] + 1)
                    for j in range(HG):
                        h = 3 * NHG * (j % 2)
                        sp.dma_start(rows_s[0:3, j, :, :], AT[h:h + 3 * NHG, j // 2, :]).then_inc(rows_landed, 16)
                    for h in range(2):
                        sp.dma_start(rows_z[3 + 6 * h:9 + 6 * h, :, :], nAT[:, h, :]).then_inc(rows_landed, 16)
            for b in range(B):
                sp.wait_ge(*added(stages[-1], b))
                sp.dma_start(out_v[:, NT * b:NT * b + NT, :], x[:, NT * b:NT * b + NT, :]).then_inc(stored, 16)
            sp.wait_ge(stored, 16 * B)

        @block.gpsimd
        def _(pool):
            g = nc.gpsimd
            own = [0]

            def link(ins):
                own[0] += 1
                ins.then_inc(pl, 1)
                pool.wait_ge(pl, own[0])

            link(g.memset(mhalf[:, :], -0.5))
            for kind, s, i in steps:
                if kind == "ln":
                    n = ln_index(s, i)
                    pool.wait_ge(ve_ready, n + 1)
                    g.tensor_tensor(rstd[:, n % 2, :], ve[:, n % 2, :], mhalf[:, :], ALU.pow).then_inc(rstd_ready, 1)
                elif kind == "switch" and s in "AE":
                    if first[s]:
                        pool.wait_ge(*previous(s))
                    pool.wait_ge(rstd_ready, B * (first[s] + 1))
                    link(g.memset(KT[KQ:P, :, :, :], 1.0))
                    g.memset(vaug[:, :, :, :, HD:VW], 1.0).then_inc(init, 1)
                elif kind == "qkv_split":
                    k = attn_index(s, i)
                    nk = NKV if s == "A" else NH
                    for t in range(NT):
                        pool.wait_ge(qk_ready, NT * k + t + 1)
                        if k >= 3:
                            pool.wait_ge(pv_used, 8 * (k - 2))
                        src = qf[:, t, 320:384] if s == "A" else ctxn[:, NT * i + t, :]
                        g.tensor_copy(vaug[:, k % 3, t, 0:nk, 0:HD],
                                      src.rearrange("p (g w) -> p g w", g=nk)).then_inc(v_copied, 1)
                        pool.wait_ge(parts_ready, NT * k + t + 1)
                        st = stk[:, t]
                        g.tensor_copy(st[:, 0:NH, 1, :], st[:, 0:NH, 0, :])
                        g.tensor_copy(st[:, 0:NH, 3, :], st[:, 0:NH, 0, :])
                        g.tensor_copy(st[:, 0:NH, 2, :], st[:, 0:NH, 5, :])
                        g.tensor_copy(st[:, NH:NH + nk, 2, :], st[:, NH:NH + nk, 0, :])
                        g.tensor_copy(st[:, NH:NH + nk, 4, :], st[:, NH:NH + nk, 0, :])
                        g.tensor_copy(st[:, NH:NH + nk, 1, :], st[:, NH:NH + nk, 5, :]).then_inc(stack_ready, 1)
                elif kind == "b_mask":
                    pool.wait_ge(mask_ready, 1)
                    pool.wait_ge(t_read, at["T"]["lt", s, 2 * i + 1] + 1)
                    if i:
                        pool.wait_ge(y_full, at["Y"][s, 2 * i - 1] + 1)
                    for e in (2, 3):
                        g.tensor_tensor(xm[:, e], xnT_of(s)[:, :, i * HALF:(i + 1) * HALF],
                                        mask[:, e, i * HALF:(i + 1) * HALF].unsqueeze(1).to_broadcast([P, KD, HALF]),
                                        ALU.mult).then_inc(xm_ready, 1)
                elif kind == "b_h":
                    pool.wait_ge(hb_ready, i + 1)
                    for e in (2, 3):
                        g.tensor_tensor(xm[:, e], hb[:, :, :],
                                        mask[:, e, i * HALF:(i + 1) * HALF].unsqueeze(1).to_broadcast([P, KD, HALF]),
                                        ALU.mult).then_inc(hm_ready, 1)
                elif kind == "switch" and s == "D":
                    if first[s]:
                        pool.wait_ge(*previous(s))
                    g.memset(raw[:, :, :, 0:KS - 1], 0.0).then_inc(raw_cleared, 1)
                    pool.wait_ge(raw_cleared, 1)
                elif kind == "din" and on_pool(i[1]):
                    conv(pool, g, s, i, conv_pool)
                elif kind == "dt":
                    t = dtb[:, i % 2]
                    pool.wait_ge(t_read, at["T"]["dz", s, i] + 1)
                    if i >= 2:
                        pool.wait_ge(du_ready, i - 1)
                    link(g.tensor_scalar(t[:, 1, :], t[:, 0, :], -1.0, None, ALU.mult))
                    link(g.tensor_scalar(t[:, 6, :], t[:, 0, :], 0.0, None, ALU.max))
                    link(g.tensor_scalar(t[:, 5, :], t[:, 1, :], 0.0, None, ALU.max))
                    g.tensor_tensor(t[:, 1, :], t[:, 6, :], t[:, 5, :], ALU.add).then_inc(nab_ready, 1)
                    pool.wait_ge(u_ready, i + 1)
                    link(g.tensor_scalar(t[:, 3, :], t[:, 2, :], 1.0, None, ALU.add))
                    link(g.tensor_scalar(t[:, 4, :], t[:, 3, :], -1.0, None, ALU.add))
                    g.tensor_tensor(t[:, 4, :], t[:, 2, :], t[:, 4, :], ALU.subtract).then_inc(w_ready, 1)
                elif kind == "xt":
                    c = i % 2
                    pool.wait_ge(a_read, at["A"]["xt", s, i, 0] + 1)
                    pool.wait_ge(dt_ready, i + 1)
                    if i >= 2:
                        pool.wait_ge(yf_ready, i - 1)
                    g.tensor_tensor(Du[:, c, :].rearrange("p (h w) -> p h w", w=PV),
                                    Xt[:, c, :].rearrange("p (h w) -> p h w", w=PV),
                                    dtb[:, c, 7, :].unsqueeze(2).to_broadcast([P, NV, PV]), ALU.mult).then_inc(du_ready, 1)
                    if c == 0:
                        pool.wait_ge(dec_ready, i + 1)
                        if i:
                            pool.wait_ge(t_full, at["T"]["state", s, i - 2] + 1)
                        g.tensor_tensor(XD.rearrange("p (h w) -> p h w", w=PV),
                                        Xt[:, c, :].rearrange("p (h w) -> p h w", w=PV),
                                        dec[:, c, :].unsqueeze(2).to_broadcast([P, NV, PV]), ALU.mult).then_inc(xd_ready, 1)
                elif kind == "ssd":
                    decayed(pool, g, s, i, True)


        @block.scalar
        def _(act):
            a = nc.scalar
            own = [0]

            def link(ins):
                own[0] += 1
                ins.then_inc(ac, 1)
                act.wait_ge(ac, own[0])

            def start(s):
                if first[s]:
                    act.wait_ge(*previous(s))

            for kind, s, i in steps:
                if kind == "switch":
                    start(s)
                elif kind == "lt":
                    act.wait_ge(t_full, at["T"]["lt", s, i] + 1)
                    a.copy(xnT_of(s)[:, :, i * L:(i + 1) * L], T[:, :].rearrange("p (k q) -> p k q", k=KD)
                           ).then_inc(t_read, 1)
                elif kind == "stack_t":
                    k = attn_index(s, i)
                    if k >= 2:
                        act.wait_ge(pv_used, 8 * (k - 1))
                    for t in range(NT):
                        for j in range(3 if s == "A" else 4):
                            n = at["A"]["stack_t", s, i, t, j]
                            act.wait_ge(a_full, n + 1)
                            heads = 4 if j == 2 and s == "A" else 8
                            src = AR[n % 3][:, :].bitcast(BF16)[0:KQ, 0:heads * P].rearrange("p (h q) -> p h q", h=heads)
                            to = QT if j < 2 else KT
                            h0 = 8 * (j % 2)
                            a.copy(to[0:KQ, k % 2, h0:h0 + heads, t * P:(t + 1) * P], src).then_inc(a_read, 1)
                elif kind == "m_t":
                    k = attn_index(s, i)
                    act.wait_ge(t_full, at["T"]["m_t", s, i] + 1)
                    if k:
                        act.wait_ge(m_landed, 32 * k)
                    a.copy(MT[:, :], T[:, :].bitcast(BF16)[0:2 * NH, 0:L]).then_inc(t_read, 1)
                elif kind == "pv":
                    for j in range(12):
                        n = at["A"]["pv", s, i, j]
                        p = 12 * attn_index(s, i) + j
                        act.wait_ge(a_full, n + 1)
                        if p >= NPT:
                            kk, jj = divmod(p - NPT, 12)
                            act.wait_ge(pv_used, 8 * kk + 1 + (jj if jj < 4 else 4 + (jj - 4) // 2))
                        a.activation(PT[:, p % NPT, :], AR[n % 3][:, :], ACT.Exp).then_inc(a_read, 1)
                elif kind == "o" and s == "A":
                    act.wait_ge(t_full, at["T"]["o", s, i] + 1)
                    if i:
                        act.wait_ge(v_full, at["V"]["o", s, i - 1] + 1)
                    a.copy(yT[:, :, :], T[:, :].rearrange("p (k q) -> p k q", k=KD)).then_inc(t_read, 1)
                elif kind == "b_h":
                    for f in range(KD):
                        n = at["G"]["b_h", s, i, f]
                        act.wait_ge(g_full, n + 1)
                        if n >= 2:
                            act.wait_ge(g_read, n - 1)
                        a.activation(sg[:, n % 2, :], G[2 * (n % 2)][:, :], ACT.Silu).then_inc(s_ready, 1)
                elif kind == "gate":
                    act.wait_ge(t_full, at["T"]["gate", s, i] + 1)
                    h = 2 * (s == "F" and "C" in first) + i
                    if h:
                        act.wait_ge(cwp_ready, h)
                    a.copy(lg[:, :, :], T[:, 0:TH * NE].rearrange("p (t e) -> p t e", t=TH)).then_inc(t_read, 1)
                    act.wait_ge(gsub_ready, h + 1)
                    a.activation(g2[:, :, :], g1[:, :, :], ACT.Exp).then_inc(gexp_ready, 1)
                elif kind == "cw_t":
                    act.wait_ge(t_full, at["T"]["cw_t", s, i] + 1)
                    m = [v for (kk, ss, hh, jj), v in at["W"].items() if (ss, hh) < (s, i)]
                    if m:
                        act.wait_ge(cw_full, max(m) + 1)
                    a.copy(cwT[:, :], T[:, :].bitcast(BF16)[0:3 * NE, 0:HALF]).then_inc(t_read, 1)
                elif kind == "moe" and i[1] < SHARED[s] + ROUTED:
                    n = at["G"]["moe", s, i[0], i[1]]
                    act.wait_ge(g_full, n + 1)
                    if n >= 2:
                        act.wait_ge(g_read, n - 1)
                    a.activation(sg[:, n % 2, :], G[2 * (n % 2)][:, :], ACT.Silu).then_inc(s_ready, 1)
                elif kind == "din":
                    b, j = i
                    m = b * (CT // 2) + j
                    n = at["A"]["din", s, b, j]
                    act.wait_ge(a_full, n + 1)
                    if m >= NRAW:
                        bb, jj = divmod(m - NRAW, CT // 2)
                        act.wait_ge(conv_pool if on_pool(jj) else conv_dve, KS * (conv_index((bb, jj)) + 1))
                    a.copy(raw[:, m % NRAW, :, KS - 1:], AR[n % 3][:, :].rearrange("p (i t) -> p i t", i=2)
                           ).then_inc(a_read, 1)
                    if j:
                        silu(act, a, s, m - 1)
                elif kind == "dz":
                    if i % NT == 0:
                        silu(act, a, s, i // NT * (CT // 2) + CT // 2 - 1)
                    act.wait_ge(t_full, at["T"]["dz", s, i] + 1)
                    if i >= 2:
                        act.wait_ge(du_ready, i - 1)
                    a.copy(dtb[:, i % 2, 0, :], T[:, 0:NV]).then_inc(t_read, 1)
                    act.wait_ge(v_read, at["V"]["dz", s, i] + 1)
                    if i >= 2:
                        act.wait_ge(yf_ready, i - 1)
                    a.activation(zs[:, i % 2, :], zt[:, :], ACT.Silu).then_inc(zs_ready, 1)
                elif kind == "dt":
                    t = dtb[:, i % 2]
                    act.wait_ge(nab_ready, i + 1)
                    a.activation(t[:, 2, :], t[:, 1, :], ACT.Exp, scale=-1.0).then_inc(u_ready, 1)
                    act.wait_ge(w_ready, i + 1)
                    a.activation(t[:, 5, :], t[:, 3, :], ACT.Ln).then_inc(ln_ready, 1)
                elif kind == "acum":
                    act.wait_ge(t_full, at["T"]["acum", s, i] + 1)
                    if i >= 2:
                        act.wait_ge(yf_ready, i - 1)
                    a.copy(acs[:, i % 2, :, :], T[:, 0:2 * NV].rearrange("p (i h) -> p i h", i=2)).then_inc(t_read, 1)
                    act.wait_ge(decin_ready, i + 1)
                    a.activation(dec[:, i % 2, :], dec[:, i % 2, :], ACT.Exp).then_inc(dec_ready, 1)
                elif kind == "at":
                    act.wait_ge(t_full, at["T"]["at", s, i] + 1)
                    if i:
                        act.wait_ge(rows_landed, 16 * 6 * i)
                    src = T[:, :].bitcast(BF16)[0:RA, 0:2 * P].rearrange("p (i s) -> p i s", i=2)
                    a.copy(AT[:, :, :], src)
                    a.activation(nAT[:, :, :], src, ACT.Copy, scale=-1.0).then_inc(t_read, 1)
                elif kind == "xt":
                    n = at["A"]["xt", s, i, 0]
                    act.wait_ge(a_full, n + 1)
                    if i >= 2:
                        act.wait_ge(m_used, NHG * (i - 1))
                        act.wait_ge(du_ready, i - 1)
                    a.copy(Xt[:, i % 2, :], AR[n % 3][:, :]).then_inc(a_read, 1)
                    if i % 2 == 0:
                        n = at["A"]["xt", s, i, 1]
                        act.wait_ge(a_full, n + 1)
                        if i:
                            act.wait_ge(t_full, at["T"]["state", s, i - 2] + 1)
                        a.copy(Bt, AR[n % 3][:, :]).then_inc(a_read, 1)
                elif kind == "ssd":
                    u, q = i
                    for hg in range(4 * q, 4 * q + 4):
                        n = at["A"]["ssd", s, u, hg]
                        k = NHG * u + hg
                        act.wait_ge(a_full, n + 1)
                        if k >= NM:
                            act.wait_ge(m_used, k - NM + 1)
                        a.activation(M[:, k % NM, :], AR[n % 3][:, :], ACT.Exp).then_inc(a_read, 1)
                elif kind == "state" and i % 2 == 0:
                    act.wait_ge(t_full, at["T"]["state", s, i] + 1)
                    if i:
                        act.wait_ge(v_full, at["V"]["state", s, i - 1, 1] + 1)
                    a.copy(stt[:, :, :], T[:, 0:NG // 2 * NS].rearrange("p (g n) -> p g n", g=NG // 2)).then_inc(t_read, 1)
                elif kind == "dy":
                    act.wait_ge(t_full, at["T"]["dy", s, i] + 1)
                    if i:
                        act.wait_ge(v_full, at["V"]["dy", s, i - 1] + 1)
                    a.copy(yfT[:, :, :], T[:, :].rearrange("p (k q) -> p k q", k=DI // P)).then_inc(t_read, 1)

        @block.tensor
        def _(pe):
            mm = nc.tensor.matmul
            tr = nc.tensor.transpose

            def t_bank(*key):
                if at["T"][key]:
                    pe.wait_ge(t_read, at["T"][key])
                return T

            def v_bank(*key):
                n = at["V"][key]
                if n >= 2:
                    pe.wait_ge(v_read, n - 1)
                return V[n % 2]

            def a_bank(*key):
                n = at["A"][key]
                if n >= 3:
                    pe.wait_ge(a_read, n - 2)
                return AR[n % 3]

            def o_bank(*key):
                n = at["O"][key]
                if n >= 2:
                    pe.wait_ge(o_read, n - 1)
                return O[n % 2]

            def scan(s, u, hg):
                pe.wait_ge(m_sem(hg), m_value(u, hg))
                k = NHG * u + hg
                bk = O[at["O"]["ssd", s, u] % 2]
                for h in range(HG):
                    head = NHG * h + hg
                    ins = mm(bk[:, head * PV:(head + 1) * PV], M[:, k % NM, h * P:(h + 1) * P],
                             Xt[:, u % 2, head * PV:(head + 1) * PV], start=True, stop=True)
                ins.then_inc(m_used, 1)

            pe.wait_ge(const_in, 64)
            for kind, s, i in steps:
                if kind == "switch":
                    if first[s]:
                        pe.wait_ge(*previous(s))
                        for ring, read in (("V", v_read), ("A", a_read), ("O", o_read), ("G", g_read),
                                           ("W", cw_read), ("Y", y_read)):
                            done = sum(1 for key in at[ring] if stage_of(ring, key) in first
                                       and first[stage_of(ring, key)] < first[s])
                            if done:
                                pe.wait_ge(read, done)
                    if s == "A":
                        pe.wait_ge(attn_in, 80)
                    if s == "B":
                        pe.wait_ge(ctx_in, 32)
                    if s in "CF":
                        pe.wait_ge(gate_in, 48)
                    if s == "D":
                        pe.wait_ge(mix_in, 96)
                        pe.wait_ge(hot_in, 32)
                elif kind == "lt":
                    n = ln_index(s, i)
                    bk = t_bank("lt", s, i)
                    pe.wait_ge(xn_ready, n + 1)
                    for k in range(KD):
                        for t in range(NT):
                            ins = tr(bk[:, (k * NT + t) * P:(k * NT + t + 1) * P], xn_of(s, i)[:, t, k * P:(k + 1) * P],
                                     ident[:, :])
                    ins.then_inc(t_full, 1)
                elif kind == "qkv_mm" and s == "A":
                    pe.wait_ge(t_read, at["T"]["lt", s, i] + 1)
                    for t in range(NT):
                        bk = v_bank("qkv_mm", s, i, t)
                        for k in range(KD):
                            ins = mm(bk[:, 0:384], xnT_of(s)[:, k, i * L + t * P:i * L + (t + 1) * P], wqkv[:, k, :],
                                     start=(k == 0), stop=(k == KD - 1))
                        ins.then_inc(v_full, 1)
                elif kind == "stack_t":
                    kk = attn_index(s, i)
                    for t in range(NT):
                        pe.wait_ge(stack_ready, NT * kk + t + 1)
                        for j in range(3 if s == "A" else 4):
                            heads = 4 if j == 2 and s == "A" else 8
                            bk = a_bank("stack_t", s, i, t, j)
                            for h in range(heads):
                                ins = tr(bk[:, :].bitcast(BF16)[0:KQ, h * P:(h + 1) * P],
                                         stk[:, t, 8 * j + h, :, :].rearrange("p s d -> p (s d)"), identb[:, :])
                            ins.then_inc(a_full, 1)
                elif kind == "s":
                    c = attn_index(s, i) % 2
                    pe.wait_ge(a_read, at["A"]["stack_t", s, i, NT - 1, 2 if s == "A" else 3] + 1)
                    for j in range(12):
                        bk = v_bank("s", s, i, j)
                        if j < 4:
                            mm(bk[:, :], identb[:, :], masks[:, P:2 * P].unsqueeze(1).to_broadcast([P, 4, P]),
                               start=True, stop=False, skip_group_check=True)
                            for h in range(4 * j, 4 * j + 4):
                                g = h // (NH // NKV) if s == "A" else h
                                ins = mm(bk[:, (h % 4) * P:(h % 4 + 1) * P], QT[0:KQ, c, h, 0:P], KT[0:KQ, c, g, 0:P],
                                         start=False, stop=(h % 4 == 3), skip_group_check=True)
                        else:
                            mm(bk[:, :], identb[:, :], masks[:, :].unsqueeze(1).to_broadcast([P, 2, 2 * P]),
                               start=True, stop=False, skip_group_check=True)
                            for h in range(2 * (j - 4), 2 * (j - 4) + 2):
                                g = h // (NH // NKV) if s == "A" else h
                                ins = mm(bk[:, (h % 2) * L:(h % 2 + 1) * L], QT[0:KQ, c, h, P:L], KT[0:KQ, c, g, :],
                                         start=False, stop=(h % 2 == 1), skip_group_check=True)
                        ins.then_inc(v_full, 1)
                elif kind == "m_t":
                    k = attn_index(s, i)
                    bk = t_bank("m_t", s, i)
                    pe.wait_ge(mp_ready, k + 1)
                    for q in range(NT):
                        ins = tr(bk[:, :].bitcast(BF16)[0:2 * NH, q * P:(q + 1) * P],
                                 mp[:, q, :, :].rearrange("p m h -> p (m h)"), identb[:, :])
                    ins.then_inc(t_full, 1)
                elif kind == "pv":
                    ka = attn_index(s, i)
                    c = ka % 2
                    pe.wait_ge(m_landed, 32 * (ka + 1))
                    pe.wait_ge(v_copied, NT * (ka + 1))
                    pe.wait_ge(init, attns.index(s) + 1)
                    def scores(j):
                        q, kt, h4 = (0, 0, j) if j < 4 else (1, (j - 4) % 2, (j - 4) // 2)
                        bk = a_bank("pv", s, i, j)
                        diag = q == kt
                        if diag:
                            mm(bk[:, :], identb[:, :], maskt[:, :].unsqueeze(1).to_broadcast([P, 4, P]),
                               start=True, stop=False, skip_group_check=True)
                        if s == "A":
                            ins = mm(bk[:, :], KT[0:KQ + 2, c, h4, kt * P:(kt + 1) * P],
                                     QT[0:KQ + 2, c, 4 * h4:4 * h4 + 4, q * P:(q + 1) * P],
                                     start=not diag, stop=True, skip_group_check=True)
                        else:
                            for h in range(4 * h4, 4 * h4 + 4):
                                ins = mm(bk[:, (h % 4) * P:(h % 4 + 1) * P], KT[0:KQ + 2, c, h, kt * P:(kt + 1) * P],
                                         QT[0:KQ + 2, c, h, q * P:(q + 1) * P],
                                         start=not diag, stop=True, skip_group_check=True)
                        ins.then_inc(a_full, 1)

                    def values(j):
                        q, h4 = (0, j) if j < 4 else (1, j - 4)
                        kept = [12 * ka + j] if q == 0 else [12 * ka + 4 + 2 * h4, 12 * ka + 5 + 2 * h4]
                        bk = O[at["O"]["pv", s, i, q] % 2]
                        if h4 == 0:
                            o_bank("pv", s, i, q)
                        pe.wait_ge(a_read, at["A"]["pv", s, i, j if q == 0 else 5 + 2 * h4] + 1)
                        for h in range(4 * h4, 4 * h4 + 4):
                            g = h // (NH // NKV) if s == "A" else h
                            for kt in range(q + 1):
                                ins = mm(bk[:, h * VW:(h + 1) * VW], PT[:, kept[kt] % NPT, (h % 4) * P:(h % 4 + 1) * P],
                                         vaug[:, ka % 3, kt, g, :], start=(kt == 0), stop=(kt == q))
                        ins.then_inc(pv_used, 1)

                    scores(0)
                    for j in range(1, 4):
                        scores(j)
                        values(j - 1)
                    for h4 in range(4):
                        scores(4 + 2 * h4)
                        if h4 == 0:
                            values(3)
                        scores(5 + 2 * h4)
                        if h4:
                            values(4 + h4 - 1)
                    values(7)
                elif kind == "o" and s == "A":
                    k = attn_index(s, i)
                    bk = t_bank("o", s, i)
                    pe.wait_ge(y_ready, i + 1)
                    for d in range(KD):
                        for t in range(NT):
                            ins = tr(bk[:, (d * NT + t) * P:(d * NT + t + 1) * P], y[:, k % 2, t, d * P:(d + 1) * P],
                                     ident[:, :])
                    ins.then_inc(t_full, 1)
                    bk = v_bank("o", s, i)
                    pe.wait_ge(t_read, at["T"]["o", s, i] + 1)
                    for t in range(NT):
                        for d in range(KD):
                            ins = mm(bk[:, t * D:(t + 1) * D], yT[:, d, t * P:(t + 1) * P], wo[:, d, :],
                                     start=(d == 0), stop=(d == KD - 1))
                    ins.then_inc(v_full, 1)
                elif kind == "b_h":
                    pe.wait_ge(xm_ready, E0 * (i + 1))
                    for f in range(KD):
                        n = at["G"]["b_h", s, i, f]
                        if n >= 2:
                            pe.wait_ge(g_read, n - 1)
                        bk = G[2 * (n % 2)]
                        for e in range(E0):
                            for k in range(KD):
                                ins = mm(bk[:, :], ctxT[:, e, k, f * P:(f + 1) * P], xm[:, e, k, :],
                                         start=(e == 0 and k == 0), stop=(e == E0 - 1 and k == KD - 1))
                        ins.then_inc(g_full, 1)
                elif kind == "b_y":
                    pe.wait_ge(hm_ready, E0 * (i + 1))
                    for b in range(2):
                        n = at["Y"][s, 2 * i + b]
                        if n >= 2:
                            pe.wait_ge(y_read, n - 1)
                        for t in range(NT):
                            for e in range(E0):
                                for k in range(KD):
                                    ins = mm(Y[b][:, t * D:(t + 1) * D], xm[:, e, k, (b * NT + t) * P:(b * NT + t + 1) * P],
                                             ctxT[:, e, k, :], start=(e == 0 and k == 0), stop=(e == E0 - 1 and k == KD - 1))
                        ins.then_inc(y_full, 1)
                elif kind == "gate":
                    bk = t_bank("gate", s, i)
                    pe.wait_ge(t_read, at["T"]["lt", s, 2 * i + 1] + 1)
                    for t in range(TH):
                        for k in range(KD):
                            ins = mm(bk[:, t * NE:(t + 1) * NE], xnT_of(s)[:, k, (TH * i + t) * P:(TH * i + t + 1) * P],
                                     gatew[:, int(s == "F"), k, :], start=(k == 0), stop=(k == KD - 1))
                    ins.then_inc(t_full, 1)
                elif kind == "cw_t":
                    bk = t_bank("cw_t", s, i)
                    pe.wait_ge(cwp_ready, moe_half(s, i) + 1)
                    for t in range(TH):
                        ins = tr(bk[:, :].bitcast(BF16)[0:3 * NE, t * P:(t + 1) * P],
                                 cwp[:, t, :, :].rearrange("p m e -> p (m e)"), identb[:, :])
                    ins.then_inc(t_full, 1)
                elif kind == "moe":
                    hf, j = i
                    last = SHARED[s] + ROUTED
                    if j < last:
                        n = at["G"]["moe", s, hf, j]
                        w = n - g_other(s)
                        wt = wmoe[:, w % NW, 0:2 * KD * P].rearrange("p (k g f) -> p k g f", k=KD, g=2)
                        if n >= 2:
                            pe.wait_ge(g_read, n - 1)
                        pe.wait_ge(w_in[w % NW], 16 * (w // NW + 1))
                        for half, full in ((0, g_full), (1, u_full)):
                            for k in range(KD):
                                ins = mm(G[2 * (n % 2) + half][:, :], wt[:, k, half, :],
                                         xnT_of(s)[:, k, hf * HALF:(hf + 1) * HALF], start=(k == 0), stop=(k == KD - 1))
                            ins.then_inc(full, 1)
                        if j >= SHARED[s]:
                            m = at["W"]["moe", s, hf, j]
                            if m:
                                pe.wait_ge(cw_read, m)
                            if j == SHARED[s]:
                                pe.wait_ge(t_read, at["T"]["cw_t", s, hf] + 1)
                            mm(CW[:, :], sel[:, j - SHARED[s], :], cwT[:, :], start=True, stop=True).then_inc(cw_full, 1)
                    if j:
                        j -= 1
                        n = at["G"]["moe", s, hf, j]
                        w = n - g_other(s)
                        if j < SHARED[s]:
                            pe.wait_ge(g_read, n + 1)
                        else:
                            pe.wait_ge(cw_read, at["W"]["moe", s, hf, j] + 1)
                        if j == 0:
                            m = at["Y"][s, 2 * hf]
                            if m:
                                pe.wait_ge(y_read, m)
                        for t in range(TH):
                            ins = mm(Y[t // NT][:, (t % NT) * D:(t % NT + 1) * D], act_[:, w % NA, t * P:(t + 1) * P],
                                     wmoe[:, w % NW, 2 * KD * P:], start=(j == 0 and t % NT == 0), stop=(j == last - 1),
                                     skip_group_check=True)
                        ins.then_inc(w_used, 1)
                elif kind == "din":
                    b, j = i
                    bk = a_bank("din", s, b, j)
                    pe.wait_ge(t_read, at["T"]["lt", s, b] + 1)
                    for h in range(2):
                        ct = 2 * j + h
                        for k in range(KD):
                            ins = mm(bk[:, h * L:(h + 1) * L], win[:, k, ct * P:(ct + 1) * P],
                                     xnT_of(s)[:, k, b * L:(b + 1) * L], start=(k == 0), stop=(k == KD - 1))
                    ins.then_inc(a_full, 1)
                elif kind == "dz":
                    bz, bt_ = v_bank("dz", s, i), t_bank("dz", s, i)
                    for bk, lo, n, full in ((bt_, CONV + DI, NV, t_full), (bz, CONV, DI, v_full)):
                        for k in range(KD):
                            ins = mm(bk[:, 0:n], xnT_of(s)[:, k, i * P:(i + 1) * P], win[:, k, lo:lo + n],
                                     start=(k == 0), stop=(k == KD - 1))
                        ins.then_inc(full, 1)
                elif kind == "acum":
                    bk = t_bank("acum", s, i)
                    pe.wait_ge(dt_ready, i + 1)
                    for k in range(2):
                        ins = mm(bk[:, k * NV:(k + 1) * NV], tri[:, k, :], dtb[:, i % 2, 6, :], start=True, stop=True)
                    ins.then_inc(t_full, 1)
                elif kind == "at":
                    bk = t_bank("at", s, i)
                    pe.wait_ge(ap_ready, i + 1)
                    for h in range(2):
                        ins = tr(bk[:, :].bitcast(BF16)[0:RA, h * P:(h + 1) * P],
                                 ap_[:, 2 * h:2 * h + 2, :, :].rearrange("p j m g -> p (j m g)"), identb[:, :])
                    ins.then_inc(t_full, 1)
                elif kind == "xt":
                    b, c = divmod(i, NT)
                    pe.wait_ge(xs_ready, (CT // 2) * (b + 1))
                    for part in range(2 if c == 0 else 1):
                        bk = a_bank("xt", s, i, part)
                        for k in range(4):
                            ins = tr(bk[:, k * P:(k + 1) * P], xs[:, b % 2, 4 * part + k, c * P:(c + 1) * P], ident[:, :])
                        ins.then_inc(a_full, 1)
                elif kind == "cb":
                    b, c = divmod(i, NT)
                    for par in range(2):
                        bk = v_bank("cb", s, i, par)
                        rows = slice(NS * par, NS * par + NS)
                        for g2_ in range(NG // 2):
                            ins = mm(bk[:, g2_ * P:(g2_ + 1) * P], xs[rows, b % 2, 4 + g2_, c * P:(c + 1) * P],
                                     xs[rows, b % 2, 8 + g2_, c * P:(c + 1) * P], start=True, stop=True)
                        ins.then_inc(v_full, 1)
                elif kind == "ssd":
                    u, q = i
                    if q == 0:
                        pe.wait_ge(rows_landed, 16 * 6 * (u + 1))
                        o_bank("ssd", s, u)
                        pe.wait_ge(a_read, at["A"]["xt", s, u, 0] + 1)
                    for hg in range(4 * q, 4 * q + 4):
                        bk = a_bank("ssd", s, u, hg)
                        mm(bk[:, :], identb[:, :], maskt[:, :].unsqueeze(1).to_broadcast([P, HG, P]),
                           start=True, stop=False, skip_group_check=True)
                        mm(bk[:, :], rows_z[:, hg, :], rows_s[:, :, hg, :], start=False, stop=True,
                           skip_group_check=True).then_inc(a_full, 1)
                        if hg:
                            scan(s, u, hg - 1)
                    if q == 3:
                        scan(s, u, NHG - 1)
                elif kind == "state" and i % 2 == 0:
                    bk = t_bank("state", s, i)
                    pe.wait_ge(xd_ready, i // 2 + 1)
                    pe.wait_ge(a_read, at["A"]["xt", s, i, 1] + 1)
                    for g_ in range(NG):
                        lo = NS * (g_ % 2)
                        ins = mm(bk[lo:lo + NS, (g_ // 2) * NS:(g_ // 2 + 1) * NS], Bt[:, g_ * NS:(g_ + 1) * NS],
                                 XD[:, g_ * NS:(g_ + 1) * NS], start=True, stop=True)
                    ins.then_inc(t_full, 1)
                elif kind == "state":
                    b = i // NT
                    pe.wait_ge(t_read, at["T"]["state", s, i - 1] + 1)
                    for par in range(2):
                        bk = v_bank("state", s, i, par)
                        rows = slice(NS * par, NS * par + NS)
                        for g2_ in range(NG // 2):
                            ins = mm(bk[:, g2_ * NS:(g2_ + 1) * NS], xs[rows, b % 2, 8 + g2_, P:L], stt[rows, g2_, :],
                                     start=True, stop=True)
                        ins.then_inc(v_full, 1)
                elif kind == "dy":
                    bk = t_bank("dy", s, i)
                    pe.wait_ge(yf_ready, i + 1)
                    for k in range(DI // P):
                        ins = tr(bk[:, k * P:(k + 1) * P], yf[:, k * P:(k + 1) * P], ident[:, :])
                    ins.then_inc(t_full, 1)
                    bk = v_bank("dy", s, i)
                    pe.wait_ge(t_read, at["T"]["dy", s, i] + 1)
                    for k in range(DI // P):
                        ins = mm(bk[:, 0:D], yfT[:, k, :], wout[:, k, :], start=(k == 0), stop=(k == DI // P - 1))
                    ins.then_inc(v_full, 1)

        @block.vector
        def _(dve):
            v = nc.vector
            own = [0]

            def link(ins):
                own[0] += 1
                ins.then_inc(dv, 1)
                dve.wait_ge(dv, own[0])

            dve.wait_ge(x_in, 64)
            for kind, s, i in steps:
                if kind == "ln":
                    n = ln_index(s, i)
                    c = n % 2
                    if first[s]:
                        dve.wait_ge(*added(stages[first[s] - 1], i))
                    for t in range(NT):
                        link(v.bn_stats(stats[:, c, t, :], x[:, NT * i + t, :]))
                    for t in range(NT):
                        link(v.bn_aggr(mv[:, c, t, :], stats[:, c, t, :]))
                    v.tensor_scalar(ve[:, c, :], mv[:, c, :, 1], EPS, None, ALU.add).then_inc(ve_ready, 1)
                    dve.wait_ge(rstd_ready, n + 1)
                    if s != "E":
                        m = n - 2
                        if m >= 0 and stages[m // B] != "E":
                            dve.wait_ge(t_full, at["T"]["lt", stages[m // B], m % B] + 1)
                    for t in range(NT):
                        ins = v.tensor_scalar(xn_of(s, i)[:, t, :], x[:, NT * i + t, :], mv[:, c, t, 0:1], rstd[:, c, t:t + 1],
                                              ALU.subtract, ALU.mult)
                    ins.then_inc(xn_ready, 1)
                elif kind == "qkv_split":
                    k = attn_index(s, i)
                    nk = NKV if s == "A" else NH
                    wide = NH * HD + nk * HD
                    for t in range(NT):
                        if k:
                            dve.wait_ge(v_copied, NT * (k - 1) + t + 1)
                        q_ = qf[:, t, 0:wide]
                        if s == "A":
                            if k == 0:
                                dve.wait_ge(attn_in, 80)
                            n = at["V"]["qkv_mm", s, i, t]
                            dve.wait_ge(v_full, n + 1)
                            v.tensor_tensor(qf[:, t, 0:384], V[n % 2][:, 0:384], bqkv[:, :], ALU.add).then_inc(v_read, 1)
                            dve.wait_ge(v_read, n + 1)
                            v.tensor_tensor(q_, q_, rope[:, t, :], ALU.mult).then_inc(qk_ready, 1)
                        else:
                            if k % B == 0:
                                dve.wait_ge(ctx_in, 32)
                            dve.wait_ge(xn_ready, ln_index(s, i) + 1)
                            v.tensor_scalar(qf[:, t, 0:D], xn_of(s, i)[:, t, :], QSCALE, None, ALU.mult)
                            v.tensor_copy(qf[:, t, D:2 * D], ctxn[:, NT * i + t, :]).then_inc(qk_ready, 1)
                        dve.wait_ge(qk_ready, NT * k + t + 1)
                        if k:
                            dve.wait_ge(a_full, stack_end(k - 1, t) + 1)
                        st = stk[:, t]
                        heads = NH + nk
                        q3 = q_.rearrange("p (h w) -> p h w", w=HD)
                        r3 = r1[:, 0:wide].rearrange("p (h w) -> p h w", w=HD)
                        link(v.tensor_copy(st[:, 0:heads, 0, :], q3))
                        link(v.tensor_tensor(r3, q3, st[:, 0:heads, 0, :], ALU.subtract))
                        link(v.tensor_copy(st[:, 0:heads, 5, :], r3))
                        v.tensor_tensor(st[:, 0:NH, 4, :], r3[:, 0:NH], st[:, 0:NH, 5, :], ALU.subtract)
                        v.tensor_tensor(st[:, NH:heads, 3, :], r3[:, NH:heads], st[:, NH:heads, 5, :],
                                        ALU.subtract).then_inc(parts_ready, 1)
                elif kind == "s":
                    for j in range(12):
                        n = at["V"]["s", s, i, j]
                        dve.wait_ge(v_full, n + 1)
                        if j < 4:
                            v.tensor_reduce(nM[:, 0, 4 * j:4 * j + 4], V[n % 2][:, :].rearrange("p (h k) -> p h k", h=4),
                                            AX.X, ALU.max, negate=True).then_inc(v_read, 1)
                        else:
                            v.tensor_reduce(nM[:, 1, 2 * (j - 4):2 * (j - 4) + 2],
                                            V[n % 2][:, :].rearrange("p (h k) -> p h k", h=2),
                                            AX.X, ALU.max, negate=True).then_inc(v_read, 1)
                elif kind == "m_split":
                    k = attn_index(s, i)
                    dve.wait_ge(v_read, at["V"]["s", s, i, 11] + 1)
                    if k:
                        dve.wait_ge(t_full, at["T"]["m_t", attns[(k - 1) // B], (k - 1) % B] + 1)
                    link(v.tensor_copy(mp[:, :, 0, :], nM))
                    v.tensor_tensor(mp[:, :, 1, :], nM, mp[:, :, 0, :], ALU.subtract).then_inc(mp_ready, 1)
                elif kind == "pv":
                    k = attn_index(s, i)
                    for q in range(NT):
                        n = at["O"]["pv", s, i, q]
                        dve.wait_ge(pv_used, 8 * k + 4 * (q + 1))
                        o3 = O[n % 2][:, 0:NH * VW].rearrange("p (h w) -> p h w", w=VW)
                        link(v.reciprocal(rs[:, q, :].unsqueeze(2), o3[:, :, HD:VW]))
                        if s == "A" and q == 0 and i >= 2:
                            dve.wait_ge(t_full, at["T"]["o", s, i - 2] + 1)
                        v.tensor_tensor(y[:, k % 2, q, :].rearrange("p (h w) -> p h w", w=HD), o3[:, :, 0:HD],
                                        rs[:, q, :].unsqueeze(2).to_broadcast([P, NH, HD]), ALU.mult).then_inc(o_read, 1)
                    dve.wait_ge(o_read, at["O"]["pv", s, i, 1] + 1)
                    if s == "A":
                        v.tensor_copy(gs[:, 0:1], rs[:, 0, 0:1]).then_inc(y_ready, 1)
                elif kind == "o":
                    k = attn_index(s, i)
                    xb = x[:, NT * i:NT * i + NT, :]
                    if s == "A":
                        n = at["V"]["o", s, i]
                        dve.wait_ge(v_full, n + 1)
                        tmp = y[:, k % 2]
                        v.tensor_tensor(tmp, V[n % 2][:, :].rearrange("p (t d) -> p t d", t=NT),
                                        bo[:, :].unsqueeze(1).to_broadcast([P, NT, D]), ALU.add).then_inc(v_read, 1)
                        dve.wait_ge(v_read, n + 1)
                    v.tensor_tensor(xb, xb, y[:, k % 2], ALU.add).then_inc(attn_added, 1)
                elif kind == "b_mask":
                    if i == 0:
                        dve.wait_ge(tok_in, 16)
                        link(v.tensor_copy(tokf, tok32))
                        for e in range(1, E0):
                            link(v.tensor_scalar(gef[:, e - 1, :], tokf, float(PER_EXPERT * e), None, ALU.is_ge))
                        v.tensor_scalar(mask[:, 0, :], gef[:, 0, :], -1.0, 1.0, ALU.mult, ALU.add)
                        v.tensor_tensor(mask[:, 1, :], gef[:, 0, :], gef[:, 1, :], ALU.subtract)
                        v.tensor_tensor(mask[:, 2, :], gef[:, 1, :], gef[:, 2, :], ALU.subtract)
                        v.tensor_copy(mask[:, 3, :], gef[:, 2, :]).then_inc(mask_ready, 1)
                        dve.wait_ge(mask_ready, 1)
                    dve.wait_ge(t_read, at["T"]["lt", s, 2 * i + 1] + 1)
                    if i:
                        dve.wait_ge(y_full, at["Y"][s, 2 * i - 1] + 1)
                    for e in (0, 1):
                        v.tensor_tensor(xm[:, e], xnT_of(s)[:, :, i * HALF:(i + 1) * HALF],
                                        mask[:, e, i * HALF:(i + 1) * HALF].unsqueeze(1).to_broadcast([P, KD, HALF]),
                                        ALU.mult).then_inc(xm_ready, 1)
                elif kind == "b_h":
                    if i:
                        dve.wait_ge(hm_ready, E0 * i)
                    for f in range(KD):
                        n = at["G"]["b_h", s, i, f]
                        dve.wait_ge(s_ready, n + 1)
                        v.tensor_tensor(hb[:, f, :], G[2 * (n % 2)][:, :], sg[:, n % 2, :], ALU.mult).then_inc(g_read, 1)
                    dve.wait_ge(g_read, n + 1)
                    v.tensor_copy(gs[:, 0:1], rstd[:, 0, 0:1]).then_inc(hb_ready, 1)
                    for e in (0, 1):
                        v.tensor_tensor(xm[:, e], hb[:, :, :],
                                        mask[:, e, i * HALF:(i + 1) * HALF].unsqueeze(1).to_broadcast([P, KD, HALF]),
                                        ALU.mult).then_inc(hm_ready, 1)
                elif kind in ("b_y", "moe_y"):
                    for b in range(2):
                        n = at["Y"][s, 2 * i + b]
                        if kind == "b_y":
                            dve.wait_ge(y_full, n + 1)
                        else:
                            dve.wait_ge(w_used, (SHARED[s] + ROUTED) * (i + 1) + (w_all("C") if s == "F" and "C" in first else 0))
                        xb = x[:, NT * (2 * i + b):NT * (2 * i + b) + NT, :]
                        v.tensor_tensor(xb, xb, Y[b][:, :].rearrange("p (t d) -> p t d", t=NT), ALU.add).then_inc(y_read, 1)
                elif kind == "gate":
                    h = moe_half(s, i)
                    if h == 0:
                        dve.wait_ge(gate_in, 48)
                    dve.wait_ge(t_read, at["T"]["gate", s, i] + 1)
                    wide = [P, TH, NE]
                    link(v.tensor_reduce(gs[:, :], lg[:, :, :], AX.X, ALU.max))
                    v.tensor_tensor(g1[:, :, :], lg[:, :, :], gs[:, :].unsqueeze(2).to_broadcast(wide),
                                    ALU.subtract).then_inc(gsub_ready, 1)
                    dve.wait_ge(gexp_ready, h + 1)
                    link(v.tensor_reduce(gs[:, :], g2[:, :, :], AX.X, ALU.add))
                    link(v.reciprocal(gs[:, :], gs[:, :]))
                    link(v.tensor_tensor(g1[:, :, :], g2[:, :, :], gs[:, :].unsqueeze(2).to_broadcast(wide), ALU.mult))
                    for t in range(TH):
                        link(v.max(top[:, t, :], g1[:, t, :]))
                        link(v.max_index(topi[:, t, :], top[:, t, :], g1[:, t, :]))
                    link(v.tensor_copy(topf[:, :, :], topi[:, :, 0:2]))
                    io = iota[:, :].unsqueeze(1).to_broadcast(wide)
                    link(v.tensor_tensor(g2[:, :, :], io, topf[:, :, 0:1].to_broadcast(wide), ALU.is_equal))
                    link(v.tensor_tensor(lg[:, :, :], io, topf[:, :, 1:2].to_broadcast(wide), ALU.is_equal))
                    link(v.tensor_tensor(g2[:, :, :], g2[:, :, :], lg[:, :, :], ALU.add))
                    link(v.tensor_tensor(g1[:, :, :], g1[:, :, :], g2[:, :, :], ALU.mult))
                    if s == "C":
                        link(v.tensor_reduce(gs[:, :], g1[:, :, :], AX.X, ALU.add))
                        link(v.tensor_scalar(gs[:, :], gs[:, :], 1e-20, None, ALU.add))
                        link(v.reciprocal(gs[:, :], gs[:, :]))
                        link(v.tensor_tensor(g1[:, :, :], g1[:, :, :], gs[:, :].unsqueeze(2).to_broadcast(wide), ALU.mult))
                    link(v.tensor_copy(cwp[:, :, 0, :], g1[:, :, :]))
                    link(v.tensor_tensor(g2[:, :, :], g1[:, :, :], cwp[:, :, 0, :], ALU.subtract))
                    link(v.tensor_copy(cwp[:, :, 1, :], g2[:, :, :]))
                    v.tensor_tensor(cwp[:, :, 2, :], g2[:, :, :], cwp[:, :, 1, :], ALU.subtract).then_inc(cwp_ready, 1)
                elif kind == "moe" and i[1] < SHARED[s] + ROUTED:
                    hf, j = i
                    n = at["G"]["moe", s, hf, j]
                    w = n - g_other(s)
                    dve.wait_ge(u_full, w + 1)
                    dve.wait_ge(s_ready, n + 1)
                    if w >= NA:
                        dve.wait_ge(w_used, w - NA + 1)
                    v.tensor_tensor(act_[:, w % NA, :], G[2 * (n % 2) + 1][:, :], sg[:, n % 2, :], ALU.mult).then_inc(g_read, 1)
                    if j >= SHARED[s]:
                        m = at["W"]["moe", s, hf, j]
                        dve.wait_ge(cw_full, m + 1)
                        dve.wait_ge(g_read, n + 1)
                        v.tensor_tensor(act_[:, w % NA, :], act_[:, w % NA, :], CW[:, :], ALU.mult).then_inc(cw_read, 1)
                elif kind == "switch" and s == "D":
                    dve.wait_ge(mix_in, 96)
                    dve.wait_ge(raw_cleared, 1)
                elif kind == "din" and not on_pool(i[1]):
                    conv(dve, v, s, i, conv_dve)
                elif kind == "dz":
                    n = at["V"]["dz", s, i]
                    dve.wait_ge(v_full, n + 1)
                    if i:
                        dve.wait_ge(zs_ready, i)
                    v.tensor_tensor(zt[:, :], V[n % 2][:, :], zb[:, :], ALU.add).then_inc(v_read, 1)
                elif kind == "dt":
                    t = dtb[:, i % 2]
                    dve.wait_ge(w_ready, i + 1)
                    link(v.reciprocal(t[:, 7, :], t[:, 3, :]))
                    link(v.tensor_tensor(t[:, 4, :], t[:, 4, :], t[:, 7, :], ALU.mult))
                    dve.wait_ge(ln_ready, i + 1)
                    link(v.tensor_tensor(t[:, 4, :], t[:, 4, :], t[:, 5, :], ALU.add))
                    link(v.tensor_tensor(t[:, 6, :], t[:, 4, :], t[:, 6, :], ALU.add))
                    link(v.reciprocal(t[:, 7, :], t[:, 6, :]))
                    v.tensor_tensor(t[:, 7, :], t[:, 7, :], dskip[:, :], ALU.mult).then_inc(dt_ready, 1)
                elif kind == "acum":
                    c = i % 2
                    dve.wait_ge(t_read, at["T"]["acum", s, i] + 1)
                    if i:
                        dve.wait_ge(t_full, at["T"]["at", s, i - 1] + 1)
                    if i >= 2:
                        dve.wait_ge(yf_ready, i - 1)
                        if c == 0:
                            dve.wait_ge(xd_ready, i // 2)
                    cum, last = acs[:, c, 0, :], acs[:, c, 1, :]
                    if c == 0:
                        v.tensor_tensor(dec[:, c, :], last, cum, ALU.subtract).then_inc(decin_ready, 1)
                    else:
                        v.tensor_copy(dec[:, c, :], cum).then_inc(decin_ready, 1)
                    cum = cum.rearrange("p (j g) -> p j g", j=HG)
                    rest = dtb[:, c, 5, :].rearrange("p (j g) -> p j g", j=HG)
                    link(v.tensor_copy(ap_[:, :, 0, :], cum))
                    link(v.tensor_tensor(rest, cum, ap_[:, :, 0, :], ALU.subtract))
                    link(v.tensor_copy(ap_[:, :, 1, :], rest))
                    v.tensor_tensor(ap_[:, :, 2, :], rest, ap_[:, :, 1, :], ALU.subtract).then_inc(ap_ready, 1)
                elif kind == "cb":
                    if i:
                        dve.wait_ge(m_pool, m_value(i - 1, NHG - 1))
                    for par in range(2):
                        n = at["V"]["cb", s, i, par]
                        dve.wait_ge(v_full, n + 1)
                        v.tensor_copy(CBs[:, par:NG:2, :], V[n % 2][:, :].rearrange("p (g s) -> p g s", g=NG // 2)
                                      ).then_inc(v_read, 1)
                elif kind == "ssd":
                    decayed(dve, v, s, i, False)
                elif kind == "state" and i % 2 == 1:
                    dve.wait_ge(dec_ready, i + 1)
                    for par in range(2):
                        n = at["V"]["state", s, i, par]
                        dve.wait_ge(v_full, n + 1)
                        o4 = yo.rearrange("p (g j h w) -> p g j h w", g=NG // 2, j=2, w=PV)[:, :, par]
                        e4 = dec[:, 1, :].rearrange("p (g j h) -> p g j h", g=NG // 2, j=2)[:, :, par]
                        for g_ in range(NG // 2):
                            ins = v.tensor_tensor(o4[:, g_], V[n % 2][:, g_ * NS:(g_ + 1) * NS].rearrange("p (h w) -> p h w", w=PV),
                                                  e4[:, g_].unsqueeze(2).to_broadcast([P, NG, PV]), ALU.mult)
                        ins.then_inc(v_read, 1)
                elif kind == "dy":
                    b, c = divmod(i, NT)
                    n = at["O"]["ssd", s, i]
                    dve.wait_ge(m_used, NHG * (i + 1))
                    dve.wait_ge(du_ready, i + 1)
                    dve.wait_ge(zs_ready, i + 1)
                    if i:
                        dve.wait_ge(t_full, at["T"]["dy", s, i - 1] + 1)
                    v.tensor_tensor(yf, O[n % 2][:, :], Du[:, c, :], ALU.add).then_inc(o_read, 1)
                    dve.wait_ge(o_read, n + 1)
                    if c:
                        dve.wait_ge(v_read, at["V"]["state", s, i, 1] + 1)
                        link(v.tensor_tensor(yf, yf, yo, ALU.add))
                    v.tensor_tensor(yf, yf, zs[:, c, :], ALU.mult).then_inc(yf_ready, 1)
                    n = at["V"]["dy", s, i]
                    dve.wait_ge(v_full, n + 1)
                    v.tensor_tensor(x[:, i, :], x[:, i, :], V[n % 2][:, 0:D], ALU.add).then_inc(v_read, 1)


def layouts(inp):

    bf = np.dtype("bfloat16")
    f = {k: np.asarray(v) for k, v in inp.items()}

    def rows(w):
        return np.ascontiguousarray(w.reshape(-1, P, w.shape[1]).transpose(1, 0, 2))

    arrays = {
        "x": f["x"], "ctx": f["ctx_2048"], "tok": f["itok_BxS_13_99985"].reshape(-1),
        "wqkv": rows(np.concatenate([f["L0_attn_Wq"].T, f["L0_attn_Wk"].T, f["L0_attn_Wv"].T], 1)),
        "wo": rows(f["L0_attn_Wo"].T),
        "bqkv": np.concatenate([f["L0_attn_bq"], f["L0_attn_bk"], f["L0_attn_bv"]]),
        "bo": f["L0_attn_bo"],
        "ctxT": np.ascontiguousarray(f["ctx_2048"].transpose(0, 2, 1).reshape(E0, KD, P, D).transpose(2, 0, 1, 3)),
        "gatew": np.ascontiguousarray(np.stack([rows(f["L0_ffn_gate_w"].T), rows(f["L1_ffn_gate_weight"].T)], 1)),
        "win": rows(f["L1_attn_in_proj_w"].T),
        "wout": rows(f["L1_attn_out_proj_w"].T),
        "zb": f["L1_attn_z_bias"], "dskip": f["L1_attn_D"],
        "convw": np.ascontiguousarray(np.concatenate([f["L1_attn_conv1d_weight"][:, 0, :], f["L1_attn_conv1d_bias"][:, None]],
                                                     1).reshape(CT, P, KS + 1).transpose(1, 0, 2)),
    }

    def tiles(gate, up, down, n):
        pad = n * P - gate.shape[1]
        gate, up = (np.pad(w, ((0, 0), (0, pad))).reshape(KD, P, n, P) for w in (gate, up))
        down = np.pad(down, ((0, pad), (0, 0))).reshape(n, P, D)
        gu = np.stack([gate, up], 3).transpose(2, 1, 0, 3, 4).reshape(n, P, 2 * KD * P)
        return np.concatenate([gu, down], 2)

    def cat(w):
        return w.transpose(1, 0, 2).reshape(D, NE * FE)

    w1 = f["L0_ffn_w1"]
    arrays["wC"] = np.ascontiguousarray(np.concatenate([
        tiles(f["L0_ffn_sw1"].T, f["L0_ffn_sw2"].T, f["L0_ffn_sw3"].T, SHARED["C"]),
        tiles(cat(w1[:, :, :FE]), cat(w1[:, :, FE:]), f["L0_ffn_w2"].reshape(NE * FE, D), ROUTED)]))
    gu, sgu = f["L1_ffn_gate_up_weights"], f["L1_ffn_shared_gate_up"]
    fs = sgu.shape[0] // 2
    arrays["wF"] = np.ascontiguousarray(np.concatenate([
        tiles(sgu[:fs].T, sgu[fs:].T, f["L1_ffn_shared_down"].T, SHARED["F"]),
        tiles(cat(gu[:, :FE].transpose(0, 2, 1)), cat(gu[:, FE:].transpose(0, 2, 1)),
              f["L1_ffn_down_weights"].transpose(0, 2, 1).reshape(NE * FE, D), ROUTED)]))

    i = np.arange(P)
    arrays["ident"] = np.eye(P, dtype=np.float32)
    arrays["identb"] = np.eye(P).astype(bf)
    later = np.where(i[None, :] > i[:, None], NEG, 0.0)
    arrays["masks"] = np.concatenate([np.zeros((P, P)), later], 1).astype(bf)
    arrays["maskt"] = later.T.astype(bf)
    inv = np.float32(10000.0) ** (np.float32(-2.0) * np.arange(HD // 2, dtype=np.float32) / np.float32(HD))
    theta = np.arange(L, dtype=np.float32)[:, None] * inv[None, :].astype(np.float32)
    turn = np.tile(np.cos(theta) + np.sin(theta), (1, 2)).astype(np.float32)
    arrays["rope"] = np.ascontiguousarray(np.concatenate([np.tile(turn * np.float32(QSCALE), (1, NH)), np.tile(turn, (1, NKV))],
                                                         1).reshape(NT, P, -1).transpose(1, 0, 2))
    expert = (np.arange(ROUTED * P) // FE).reshape(ROUTED, P)
    arrays["sel"] = np.tile(expert[None] == np.arange(NE)[:, None, None], (3, 1, 1)).astype(bf)
    arrays["iota"] = np.tile(np.arange(NE, dtype=np.float32), (P, 1))
    arrays["tri"] = np.stack([-(i[:, None] <= i[None, :]).astype(np.float32), -np.ones((P, P), np.float32)], 1)
    arrays["onehot"] = np.tile(np.repeat(np.eye(HG), 3, 0)[:, :, None, None], (1, 1, NHG, P)).astype(bf)
    arrays["ones3"] = np.ones((3, NHG, P)).astype(bf)
    return arrays


def kernel(**inputs):
    import concourse.bacc as bacc
    from concourse.bass_utils import run_bass_kernel_spmd

    nc = bacc.Bacc("TRN2", target_bir_lowering=False, num_devices=1)
    arrays = layouts(inputs)
    args = {n: nc.dram_tensor(f"in_{n}", a.shape, mybir.dt.from_np(a.dtype), kind="ExternalInput").ap()
            for n, a in arrays.items()}
    out = nc.dram_tensor("out_x", (B, L, D), F32, kind="ExternalOutput").ap()
    decoder(nc, args, out)
    r = run_bass_kernel_spmd(nc, [{f"in_{n}": a for n, a in arrays.items()}], core_ids=[0])
    return r.results[0]["out_x"]
```

```python
from contextlib import ExitStack

import numpy as np

import concourse.bass as bass
from concourse import mybir

ALU = mybir.AluOpType
ACT = mybir.ActivationFunctionType
AX = mybir.AxisListType
F32 = mybir.dt.float32
BF16 = mybir.dt.bfloat16
I32 = mybir.dt.int32
U32 = mybir.dt.uint32

P = 128
B, L, D = 4, 256, 256
TOK = B * L
NT = L // P
KD = D // P
EPS = 1e-5
NH, HD = 16, 16
NKV = 4
QSCALE = HD ** -0.5
NEG = -1e30
SLOTS = 6
KQ = SLOTS * HD
VW = 32
VOCAB, E0 = 12500, 4
PER_EXPERT = VOCAB // E0
NE, FE = 8, 176
HALF = TOK // 2
TH = HALF // P
ROUTED = NE * FE // P
SHARED = {"C": 2, "F": 3}
EARLY = KD * (384 + D) + E0 * KD * D + E0 * TOK // 2
WCOLS = KD * 2 * P + D
DI, NS, NG, NV = 512, 64, 8, 64
PV = DI // NV
CONV = DI + 2 * NG * NS
CT = CONV // P
KS = 4
NB = 12
HG = 4
NHG = NV // HG
LAG = 2
RR = 3 + 3 * HG
RA = HG // 2 * 3 * NHG


def schedule(stages):
    steps = []
    after = {s: stages[i + 1] if i + 1 < len(stages) else None for i, s in enumerate(stages)}

    def norm(s, b):
        if after[s] is not None:
            steps.append(("ln", after[s], b))

    def turn(s, b):
        if s is not None and s != "E":
            steps.append(("lt", s, b))

    for b in range(B):
        steps.append(("ln", stages[0], b))
        turn(stages[0], b)
    late = []
    for s in stages:
        steps.append(("switch", s, 0))
        nxt = after[s]
        if s in "AE":
            steps.append(("qkv_mm", s, 0))
            steps.append(("qkv_split", s, 0))
            while late:
                turn(*late.pop(0))
            steps.append(("qkv_mm", s, 1))
            steps.append(("stack_t", s, 0))
            steps.append(("qkv_split", s, 1))
            for k in range(NB):
                steps.append(("s", s, (0, k)))
            steps.append(("m_split", s, 0))
            steps.append(("m_t", s, 0))
            steps.append(("stack_t", s, 1))
            for b in range(B):
                for k in range(NB):
                    if b + 1 < B:
                        steps.append(("s", s, (b + 1, k)))
                        if k == NB - 1:
                            steps.append(("m_split", s, b + 1))
                    if k == 4 and b + 2 < B:
                        steps.append(("qkv_mm", s, b + 2))
                    steps.append(("pv", s, (b, k)))
                    if k == 4 and b + 2 < B:
                        steps.append(("qkv_split", s, b + 2))
                    if k == 1 and b:
                        steps.append(("o_t", s, b - 1))
                    if k == 3 and b:
                        steps.append(("o", s, b - 1))
                        norm(s, b - 1)
                    if k == 6:
                        steps.append(("y_t", s, (b, 0)))
                    if k == 9 and b:
                        turn(nxt, b - 1)
                if b + 1 < B:
                    steps.append(("m_t", s, b + 1))
                steps.append(("y_t", s, (b, 1)))
                if b + 2 < B:
                    steps.append(("stack_t", s, b + 2))
            steps.append(("o_t", s, B - 1))
            steps.append(("o", s, B - 1))
            norm(s, B - 1)
            late.append((nxt, B - 1))
        elif s == "B":
            for hf in range(2):
                steps.append(("b_mask", s, hf))
                steps.append(("b_h", s, hf))
                while late:
                    turn(*late.pop(0))
                steps.append(("b_y", s, hf))
                for b in (2 * hf, 2 * hf + 1):
                    norm(s, b)
                    late.append((nxt, b))
        elif s in "CF":
            for hf in range(2):
                steps.append(("gate", s, hf))
                n = SHARED[s] + ROUTED
                for j in range(n + 1):
                    if j == 1:
                        steps.append(("cw_t", s, hf))
                    if j == 3:
                        while late:
                            turn(*late.pop(0))
                    steps.append(("moe", s, (hf, j)))
                steps.append(("moe_y", s, hf))
                for b in (2 * hf, 2 * hf + 1):
                    norm(s, b)
                    late.append((nxt, b))
        elif s == "D":
            steps.append(("dz", s, 0))
            for i in range(CT // 2):
                steps.append(("din", s, (0, i)))
                if i < 3:
                    steps.append((("dt", "acum", "at")[i], s, 0))
            while late:
                turn(*late.pop(0))
            steps.append(("zs", s, 0))
            steps.append(("xt", s, 0))
            steps.append(("cb", s, 0))
            units = B * NT
            for u in range(units + 1):
                b, c = divmod(u, NT)
                beside = {}
                if u:
                    beside[LAG] = [("y_t", s, u - 1)]
                    beside[LAG + 1] = [("dy_t", s, u - 1)]
                    beside[LAG + 3] = [("dy", s, u - 1)]
                if u < units:
                    beside.setdefault(1, []).append(("state", s, u))
                if u < units and b + 1 < B:
                    for i in range(3):
                        beside.setdefault(4 * i + 1, []).append(("din", s, (b + 1, 3 * c + i)))
                if u + 1 < units:
                    for hg, kind in ((4, "dz"), (5, "dt"), (8, "acum"), (10, "at"), (11, "zs"), (13, "xt"), (14, "cb")):
                        beside.setdefault(hg, []).append((kind, s, u + 1))
                for hg in range(NHG if u < units else LAG + 4):
                    if u < units:
                        steps.append(("ssd", s, (u, hg)))
                    elif hg == 0:
                        steps.append(("ssd_end", s, units))
                    steps.extend(beside.get(hg, []))
                if c == 0 and b:
                    norm(s, b - 1)
                    if b > 1:
                        turn(nxt, b - 2)
            turn(nxt, B - 2)
            late.append((nxt, B - 1))
    return steps



def number(steps):
    at = {r: {} for r in "TVAOGWY"}

    def fill(ring, *key):
        at[ring][key] = len(at[ring])

    for kind, s, i in steps:
        if kind in ("lt", "m_t", "gate", "cw_t", "acum", "at", "dy_t"):
            fill("T", kind, s, i)
        if kind == "dz":
            fill("V", kind, s, i)
            fill("T", kind, s, i)
        if kind == "qkv_mm" and s == "A":
            for t in range(NT):
                fill("V", kind, s, i, t)
        if kind == "s":
            fill("V", kind, s, *i)
        if kind == "stack_t":
            for t in range(NT):
                for k in range(3 if s == "A" else 4):
                    fill("A", kind, s, i, t, k)
        if kind == "pv":
            fill("A", kind, s, *i)
            if i[1] in (0, 4):
                fill("O", kind, s, i[0], i[1] // 4)
        if kind == "y_t":
            fill("V", kind, s, i)
        if kind == "o_t" and s == "A":
            fill("T", kind, s, i)
        if kind == "o" and s == "A":
            fill("V", kind, s, i)
        if kind == "b_h":
            for f in range(KD):
                fill("G", kind, s, i, f)
        if kind == "moe" and i[1] < SHARED[s] + ROUTED:
            fill("G", kind, s, *i)
            if i[1] >= SHARED[s]:
                fill("W", kind, s, *i)
        if kind in ("b_y", "moe_y"):
            for b in (2 * i, 2 * i + 1):
                fill("Y", s, b)
        if kind == "din":
            fill("A", kind, s, *i)
        if kind == "xt":
            fill("A", kind, s, i, 0)
            if i % 2 == 0:
                fill("A", kind, s, i, 1)
        if kind == "cb":
            for par in range(2):
                fill("V", kind, s, i, par)
        if kind == "ssd":
            fill("A", kind, s, *i)
            if i[1] == 0:
                fill("O", kind, s, i[0])
        if kind == "state" and i % 2 == 0:
            fill("T", kind, s, i)
        if kind == "state" and i % 2 == 1:
            for par in range(2):
                fill("V", kind, s, i, par)
        if kind == "dy":
            fill("V", kind, s, i)
    return at


def decoder(nc, A, out, stages="ABCDEF"):
    steps = schedule(stages)
    at = number(steps)
    with ExitStack() as ctx:
        def sb(name, shape, dt=F32):
            return ctx.enter_context(nc.sbuf_tensor("s_" + name, shape, dt))

        def ps(name):
            return ctx.enter_context(nc.psum_tensor(name, [P, 512], F32))

        def sem(name):
            return ctx.enter_context(nc.semaphore(name))

        bank = [ps(f"bank{i}") for i in range(8)]
        V = bank[0:2]
        AR = [bank[2], bank[3], bank[6]]
        O = bank[4:6]
        T = bank[7]
        G = bank[0:4]
        CW = bank[4]
        Y = bank[5:7]

        x = sb("x", [P, B * NT, D])
        xn = sb("xn", [P, 2, NT, D])
        xnT = sb("xnT", [P, 2, KD, TOK])
        stats = sb("stats", [P, 2, NT, 6])
        mv = sb("mv", [P, 2, NT, 2])
        ve = sb("ve", [P, 2, NT])
        rstd = sb("rstd", [P, 2, NT])
        mhalf = sb("mhalf", [P, NT])
        ident = sb("ident", [P, P])
        identb = sb("identb", [P, P], BF16)
        masks = sb("masks", [P, 2 * P], BF16)
        maskt = sb("maskt", [P, P], BF16)
        ctxn = sb("ctxn", [P, B * NT, D])

        early = sb("early", [P, EARLY])
        wqkv = early[:, 0:KD * 384].rearrange("p (k n) -> p k n", k=KD)
        wo = early[:, KD * 384:KD * (384 + D)].rearrange("p (k n) -> p k n", k=KD)
        bqkv = sb("bqkv", [P, 384])
        bo = sb("bo", [P, D])
        rope = sb("rope", [P, NT, 320])

        ctxT = early[:, KD * (384 + D):KD * (384 + D) + E0 * KD * D].rearrange("p (e k d) -> p e k d", e=E0, k=KD)
        mask = early[:, EARLY - E0 * TOK // 2:].bitcast(BF16).rearrange("p (e t) -> p e t", e=E0)

        NW = 3
        wmoe = sb("wmoe", [P, NW, WCOLS])
        gatew = sb("gatew", [P, 2, KD, NE])
        iota = sb("iota", [P, NE])
        sel = sb("sel", [3 * NE, ROUTED, P], BF16)
        lg = sb("lg", [P, TH, NE])
        g1 = sb("g1", [P, TH, NE])
        g2 = sb("g2", [P, TH, NE])
        gs = sb("gs", [P, TH])
        top = sb("top", [P, TH, NE])
        topi = sb("topi", [P, TH, NE], U32)
        topf = sb("topf", [P, TH, 2])
        cwp = sb("cwp", [P, TH, 3, NE], BF16)
        cwT = sb("cwT", [3 * NE, HALF], BF16)

        win = sb("win", [P, KD, CONV + DI + NV])
        wout = sb("wout", [P, DI // P, D])
        convw = sb("convw", [P, CT, KS + 1])
        zb = sb("zb", [P, DI])
        dskip = sb("dskip", [P, NV])
        tri = sb("tri", [P, 2, P])

        ARENA = 27200
        arena = sb("arena", [P, ARENA])
        at_ = [0]

        def cut(words, dt=F32, parts=P):
            a = arena[0:parts, at_[0]:at_[0] + words]
            at_[0] += words
            assert at_[0] <= ARENA, at_
            return a if dt is F32 else a.bitcast(dt)

        QT = cut(2 * NH * L // 2, BF16).rearrange("p (c h q) -> p c h q", c=2, h=NH)
        KT = cut(2 * NH * L // 2, BF16).rearrange("p (c h q) -> p c h q", c=2, h=NH)
        qf = cut(2 * 512).rearrange("p (c n) -> p c n", c=2)
        r1 = cut(512)
        stk = cut(2 * 32 * KQ // 2, BF16).rearrange("p (c h s d) -> p c h s d", c=2, h=32, s=SLOTS)
        vaug = cut(3 * NT * NH * VW).rearrange("p (c t g w) -> p c t g w", c=3, t=NT, g=NH)
        nM = cut(NT * NH).rearrange("p (t h) -> p t h", t=NT)
        mp = cut(NT * 2 * NH // 2, BF16).rearrange("p (t m h) -> p t m h", t=NT, m=2)
        MT = cut(L // 2, BF16, 2 * NH)
        NPT = 4
        PT = cut(NPT * 512).rearrange("p (c n) -> p c n", c=NPT)
        rs = cut(NT * NH).rearrange("p (t h) -> p t h", t=NT)
        y = cut(2 * NT * D).rearrange("p (c t d) -> p c t d", c=2, t=NT)
        yT = cut(KD * L).rearrange("p (k q) -> p k q", k=KD)
        yp = cut(512)

        at_[0] = 0
        xm = cut(E0 * KD * HALF).rearrange("p (e k t) -> p e k t", e=E0, k=KD)
        hb = cut(KD * HALF).rearrange("p (k t) -> p k t", k=KD)
        sg = cut(2 * HALF).rearrange("p (c t) -> p c t", c=2)
        NA = 3
        act_ = cut(NA * HALF).rearrange("p (c t) -> p c t", c=NA)
        tok32 = cut(TOK, I32)
        tokf = cut(TOK)
        gef = cut(3 * TOK // 2, BF16).rearrange("p (e t) -> p e t", e=3)

        at_[0] = 0
        NRAW = 2
        raw = cut(NRAW * 2 * (KS - 1 + L)).rearrange("p (c i t) -> p c i t", c=NRAW, i=2)
        xs = cut(2 * CT * L).rearrange("p (c i t) -> p c i t", c=2, i=CT)
        zt = cut(DI)
        zs = cut(2 * DI).rearrange("p (c n) -> p c n", c=2)
        dtb = cut(2 * 8 * NV).rearrange("p (c i h) -> p c i h", c=2, i=8)
        acs = cut(2 * 2 * NV).rearrange("p (c i h) -> p c i h", c=2, i=2)
        dec = cut(2 * NV).rearrange("p (c h) -> p c h", c=2)
        ap_ = cut(3 * NV // 2, BF16).rearrange("p (j m g) -> p j m g", j=HG, m=3)
        AT = cut(2 * P // 2, BF16, RA).rearrange("p (i s) -> p i s", i=2)
        nAT = cut(2 * P // 2, BF16, RA).rearrange("p (i s) -> p i s", i=2)
        RS, RZ = NHG * HG * P // 2, NHG * P // 2
        rows_s = [a.rearrange("p (j g s) -> p j g s", j=HG, g=NHG)
                  for a in (cut(RS, BF16, RR), early[0:RR, 0:RS].bitcast(BF16))]
        rows_z = [a.rearrange("p (g z) -> p g z", g=NHG)
                  for a in (cut(RZ, BF16, RR), early[0:RR, RS:RS + RZ].bitcast(BF16))]
        XS = NHG * P
        xsp = [a.rearrange("p (g h j q w) -> p g h j q w", g=HG, h=NHG // HG, j=HG, w=PV)
               for a in (cut(XS), wmoe[:, :, :].rearrange("p n w -> p (n w)")[:, 0:XS])]
        ys = cut(DI)
        Xt = cut(2 * DI).rearrange("p (c n) -> p c n", c=2)
        Bt = cut(DI)
        XD = cut(DI)
        Du = cut(2 * DI).rearrange("p (c n) -> p c n", c=2)
        CBs = cut(2 * NG * P).rearrange("p (c g s) -> p c g s", c=2, g=NG)
        NM = 4
        M = cut(NM * 512).rearrange("p (c n) -> p c n", c=NM)
        stt = cut(NG // 2 * NS).rearrange("p (g n) -> p g n", g=NG // 2)
        yo = cut(DI)
        yf = cut(DI)
        yfT = cut(DI).rearrange("p (k q) -> p k q", k=DI // P)

        def sems(names):
            return [sem(n) for n in names.split()]

        x_in, const_in, attn_in, ctx_in, tok_in, gate_in, mix_in, hot_in = sems(
            "x_in const_in attn_in ctx_in tok_in gate_in mix_in hot_in")
        w_in = [sem(f"w_in{i}") for i in range(NW)]
        w_used, stored, init = sems("w_used stored init")
        dv, ac, pl = sems("dv ac pl")
        t_full, t_read, v_full, v_read, a_full, a_read, o_read = sems(
            "t_full t_read v_full v_read a_full a_read o_read")
        g_full, u_full, g_read, cw_full, cw_read, y_full, y_read = sems("g_full u_full g_read cw_full cw_read y_full y_read")
        ve_ready, rstd_ready, xn_ready = sems("ve_ready rstd_ready xn_ready")
        qk_ready, v_copied, parts_ready, q_stacked, stack_ready = sems(
            "qk_ready v_copied parts_ready q_stacked stack_ready")
        mp_ready, m_landed, pv_used, attn_added = sems(
            "mp_ready m_landed pv_used attn_added")
        mask_ready, xm_ready, hb_ready, hm_ready, s_ready = sems("mask_ready xm_ready hb_ready hm_ready s_ready")
        gsub_ready, gexp_ready, cwp_ready = sems("gsub_ready gexp_ready cwp_ready")
        raw_cleared, conv_dve, conv_pool, xs_ready = sems("raw_cleared conv_dve conv_pool xs_ready")
        zs_ready, nab_ready, u_ready, w_ready, ln_ready, dt_ready = sems(
            "zs_ready nab_ready u_ready w_ready ln_ready dt_ready")
        ap_ready, decin_ready, dec_ready, rows_landed = sems("ap_ready decin_ready dec_ready rows_landed")
        xsp_ready = sem("xsp_ready")
        du_ready, xd_ready, m_ready, m_used, yf_ready = sems("du_ready xd_ready m_ready m_used yf_ready")

        first = {s: i for i, s in enumerate(stages)}
        turned = [s for s in stages if s != "E"]
        attns = [s for s in stages if s in "AE"]

        def ln_index(s, b):
            return first[s] * B + b

        def attn_index(s, b):
            return attns.index(s) * B + b

        def xn_of(s, b):
            if s == "E":
                k = sum(t < s for t in turned) % 2
                return xnT[:, k].rearrange("p k t -> p (k t)").rearrange("p (n d) -> p n d", d=D)[:, NT * b:NT * b + NT, :]
            return xn[:, ln_index(s, b) % 2]

        def xnT_of(s):
            return xnT[:, turned.index(s) % 2]

        def added(s, b):
            if s in "AE":
                return attn_added, attn_index(s, b) + 1
            if s in "BCF":
                return y_read, at["Y"][s, b] + 1
            return v_read, at["V"]["dy", s, NT * b + 1] + 1

        def previous(s):
            return added(stages[first[s] - 1], B - 1)

        def on_pool(pair):
            return False

        def ssd_on_pool(hg):
            return hg % 4 == 3

        out_v = out.rearrange("b (t p) d -> p (b t) d", p=P)
        x_v = A["x"].rearrange("b (t p) d -> p (b t) d", p=P)
        ctx_v = A["ctx"].rearrange("b (t p) d -> p (b t) d", p=P)

        def row(name, n):
            return A[name].rearrange("(a n) -> a n", a=1).to_broadcast([P, n])

        block = ctx.enter_context(nc.Block())

        m_pool = sem("m_pool")

        def g_other(s):
            return sum(k[0] == "b_h" for k in at["G"])

        def conv(eng, e, s, i, ready):
            b, j = i
            n = b * (CT // 2) + j
            r = raw[:, n % NRAW]
            eng.wait_ge(a_read, at["A"]["din", s, b, j] + 1)
            if b >= 2:
                eng.wait_ge(v_read, at["V"]["state", s, NT * (b - 2) + 1, 1] + 1)
            for k in range(KS):
                for h in range(2):
                    ct = 2 * j + h
                    o = xs[:, b % 2, ct, :]
                    w = convw[:, ct, KS - 1 - k:KS - k]
                    src = r[:, h, KS - 1 - k:KS - 1 - k + L]
                    if k == 0:
                        ins = e.tensor_scalar(o, src, w, convw[:, ct, KS:KS + 1], ALU.mult, ALU.add)
                    else:
                        ins = e.scalar_tensor_tensor(o, src, w, o, ALU.mult, ALU.add)
                ins.then_inc(ready, 1)
                if k < KS - 1:
                    eng.wait_ge(ready, KS * conv_index(i) + k + 1)

        def conv_index(i):
            b, j = i
            mine = [on_pool(q) == on_pool(j) for q in range(CT // 2)]
            return b * sum(mine) + sum(mine[:j])

        def decayed(eng, e, s, i, mine):
            u, hg = i
            if ssd_on_pool(hg) != mine:
                return
            k = NHG * u + hg
            if hg < 4:
                eng.wait_ge(v_read, at["V"]["cb", s, u, 1] + 1)
            eng.wait_ge(a_read, at["A"]["ssd", s, u, hg] + 1)
            m = M[:, k % NM, :].rearrange("p (h z) -> p h z", h=HG)
            e.tensor_tensor(m, m, CBs[:, u % 2, hg // (NV // NG):NG:NG // HG, :],
                            ALU.mult).then_inc(m_sem(hg), 1)

        def m_sem(hg):
            return m_pool if ssd_on_pool(hg) else m_ready

        def m_value(u, hg):
            mine = [ssd_on_pool(q) == ssd_on_pool(hg) for q in range(NHG)]
            return u * sum(mine) + sum(mine[:hg + 1])

        def silu(act, a, s, m):
            b, j = divmod(m, CT // 2)
            act.wait_ge(conv_pool if on_pool(j) else conv_dve, KS * (conv_index((b, j)) + 1))
            v = xs[:, b % 2, 2 * j:2 * j + 2, :]
            a.activation(v, v, ACT.Silu).then_inc(xs_ready, 1)

        def moe_half(s, hf):
            return 2 * (s == "F" and "C" in first) + hf

        def stage_of(ring, key):
            return key[0] if ring == "Y" else key[1]

        def w_all(s):
            return 2 * (SHARED[s] + ROUTED)

        def stack_end(k, t):
            s = attns[k // B]
            return at["A"]["stack_t", s, k % B, t, 2 if s == "A" else 3]

        @block.sync
        def _(sp):
            for b in range(B):
                sp.dma_start(x[:, NT * b:NT * b + NT, :], x_v[:, NT * b:NT * b + NT, :]).then_inc(x_in, 16)
            for dst, name in ((ident, "ident"), (identb, "identb"), (masks, "masks"), (maskt, "maskt")):
                sp.dma_start(dst[:, :], A[name]).then_inc(const_in, 16)
            for dst, name in ((wqkv, "wqkv"), (wo, "wo"), (rope, "rope")):
                sp.dma_start(dst[:, :, :], A[name]).then_inc(attn_in, 16)
            sp.dma_start(bqkv[:, :], row("bqkv", 384)).then_inc(attn_in, 16)
            sp.dma_start(bo[:, :], row("bo", D)).then_inc(attn_in, 16)
            sp.dma_start(ctxT[:, :, :, :], A["ctxT"]).then_inc(ctx_in, 16)
            sp.dma_start(ctxn[:, :, :], ctx_v).then_inc(ctx_in, 16)
            sp.dma_start(gatew[:, :, :, :], A["gatew"]).then_inc(gate_in, 16)
            sp.dma_start(iota[:, :], A["iota"]).then_inc(gate_in, 16)
            sp.dma_start(sel[:, :, :], A["sel"]).then_inc(gate_in, 16)
            sp.dma_start(win[:, :, :], A["win"]).then_inc(mix_in, 16)
            sp.dma_start(wout[:, :, :], A["wout"]).then_inc(mix_in, 16)
            sp.dma_start(convw[:, :, :], A["convw"]).then_inc(mix_in, 16)
            sp.dma_start(zb[:, :], row("zb", DI)).then_inc(mix_in, 16)
            sp.dma_start(dskip[:, :], row("dskip", NV)).then_inc(mix_in, 16)
            sp.dma_start(tri[:, :, :], A["tri"]).then_inc(mix_in, 16)
            for kind, s, i in steps:
                if kind == "m_t":
                    k = attn_index(s, i)
                    sp.wait_ge(t_read, at["T"]["m_t", s, i] + 1)
                    if k >= 2:
                        sp.wait_ge(pv_used, 8 * (k - 1))
                    for m in range(2):
                        sp.dma_start(QT[KQ + m:KQ + m + 1, k % 2, :, :],
                                     MT[m * NH:(m + 1) * NH, :]).then_inc(m_landed, 16)
                elif kind == "switch" and s == "B":
                    if first[s]:
                        sp.wait_ge(*previous(s))
                    sp.dma_start(tok32, row("tok", TOK)).then_inc(tok_in, 16)
                elif kind == "switch" and s == "D":
                    if first[s]:
                        sp.wait_ge(*previous(s))
                    sp.wait_ge(attn_in, 80)
                    sp.wait_ge(ctx_in, 32)
                    for c in range(2):
                        sp.dma_start(rows_s[c][3:RR, :, :, :], A["onehot"]).then_inc(hot_in, 16)
                        sp.dma_start(rows_z[c][0:3, :, :], A["ones3"]).then_inc(hot_in, 16)
                elif kind == "moe" and i[1] < SHARED[s] + ROUTED:
                    k = at["G"]["moe", s, i[0], i[1]] - g_other(s)
                    if k >= NW:
                        sp.wait_ge(w_used, k - NW + 1)
                    sp.dma_start(wmoe[:, k % NW, :], A["w" + s][i[1]]).then_inc(w_in[k % NW], 16)
                elif kind == "at":
                    sp.wait_ge(t_read, at["T"]["at", s, i] + 1)
                    if i >= 2:
                        sp.wait_ge(a_full, at["A"]["ssd", s, i - 2, NHG - 1] + 1)
                    for j in range(HG):
                        h = 3 * NHG * (j % 2)
                        sp.dma_start(rows_s[i % 2][0:3, j, :, :], AT[h:h + 3 * NHG, j // 2, :]).then_inc(rows_landed, 16)
                    for h in range(2):
                        sp.dma_start(rows_z[i % 2][3 + 6 * h:9 + 6 * h, :, :], nAT[:, h, :]).then_inc(rows_landed, 16)
            for landed, loads in ((x_in, 4), (const_in, 4), (attn_in, 5), (ctx_in, 2), (gate_in, 3), (mix_in, 6)):
                sp.wait_ge(landed, 16 * loads)
            for b in range(B):
                sp.wait_ge(*added(stages[-1], b))
                sp.dma_start(out_v[:, NT * b:NT * b + NT, :], x[:, NT * b:NT * b + NT, :]).then_inc(stored, 16)
            sp.wait_ge(stored, 16 * B)

        @block.gpsimd
        def _(pool):
            g = nc.gpsimd
            own = [0]

            def link(ins):
                own[0] += 1
                ins.then_inc(pl, 1)
                pool.wait_ge(pl, own[0])

            link(g.memset(mhalf[:, :], -0.5))
            for kind, s, i in steps:
                if kind == "ln":
                    n = ln_index(s, i)
                    pool.wait_ge(ve_ready, n + 1)
                    g.tensor_tensor(rstd[:, n % 2, :], ve[:, n % 2, :], mhalf[:, :], ALU.pow).then_inc(rstd_ready, 1)
                elif kind == "switch" and s in "AE":
                    if first[s]:
                        pool.wait_ge(*previous(s))
                    pool.wait_ge(rstd_ready, B * (first[s] + 1))
                    link(g.memset(KT[KQ:P, :, :, :], 1.0))
                    g.memset(vaug[:, :, :, :, HD:HD + 1], 1.0)
                    g.memset(vaug[:, :, :, :, HD + 1:VW], 0.0).then_inc(init, 1)
                elif kind == "qkv_split":
                    k = attn_index(s, i)
                    nk = NKV if s == "A" else NH
                    for t in range(NT):
                        pool.wait_ge(qk_ready, NT * k + t + 1)
                        if k >= 3:
                            pool.wait_ge(pv_used, 8 * (k - 2))
                        src = qf[:, t, 320:384] if s == "A" else ctxn[:, NT * i + t, :]
                        g.tensor_copy(vaug[:, k % 3, t, 0:nk, 0:HD],
                                      src.rearrange("p (g w) -> p g w", g=nk)).then_inc(v_copied, 1)
                        pool.wait_ge(parts_ready, NT * k + t + 1)
                        st = stk[:, t]
                        g.tensor_copy(st[:, NH:NH + nk, 2:5:2, :],
                                      st[:, NH:NH + nk, 0, :].unsqueeze(2).to_broadcast([P, nk, 2, HD]))
                        g.tensor_copy(st[:, NH:NH + nk, 1, :], st[:, NH:NH + nk, 5, :]).then_inc(stack_ready, 1)
                elif kind == "b_mask":
                    pool.wait_ge(mask_ready, 1)
                    pool.wait_ge(t_read, at["T"]["lt", s, 2 * i + 1] + 1)
                    if i:
                        pool.wait_ge(y_full, at["Y"][s, 2 * i - 1] + 1)
                    for e in (2, 3):
                        g.tensor_tensor(xm[:, e], xnT_of(s)[:, :, i * HALF:(i + 1) * HALF],
                                        mask[:, e, i * HALF:(i + 1) * HALF].unsqueeze(1).to_broadcast([P, KD, HALF]),
                                        ALU.mult).then_inc(xm_ready, 1)
                elif kind == "b_h":
                    pool.wait_ge(hb_ready, i + 1)
                    for e in (2, 3):
                        g.tensor_tensor(xm[:, e], hb[:, :, :],
                                        mask[:, e, i * HALF:(i + 1) * HALF].unsqueeze(1).to_broadcast([P, KD, HALF]),
                                        ALU.mult).then_inc(hm_ready, 1)
                elif kind == "switch" and s == "D":
                    if first[s]:
                        pool.wait_ge(*previous(s))
                    for a in xsp:
                        g.memset(a, 0.0)
                    g.memset(raw[:, :, :, 0:KS - 1], 0.0).then_inc(raw_cleared, 1)
                    pool.wait_ge(raw_cleared, 1)
                elif kind == "din" and on_pool(i[1]):
                    conv(pool, g, s, i, conv_pool)
                elif kind == "dt":
                    t = dtb[:, i % 2]
                    pool.wait_ge(t_read, at["T"]["dz", s, i] + 1)
                    if i >= 2:
                        pool.wait_ge(du_ready, i - 1)
                    link(g.tensor_scalar(t[:, 1, :], t[:, 0, :], -1.0, None, ALU.mult))
                    link(g.tensor_scalar(t[:, 6, :], t[:, 0, :], 0.0, None, ALU.max))
                    link(g.tensor_scalar(t[:, 5, :], t[:, 1, :], 0.0, None, ALU.max))
                    g.tensor_tensor(t[:, 1, :], t[:, 6, :], t[:, 5, :], ALU.add).then_inc(nab_ready, 1)
                    pool.wait_ge(u_ready, i + 1)
                    link(g.tensor_scalar(t[:, 3, :], t[:, 2, :], 1.0, None, ALU.add))
                    link(g.tensor_scalar(t[:, 4, :], t[:, 3, :], -1.0, None, ALU.add))
                    g.tensor_tensor(t[:, 4, :], t[:, 2, :], t[:, 4, :], ALU.subtract).then_inc(w_ready, 1)
                elif kind == "xt":
                    c = i % 2
                    pool.wait_ge(a_read, at["A"]["xt", s, i, 0] + 1)
                    pool.wait_ge(dt_ready, i + 1)
                    if i >= 2:
                        pool.wait_ge(yf_ready, i - 1)
                    if i >= 2:
                        pool.wait_ge(m_used, NHG * (i - 1))
                    x5 = Xt[:, c, :].rearrange("p (j g q w) -> p g j q w", j=HG, g=HG, w=PV)
                    for h in range(HG):
                        ins = g.tensor_copy(xsp[c][:, :, h, :, h, :], x5[:, :, :, h, :])
                    ins.then_inc(xsp_ready, 1)
                    g.tensor_tensor(Du[:, c, :].rearrange("p (h w) -> p h w", w=PV),
                                    Xt[:, c, :].rearrange("p (h w) -> p h w", w=PV),
                                    dtb[:, c, 7, :].unsqueeze(2).to_broadcast([P, NV, PV]), ALU.mult).then_inc(du_ready, 1)
                    if c == 0:
                        pool.wait_ge(dec_ready, i + 1)
                        if i:
                            pool.wait_ge(t_full, at["T"]["state", s, i - 2] + 1)
                        g.tensor_tensor(XD.rearrange("p (h w) -> p h w", w=PV),
                                        Xt[:, c, :].rearrange("p (h w) -> p h w", w=PV),
                                        dec[:, c, :].unsqueeze(2).to_broadcast([P, NV, PV]), ALU.mult).then_inc(xd_ready, 1)
                elif kind == "ssd":
                    decayed(pool, g, s, i, True)


        @block.scalar
        def _(act):
            a = nc.scalar
            own = [0]

            def link(ins):
                own[0] += 1
                ins.then_inc(ac, 1)
                act.wait_ge(ac, own[0])

            def start(s):
                if first[s]:
                    act.wait_ge(*previous(s))

            for kind, s, i in steps:
                if kind == "switch":
                    start(s)
                elif kind == "lt":
                    act.wait_ge(t_full, at["T"]["lt", s, i] + 1)
                    a.copy(xnT_of(s)[:, :, i * L:(i + 1) * L], T[:, :].rearrange("p (k q) -> p k q", k=KD)
                           ).then_inc(t_read, 1)
                elif kind == "stack_t":
                    k = attn_index(s, i)
                    if k >= 2:
                        act.wait_ge(pv_used, 8 * (k - 1))
                    for t in range(NT):
                        for j in range(3 if s == "A" else 4):
                            n = at["A"]["stack_t", s, i, t, j]
                            act.wait_ge(a_full, n + 1)
                            heads = 4 if j == 2 and s == "A" else 8
                            src = AR[n % 3][:, :].bitcast(BF16)[0:KQ, 0:heads * P].rearrange("p (h q) -> p h q", h=heads)
                            to = QT if j < 2 else KT
                            h0 = 8 * (j % 2)
                            a.copy(to[0:KQ, k % 2, h0:h0 + heads, t * P:(t + 1) * P], src).then_inc(a_read, 1)
                elif kind == "m_t":
                    k = attn_index(s, i)
                    act.wait_ge(t_full, at["T"]["m_t", s, i] + 1)
                    if k:
                        act.wait_ge(m_landed, 32 * k)
                    a.copy(MT[:, :], T[:, :].bitcast(BF16)[0:2 * NH, 0:L]).then_inc(t_read, 1)
                elif kind == "pv":
                    b, j = i
                    n = at["A"]["pv", s, b, j]
                    p = NB * attn_index(s, b) + j
                    act.wait_ge(a_full, n + 1)
                    if p >= NPT:
                        kk, jj = divmod(p - NPT, NB)
                        act.wait_ge(pv_used, 8 * kk + 1 + (jj if jj < 4 else 4 + (jj - 4) // 2))
                    a.activation(PT[:, p % NPT, :], AR[n % 3][:, :], ACT.Exp).then_inc(a_read, 1)
                elif kind == "y_t" and s != "D":
                    b, q = i
                    act.wait_ge(pv_used, 8 * attn_index(s, b) + 4 * (q + 1))
                    if (b, q) > (0, 0):
                        act.wait_ge(v_full, at["V"]["y_t", s, (b - 1 + q, 1 - q)] + 1)
                    a.copy(yp[:, :], O[at["O"]["pv", s, b, q] % 2][:, :]).then_inc(o_read, 1)
                elif kind == "o_t" and s == "A":
                    act.wait_ge(t_full, at["T"]["o_t", s, i] + 1)
                    if i:
                        act.wait_ge(v_full, at["V"]["o", s, i - 1] + 1)
                    a.copy(yT[:, :, :], T[:, :].rearrange("p (k q) -> p k q", k=KD)).then_inc(t_read, 1)
                elif kind == "b_h":
                    for f in range(KD):
                        n = at["G"]["b_h", s, i, f]
                        act.wait_ge(g_full, n + 1)
                        if n >= 2:
                            act.wait_ge(g_read, n - 1)
                        a.activation(sg[:, n % 2, :], G[2 * (n % 2)][:, :], ACT.Silu).then_inc(s_ready, 1)
                elif kind == "gate":
                    act.wait_ge(t_full, at["T"]["gate", s, i] + 1)
                    h = 2 * (s == "F" and "C" in first) + i
                    if h:
                        act.wait_ge(cwp_ready, h)
                    a.copy(lg[:, :, :], T[:, 0:TH * NE].rearrange("p (t e) -> p t e", t=TH)).then_inc(t_read, 1)
                    act.wait_ge(gsub_ready, h + 1)
                    a.activation(g2[:, :, :], g1[:, :, :], ACT.Exp).then_inc(gexp_ready, 1)
                elif kind == "cw_t":
                    act.wait_ge(t_full, at["T"]["cw_t", s, i] + 1)
                    m = [v for (kk, ss, hh, jj), v in at["W"].items() if (ss, hh) < (s, i)]
                    if m:
                        act.wait_ge(cw_full, max(m) + 1)
                    a.copy(cwT[:, :], T[:, :].bitcast(BF16)[0:3 * NE, 0:HALF]).then_inc(t_read, 1)
                elif kind == "moe" and i[1] < SHARED[s] + ROUTED:
                    n = at["G"]["moe", s, i[0], i[1]]
                    act.wait_ge(g_full, n + 1)
                    if n >= 2:
                        act.wait_ge(g_read, n - 1)
                    a.activation(sg[:, n % 2, :], G[2 * (n % 2)][:, :], ACT.Silu).then_inc(s_ready, 1)
                elif kind == "din":
                    b, j = i
                    m = b * (CT // 2) + j
                    n = at["A"]["din", s, b, j]
                    act.wait_ge(a_full, n + 1)
                    if m >= NRAW:
                        bb, jj = divmod(m - NRAW, CT // 2)
                        act.wait_ge(conv_pool if on_pool(jj) else conv_dve, KS * (conv_index((bb, jj)) + 1))
                    a.copy(raw[:, m % NRAW, :, KS - 1:], AR[n % 3][:, :].rearrange("p (i t) -> p i t", i=2)
                           ).then_inc(a_read, 1)
                    if j:
                        silu(act, a, s, m - 1)
                elif kind == "dz":
                    act.wait_ge(t_full, at["T"]["dz", s, i] + 1)
                    if i >= 2:
                        act.wait_ge(du_ready, i - 1)
                    a.copy(dtb[:, i % 2, 0, :], T[:, 0:NV]).then_inc(t_read, 1)
                elif kind == "zs":
                    if i % NT == 0:
                        silu(act, a, s, i // NT * (CT // 2) + CT // 2 - 1)
                    act.wait_ge(v_read, at["V"]["dz", s, i] + 1)
                    if i >= 2:
                        act.wait_ge(yf_ready, i - 1)
                    a.activation(zs[:, i % 2, :], zt[:, :], ACT.Silu).then_inc(zs_ready, 1)
                elif kind == "dt":
                    t = dtb[:, i % 2]
                    act.wait_ge(nab_ready, i + 1)
                    a.activation(t[:, 2, :], t[:, 1, :], ACT.Exp, scale=-1.0).then_inc(u_ready, 1)
                    act.wait_ge(w_ready, i + 1)
                    a.activation(t[:, 5, :], t[:, 3, :], ACT.Ln).then_inc(ln_ready, 1)
                elif kind == "acum":
                    act.wait_ge(t_full, at["T"]["acum", s, i] + 1)
                    if i >= 2:
                        act.wait_ge(yf_ready, i - 1)
                    a.copy(acs[:, i % 2, :, :], T[:, 0:2 * NV].rearrange("p (i h) -> p i h", i=2)).then_inc(t_read, 1)
                    act.wait_ge(decin_ready, i + 1)
                    a.activation(dec[:, i % 2, :], dec[:, i % 2, :], ACT.Exp).then_inc(dec_ready, 1)
                elif kind == "at":
                    act.wait_ge(t_full, at["T"]["at", s, i] + 1)
                    if i:
                        act.wait_ge(rows_landed, 16 * 6 * i)
                    src = T[:, :].bitcast(BF16)[0:RA, 0:2 * P].rearrange("p (i s) -> p i s", i=2)
                    a.copy(AT[:, :, :], src)
                    a.activation(nAT[:, :, :], src, ACT.Copy, scale=-1.0).then_inc(t_read, 1)
                elif kind == "xt":
                    n = at["A"]["xt", s, i, 0]
                    act.wait_ge(a_full, n + 1)
                    if i >= 2:
                        act.wait_ge(xsp_ready, i - 1)
                        act.wait_ge(du_ready, i - 1)
                        act.wait_ge(xd_ready, (i - 2) // 2 + 1)
                    a.copy(Xt[:, i % 2, :], AR[n % 3][:, :]).then_inc(a_read, 1)
                    if i % 2 == 0:
                        n = at["A"]["xt", s, i, 1]
                        act.wait_ge(a_full, n + 1)
                        if i:
                            act.wait_ge(t_full, at["T"]["state", s, i - 2] + 1)
                        a.copy(Bt, AR[n % 3][:, :]).then_inc(a_read, 1)
                elif kind == "ssd":
                    u, hg = i
                    n = at["A"]["ssd", s, u, hg]
                    k = NHG * u + hg
                    act.wait_ge(a_full, n + 1)
                    if k >= NM:
                        act.wait_ge(m_used, k - NM + 1)
                    a.activation(M[:, k % NM, :], AR[n % 3][:, :], ACT.Exp).then_inc(a_read, 1)
                elif kind == "state" and i % 2 == 0:
                    act.wait_ge(t_full, at["T"]["state", s, i] + 1)
                    if i:
                        act.wait_ge(v_full, at["V"]["state", s, i - 1, 1] + 1)
                    a.copy(stt[:, :, :], T[:, 0:NG // 2 * NS].rearrange("p (g n) -> p g n", g=NG // 2)).then_inc(t_read, 1)
                elif kind == "y_t" and s == "D":
                    act.wait_ge(m_used, NHG * (i + 1))
                    if i:
                        act.wait_ge(v_full, at["V"]["y_t", s, i - 1] + 1)
                    a.copy(ys, O[at["O"]["ssd", s, i] % 2][:, :]).then_inc(o_read, 1)
                elif kind == "dy_t":
                    act.wait_ge(t_full, at["T"]["dy_t", s, i] + 1)
                    if i:
                        act.wait_ge(v_full, at["V"]["dy", s, i - 1] + 1)
                    a.copy(yfT[:, :, :], T[:, :].rearrange("p (k q) -> p k q", k=DI // P)).then_inc(t_read, 1)

        @block.tensor
        def _(pe):
            mm = nc.tensor.matmul
            tr = nc.tensor.transpose

            def t_bank(*key):
                if at["T"][key]:
                    pe.wait_ge(t_read, at["T"][key])
                return T

            def v_bank(*key):
                n = at["V"][key]
                if n >= 2:
                    pe.wait_ge(v_read, n - 1)
                return V[n % 2]

            def a_bank(*key):
                n = at["A"][key]
                if n >= 3:
                    pe.wait_ge(a_read, n - 2)
                return AR[n % 3]

            def o_bank(*key):
                n = at["O"][key]
                if n >= 2:
                    pe.wait_ge(o_read, n - 1)
                return O[n % 2]

            def scan(s, u, hg):
                k = NHG * u + hg
                if hg == 0:
                    bk = o_bank("ssd", s, u)
                    pe.wait_ge(xsp_ready, u + 1)
                pe.wait_ge(m_sem(hg), m_value(u, hg))
                bk = O[at["O"]["ssd", s, u] % 2]
                quarter, h = divmod(hg, HG)
                for j in range(HG):
                    ins = mm(bk[j * 32:(j + 1) * 32, quarter * P:(quarter + 1) * P],
                             xsp[u % 2][:, quarter, h, j, :, :].rearrange("p q w -> p (q w)"),
                             M[:, k % NM, j * P:(j + 1) * P], start=(h == 0), stop=(h == HG - 1), skip_group_check=True)
                ins.then_inc(m_used, 1)

            pe.wait_ge(const_in, 64)
            for kind, s, i in steps:
                if kind == "switch":
                    if first[s]:
                        pe.wait_ge(*previous(s))
                        for ring, read in (("V", v_read), ("A", a_read), ("O", o_read), ("G", g_read),
                                           ("W", cw_read), ("Y", y_read)):
                            done = sum(1 for key in at[ring] if stage_of(ring, key) in first
                                       and first[stage_of(ring, key)] < first[s])
                            if done:
                                pe.wait_ge(read, done)
                    if s == "A":
                        pe.wait_ge(attn_in, 80)
                    if s == "B":
                        pe.wait_ge(ctx_in, 32)
                    if s in "CF":
                        pe.wait_ge(gate_in, 48)
                    if s == "D":
                        pe.wait_ge(mix_in, 96)
                        pe.wait_ge(hot_in, 64)
                elif kind == "lt":
                    n = ln_index(s, i)
                    bk = t_bank("lt", s, i)
                    pe.wait_ge(xn_ready, n + 1)
                    for k in range(KD):
                        for t in range(NT):
                            ins = tr(bk[:, (k * NT + t) * P:(k * NT + t + 1) * P], xn_of(s, i)[:, t, k * P:(k + 1) * P],
                                     ident[:, :])
                    ins.then_inc(t_full, 1)
                elif kind == "qkv_mm" and s == "A":
                    pe.wait_ge(t_read, at["T"]["lt", s, i] + 1)
                    for t in range(NT):
                        bk = v_bank("qkv_mm", s, i, t)
                        for k in range(KD):
                            ins = mm(bk[:, 0:384], xnT_of(s)[:, k, i * L + t * P:i * L + (t + 1) * P], wqkv[:, k, :],
                                     start=(k == 0), stop=(k == KD - 1))
                        ins.then_inc(v_full, 1)
                elif kind == "stack_t":
                    kk = attn_index(s, i)
                    for t in range(NT):
                        pe.wait_ge(q_stacked, NT * kk + t + 1)
                        pe.wait_ge(stack_ready, NT * kk + t + 1)
                        for j in range(3 if s == "A" else 4):
                            heads = 4 if j == 2 and s == "A" else 8
                            bk = a_bank("stack_t", s, i, t, j)
                            for h in range(heads):
                                ins = tr(bk[:, :].bitcast(BF16)[0:KQ, h * P:(h + 1) * P],
                                         stk[:, t, 8 * j + h, :, :].rearrange("p s d -> p (s d)"), identb[:, :])
                            ins.then_inc(a_full, 1)
                elif kind == "s":
                    b, j = i
                    c = attn_index(s, b) % 2
                    pe.wait_ge(a_read, at["A"]["stack_t", s, b, NT - 1, 2 if s == "A" else 3] + 1)
                    bk = v_bank("s", s, b, j)
                    if j < 4:
                        mm(bk[:, :], identb[:, :], masks[:, P:2 * P].unsqueeze(1).to_broadcast([P, 4, P]),
                           start=True, stop=False, skip_group_check=True)
                        for h in range(4 * j, 4 * j + 4):
                            g = h // (NH // NKV) if s == "A" else h
                            ins = mm(bk[:, (h % 4) * P:(h % 4 + 1) * P], QT[0:KQ, c, h, 0:P], KT[0:KQ, c, g, 0:P],
                                     start=False, stop=(h % 4 == 3), skip_group_check=True)
                    else:
                        mm(bk[:, :], identb[:, :], masks[:, :].unsqueeze(1).to_broadcast([P, 2, 2 * P]),
                           start=True, stop=False, skip_group_check=True)
                        for h in range(2 * (j - 4), 2 * (j - 4) + 2):
                            g = h // (NH // NKV) if s == "A" else h
                            ins = mm(bk[:, (h % 2) * L:(h % 2 + 1) * L], QT[0:KQ, c, h, P:L], KT[0:KQ, c, g, :],
                                     start=False, stop=(h % 2 == 1), skip_group_check=True)
                    ins.then_inc(v_full, 1)
                elif kind == "m_t":
                    k = attn_index(s, i)
                    bk = t_bank("m_t", s, i)
                    pe.wait_ge(mp_ready, k + 1)
                    for q in range(NT):
                        ins = tr(bk[:, :].bitcast(BF16)[0:2 * NH, q * P:(q + 1) * P],
                                 mp[:, q, :, :].rearrange("p m h -> p (m h)"), identb[:, :])
                    ins.then_inc(t_full, 1)
                elif kind == "pv":
                    i, step = i
                    ka = attn_index(s, i)
                    c = ka % 2
                    if step == 0:
                        pe.wait_ge(m_landed, 32 * (ka + 1))
                        pe.wait_ge(v_copied, NT * (ka + 1))
                        pe.wait_ge(init, attns.index(s) + 1)
                    def scores(j):
                        q, kt, h4 = (0, 0, j) if j < 4 else (1, (j - 4) % 2, (j - 4) // 2)
                        bk = a_bank("pv", s, i, j)
                        diag = q == kt
                        if diag:
                            mm(bk[:, :], identb[:, :], maskt[:, :].unsqueeze(1).to_broadcast([P, 4, P]),
                               start=True, stop=False, skip_group_check=True)
                        if s == "A":
                            ins = mm(bk[:, :], KT[0:KQ + 2, c, h4, kt * P:(kt + 1) * P],
                                     QT[0:KQ + 2, c, 4 * h4:4 * h4 + 4, q * P:(q + 1) * P],
                                     start=not diag, stop=True, skip_group_check=True)
                        else:
                            for h in range(4 * h4, 4 * h4 + 4):
                                ins = mm(bk[:, (h % 4) * P:(h % 4 + 1) * P], KT[0:KQ + 2, c, h, kt * P:(kt + 1) * P],
                                         QT[0:KQ + 2, c, h, q * P:(q + 1) * P],
                                         start=not diag, stop=True, skip_group_check=True)
                        ins.then_inc(a_full, 1)

                    def values(j):
                        q, h4 = (0, j) if j < 4 else (1, j - 4)
                        kept = [12 * ka + j] if q == 0 else [12 * ka + 4 + 2 * h4, 12 * ka + 5 + 2 * h4]
                        bk = O[at["O"]["pv", s, i, q] % 2]
                        if h4 == 0:
                            o_bank("pv", s, i, q)
                        pe.wait_ge(a_read, at["A"]["pv", s, i, j if q == 0 else 5 + 2 * h4] + 1)
                        for kt in range(q + 1):
                            for h in range(4 * h4, 4 * h4 + 4):
                                g = h // (NH // NKV) if s == "A" else h
                                c32 = slice(VW * (h % 4), VW * (h % 4) + VW)
                                ins = mm(bk[c32, h4 * P:(h4 + 1) * P], vaug[:, ka % 3, kt, g, :],
                                         PT[:, kept[kt] % NPT, (h % 4) * P:(h % 4 + 1) * P],
                                         start=(kt == 0), stop=(kt == q), skip_group_check=True)
                        ins.then_inc(pv_used, 1)

                    scores(step)
                    if 1 <= step <= 4:
                        values(step - 1)
                    elif step in (7, 9, 11):
                        values(4 + (step - 7) // 2)
                    if step == NB - 1:
                        values(7)
                elif kind == "y_t" and s == "D":
                    bk = v_bank("y_t", s, i)
                    pe.wait_ge(o_read, at["O"]["ssd", s, i] + 1)
                    for q in range(HG):
                        ins = tr(bk[:, q * P:(q + 1) * P], ys[:, q * P:(q + 1) * P], ident[:, :])
                    ins.then_inc(v_full, 1)
                elif kind == "y_t":
                    b, q = i
                    bk = v_bank("y_t", s, i)
                    pe.wait_ge(o_read, at["O"]["pv", s, b, q] + 1)
                    for h4 in range(4):
                        ins = tr(bk[:, h4 * P:(h4 + 1) * P], yp[:, h4 * P:(h4 + 1) * P], ident[:, :])
                    ins.then_inc(v_full, 1)
                elif kind == "o_t" and s == "A":
                    k = attn_index(s, i)
                    bk = t_bank("o_t", s, i)
                    pe.wait_ge(v_read, at["V"]["y_t", s, (i, 1)] + 1)
                    for d in range(KD):
                        for t in range(NT):
                            ins = tr(bk[:, (d * NT + t) * P:(d * NT + t + 1) * P], y[:, k % 2, t, d * P:(d + 1) * P],
                                     ident[:, :])
                    ins.then_inc(t_full, 1)
                elif kind == "o" and s == "A":
                    bk = v_bank("o", s, i)
                    pe.wait_ge(t_read, at["T"]["o_t", s, i] + 1)
                    for t in range(NT):
                        for d in range(KD):
                            ins = mm(bk[:, t * D:(t + 1) * D], yT[:, d, t * P:(t + 1) * P], wo[:, d, :],
                                     start=(d == 0), stop=(d == KD - 1))
                    ins.then_inc(v_full, 1)
                elif kind == "b_h":
                    pe.wait_ge(xm_ready, E0 * (i + 1))
                    for f in range(KD):
                        n = at["G"]["b_h", s, i, f]
                        if n >= 2:
                            pe.wait_ge(g_read, n - 1)
                        bk = G[2 * (n % 2)]
                        for e in range(E0):
                            for k in range(KD):
                                ins = mm(bk[:, :], ctxT[:, e, k, f * P:(f + 1) * P], xm[:, e, k, :],
                                         start=(e == 0 and k == 0), stop=(e == E0 - 1 and k == KD - 1))
                        ins.then_inc(g_full, 1)
                elif kind == "b_y":
                    pe.wait_ge(hm_ready, E0 * (i + 1))
                    for b in range(2):
                        n = at["Y"][s, 2 * i + b]
                        if n >= 2:
                            pe.wait_ge(y_read, n - 1)
                        for t in range(NT):
                            for e in range(E0):
                                for k in range(KD):
                                    ins = mm(Y[b][:, t * D:(t + 1) * D], xm[:, e, k, (b * NT + t) * P:(b * NT + t + 1) * P],
                                             ctxT[:, e, k, :], start=(e == 0 and k == 0), stop=(e == E0 - 1 and k == KD - 1))
                        ins.then_inc(y_full, 1)
                elif kind == "gate":
                    bk = t_bank("gate", s, i)
                    pe.wait_ge(t_read, at["T"]["lt", s, 2 * i + 1] + 1)
                    for t in range(TH):
                        for k in range(KD):
                            ins = mm(bk[:, t * NE:(t + 1) * NE], xnT_of(s)[:, k, (TH * i + t) * P:(TH * i + t + 1) * P],
                                     gatew[:, int(s == "F"), k, :], start=(k == 0), stop=(k == KD - 1))
                    ins.then_inc(t_full, 1)
                elif kind == "cw_t":
                    bk = t_bank("cw_t", s, i)
                    pe.wait_ge(cwp_ready, moe_half(s, i) + 1)
                    for t in range(TH):
                        ins = tr(bk[:, :].bitcast(BF16)[0:3 * NE, t * P:(t + 1) * P],
                                 cwp[:, t, :, :].rearrange("p m e -> p (m e)"), identb[:, :])
                    ins.then_inc(t_full, 1)
                elif kind == "moe":
                    hf, j = i
                    last = SHARED[s] + ROUTED
                    if j < last:
                        n = at["G"]["moe", s, hf, j]
                        w = n - g_other(s)
                        wt = wmoe[:, w % NW, 0:2 * KD * P].rearrange("p (k g f) -> p k g f", k=KD, g=2)
                        if n >= 2:
                            pe.wait_ge(g_read, n - 1)
                        pe.wait_ge(w_in[w % NW], 16 * (w // NW + 1))
                        for half, full in ((0, g_full), (1, u_full)):
                            for k in range(KD):
                                ins = mm(G[2 * (n % 2) + half][:, :], wt[:, k, half, :],
                                         xnT_of(s)[:, k, hf * HALF:(hf + 1) * HALF], start=(k == 0), stop=(k == KD - 1))
                            ins.then_inc(full, 1)
                        if j >= SHARED[s]:
                            m = at["W"]["moe", s, hf, j]
                            if m:
                                pe.wait_ge(cw_read, m)
                            if j == SHARED[s]:
                                pe.wait_ge(t_read, at["T"]["cw_t", s, hf] + 1)
                            mm(CW[:, :], sel[:, j - SHARED[s], :], cwT[:, :], start=True, stop=True).then_inc(cw_full, 1)
                    if j:
                        j -= 1
                        n = at["G"]["moe", s, hf, j]
                        w = n - g_other(s)
                        if j < SHARED[s]:
                            pe.wait_ge(g_read, n + 1)
                        else:
                            pe.wait_ge(cw_read, at["W"]["moe", s, hf, j] + 1)
                        if j == 0:
                            m = at["Y"][s, 2 * hf]
                            if m:
                                pe.wait_ge(y_read, m)
                        for t in range(TH):
                            ins = mm(Y[t // NT][:, (t % NT) * D:(t % NT + 1) * D], act_[:, w % NA, t * P:(t + 1) * P],
                                     wmoe[:, w % NW, 2 * KD * P:], start=(j == 0 and t % NT == 0), stop=(j == last - 1),
                                     skip_group_check=True)
                        ins.then_inc(w_used, 1)
                elif kind == "din":
                    b, j = i
                    bk = a_bank("din", s, b, j)
                    pe.wait_ge(t_read, at["T"]["lt", s, b] + 1)
                    for h in range(2):
                        ct = 2 * j + h
                        for k in range(KD):
                            ins = mm(bk[:, h * L:(h + 1) * L], win[:, k, ct * P:(ct + 1) * P],
                                     xnT_of(s)[:, k, b * L:(b + 1) * L], start=(k == 0), stop=(k == KD - 1))
                    ins.then_inc(a_full, 1)
                elif kind == "dz":
                    bz, bt_ = v_bank("dz", s, i), t_bank("dz", s, i)
                    for bk, lo, n, full in ((bt_, CONV + DI, NV, t_full), (bz, CONV, DI, v_full)):
                        for k in range(KD):
                            ins = mm(bk[:, 0:n], xnT_of(s)[:, k, i * P:(i + 1) * P], win[:, k, lo:lo + n],
                                     start=(k == 0), stop=(k == KD - 1))
                        ins.then_inc(full, 1)
                elif kind == "acum":
                    bk = t_bank("acum", s, i)
                    pe.wait_ge(dt_ready, i + 1)
                    for k in range(2):
                        ins = mm(bk[:, k * NV:(k + 1) * NV], tri[:, k, :], dtb[:, i % 2, 6, :], start=True, stop=True)
                    ins.then_inc(t_full, 1)
                elif kind == "at":
                    bk = t_bank("at", s, i)
                    pe.wait_ge(ap_ready, i + 1)
                    for h in range(2):
                        ins = tr(bk[:, :].bitcast(BF16)[0:RA, h * P:(h + 1) * P],
                                 ap_[:, 2 * h:2 * h + 2, :, :].rearrange("p j m g -> p (j m g)"), identb[:, :])
                    ins.then_inc(t_full, 1)
                elif kind == "xt":
                    b, c = divmod(i, NT)
                    pe.wait_ge(xs_ready, (CT // 2) * (b + 1))
                    for part in range(2 if c == 0 else 1):
                        bk = a_bank("xt", s, i, part)
                        for k in range(4):
                            ins = tr(bk[:, k * P:(k + 1) * P], xs[:, b % 2, 4 * part + k, c * P:(c + 1) * P], ident[:, :])
                        ins.then_inc(a_full, 1)
                elif kind == "cb":
                    b, c = divmod(i, NT)
                    for par in range(2):
                        bk = v_bank("cb", s, i, par)
                        rows = slice(NS * par, NS * par + NS)
                        for g2_ in range(NG // 2):
                            ins = mm(bk[:, g2_ * P:(g2_ + 1) * P], xs[rows, b % 2, 4 + g2_, c * P:(c + 1) * P],
                                     xs[rows, b % 2, 8 + g2_, c * P:(c + 1) * P], start=True, stop=True)
                        ins.then_inc(v_full, 1)
                elif kind == "ssd":
                    u, hg = i
                    if hg == 0:
                        pe.wait_ge(rows_landed, 16 * 6 * (u + 1))
                    bk = a_bank("ssd", s, u, hg)
                    mm(bk[:, :], identb[:, :], maskt[:, :].unsqueeze(1).to_broadcast([P, HG, P]),
                       start=True, stop=False, skip_group_check=True)
                    mm(bk[:, :], rows_z[u % 2][:, hg, :], rows_s[u % 2][:, :, hg, :], start=False, stop=True,
                       skip_group_check=True).then_inc(a_full, 1)
                    k = NHG * u + hg - LAG
                    if k >= 0:
                        scan(s, *divmod(k, NHG))
                elif kind == "ssd_end":
                    for k in range(NHG * i - LAG, NHG * i):
                        scan(s, *divmod(k, NHG))
                elif kind == "state" and i % 2 == 0:
                    bk = t_bank("state", s, i)
                    pe.wait_ge(xd_ready, i // 2 + 1)
                    pe.wait_ge(a_read, at["A"]["xt", s, i, 1] + 1)
                    for g_ in range(NG):
                        lo = NS * (g_ % 2)
                        ins = mm(bk[lo:lo + NS, (g_ // 2) * NS:(g_ // 2 + 1) * NS], Bt[:, g_ * NS:(g_ + 1) * NS],
                                 XD[:, g_ * NS:(g_ + 1) * NS], start=True, stop=True)
                    ins.then_inc(t_full, 1)
                elif kind == "state":
                    b = i // NT
                    pe.wait_ge(t_read, at["T"]["state", s, i - 1] + 1)
                    for par in range(2):
                        bk = v_bank("state", s, i, par)
                        rows = slice(NS * par, NS * par + NS)
                        for g2_ in range(NG // 2):
                            ins = mm(bk[:, g2_ * NS:(g2_ + 1) * NS], xs[rows, b % 2, 8 + g2_, P:L], stt[rows, g2_, :],
                                     start=True, stop=True)
                        ins.then_inc(v_full, 1)
                elif kind == "dy_t":
                    bk = t_bank("dy_t", s, i)
                    pe.wait_ge(yf_ready, i + 1)
                    for k in range(DI // P):
                        ins = tr(bk[:, k * P:(k + 1) * P], yf[:, k * P:(k + 1) * P], ident[:, :])
                    ins.then_inc(t_full, 1)
                elif kind == "dy":
                    bk = v_bank("dy", s, i)
                    pe.wait_ge(t_read, at["T"]["dy_t", s, i] + 1)
                    for k in range(DI // P):
                        ins = mm(bk[:, 0:D], yfT[:, k, :], wout[:, k, :], start=(k == 0), stop=(k == DI // P - 1))
                    ins.then_inc(v_full, 1)

        @block.vector
        def _(dve):
            v = nc.vector
            own = [0]

            def link(ins):
                own[0] += 1
                ins.then_inc(dv, 1)
                dve.wait_ge(dv, own[0])

            dve.wait_ge(x_in, 64)
            for kind, s, i in steps:
                if kind == "ln":
                    n = ln_index(s, i)
                    c = n % 2
                    if first[s]:
                        dve.wait_ge(*added(stages[first[s] - 1], i))
                    for t in range(NT):
                        link(v.bn_stats(stats[:, c, t, :], x[:, NT * i + t, :]))
                    for t in range(NT):
                        link(v.bn_aggr(mv[:, c, t, :], stats[:, c, t, :]))
                    v.tensor_scalar(ve[:, c, :], mv[:, c, :, 1], EPS, None, ALU.add).then_inc(ve_ready, 1)
                    dve.wait_ge(rstd_ready, n + 1)
                    if s != "E":
                        m = n - 2
                        if m >= 0 and stages[m // B] != "E":
                            dve.wait_ge(t_full, at["T"]["lt", stages[m // B], m % B] + 1)
                    for t in range(NT):
                        ins = v.tensor_scalar(xn_of(s, i)[:, t, :], x[:, NT * i + t, :], mv[:, c, t, 0:1], rstd[:, c, t:t + 1],
                                              ALU.subtract, ALU.mult)
                    ins.then_inc(xn_ready, 1)
                elif kind == "qkv_split":
                    k = attn_index(s, i)
                    nk = NKV if s == "A" else NH
                    wide = NH * HD + nk * HD
                    for t in range(NT):
                        if k:
                            dve.wait_ge(v_copied, NT * (k - 1) + t + 1)
                        q_ = qf[:, t, 0:wide]
                        if s == "A":
                            if k == 0:
                                dve.wait_ge(attn_in, 80)
                            n = at["V"]["qkv_mm", s, i, t]
                            dve.wait_ge(v_full, n + 1)
                            v.tensor_tensor(qf[:, t, 0:384], V[n % 2][:, 0:384], bqkv[:, :], ALU.add).then_inc(v_read, 1)
                            dve.wait_ge(v_read, n + 1)
                            v.tensor_tensor(q_, q_, rope[:, t, :], ALU.mult).then_inc(qk_ready, 1)
                        else:
                            if k % B == 0:
                                dve.wait_ge(ctx_in, 32)
                            dve.wait_ge(xn_ready, ln_index(s, i) + 1)
                            v.tensor_scalar(qf[:, t, 0:D], xn_of(s, i)[:, t, :], QSCALE, None, ALU.mult)
                            v.tensor_copy(qf[:, t, D:2 * D], ctxn[:, NT * i + t, :]).then_inc(qk_ready, 1)
                        dve.wait_ge(qk_ready, NT * k + t + 1)
                        if k:
                            dve.wait_ge(a_full, stack_end(k - 1, t) + 1)
                        st = stk[:, t]
                        heads = NH + nk
                        q3 = q_.rearrange("p (h w) -> p h w", w=HD)
                        r3 = r1[:, 0:wide].rearrange("p (h w) -> p h w", w=HD)
                        link(v.tensor_copy(st[:, 0:heads, 0, :], q3))
                        link(v.tensor_tensor(r3, q3, st[:, 0:heads, 0, :], ALU.subtract))
                        link(v.tensor_copy(st[:, 0:heads, 5, :], r3))
                        v.tensor_tensor(st[:, NH:heads, 3, :], r3[:, NH:heads], st[:, NH:heads, 5, :],
                                        ALU.subtract).then_inc(parts_ready, 1)
                        v.tensor_tensor(st[:, 0:NH, 4, :], r3[:, 0:NH], st[:, 0:NH, 5, :], ALU.subtract)
                        v.tensor_copy(st[:, 0:NH, 1:4:2, :], st[:, 0:NH, 0, :].unsqueeze(2).to_broadcast([P, NH, 2, HD]))
                        v.tensor_copy(st[:, 0:NH, 2, :], st[:, 0:NH, 5, :]).then_inc(q_stacked, 1)
                elif kind == "s":
                    b, j = i
                    n = at["V"]["s", s, b, j]
                    dve.wait_ge(v_full, n + 1)
                    q, h0, heads = (0, 4 * j, 4) if j < 4 else (1, 2 * (j - 4), 2)
                    v.tensor_reduce(nM[:, q, h0:h0 + heads], V[n % 2][:, :].rearrange("p (h k) -> p h k", h=heads),
                                    AX.X, ALU.max, negate=True).then_inc(v_read, 1)
                elif kind == "m_split":
                    k = attn_index(s, i)
                    dve.wait_ge(v_read, at["V"]["s", s, i, NB - 1] + 1)
                    if k:
                        dve.wait_ge(t_full, at["T"]["m_t", attns[(k - 1) // B], (k - 1) % B] + 1)
                    link(v.tensor_copy(mp[:, :, 0, :], nM))
                    v.tensor_tensor(mp[:, :, 1, :], nM, mp[:, :, 0, :], ALU.subtract).then_inc(mp_ready, 1)
                elif kind == "y_t" and s != "D":
                    b, q = i
                    k = attn_index(s, b)
                    n = at["V"]["y_t", s, i]
                    dve.wait_ge(v_full, n + 1)
                    o3 = V[n % 2][:, :].rearrange("p (h w) -> p h w", w=VW)
                    link(v.reciprocal(rs[:, q, :].unsqueeze(2), o3[:, :, HD:HD + 1]))
                    if s == "A" and q == 0 and b >= 2:
                        dve.wait_ge(t_full, at["T"]["o_t", s, b - 2] + 1)
                    v.tensor_tensor(y[:, k % 2, q, :].rearrange("p (h w) -> p h w", w=HD), o3[:, :, 0:HD],
                                    rs[:, q, :].unsqueeze(2).to_broadcast([P, NH, HD]), ALU.mult).then_inc(v_read, 1)
                elif kind == "o":
                    k = attn_index(s, i)
                    xb = x[:, NT * i:NT * i + NT, :]
                    if s == "A":
                        n = at["V"]["o", s, i]
                        dve.wait_ge(v_full, n + 1)
                        tmp = y[:, k % 2]
                        v.tensor_tensor(tmp, V[n % 2][:, :].rearrange("p (t d) -> p t d", t=NT),
                                        bo[:, :].unsqueeze(1).to_broadcast([P, NT, D]), ALU.add).then_inc(v_read, 1)
                        dve.wait_ge(v_read, n + 1)
                    else:
                        dve.wait_ge(v_read, at["V"]["y_t", s, (i, 1)] + 1)
                    v.tensor_tensor(xb, xb, y[:, k % 2], ALU.add).then_inc(attn_added, 1)
                elif kind == "b_mask":
                    if i == 0:
                        dve.wait_ge(tok_in, 16)
                        link(v.tensor_copy(tokf, tok32))
                        for e in range(1, E0):
                            link(v.tensor_scalar(gef[:, e - 1, :], tokf, float(PER_EXPERT * e), None, ALU.is_ge))
                        v.tensor_scalar(mask[:, 0, :], gef[:, 0, :], -1.0, 1.0, ALU.mult, ALU.add)
                        v.tensor_tensor(mask[:, 1, :], gef[:, 0, :], gef[:, 1, :], ALU.subtract)
                        v.tensor_tensor(mask[:, 2, :], gef[:, 1, :], gef[:, 2, :], ALU.subtract)
                        v.tensor_copy(mask[:, 3, :], gef[:, 2, :]).then_inc(mask_ready, 1)
                        dve.wait_ge(mask_ready, 1)
                    dve.wait_ge(t_read, at["T"]["lt", s, 2 * i + 1] + 1)
                    if i:
                        dve.wait_ge(y_full, at["Y"][s, 2 * i - 1] + 1)
                    for e in (0, 1):
                        v.tensor_tensor(xm[:, e], xnT_of(s)[:, :, i * HALF:(i + 1) * HALF],
                                        mask[:, e, i * HALF:(i + 1) * HALF].unsqueeze(1).to_broadcast([P, KD, HALF]),
                                        ALU.mult).then_inc(xm_ready, 1)
                elif kind == "b_h":
                    if i:
                        dve.wait_ge(hm_ready, E0 * i)
                    for f in range(KD):
                        n = at["G"]["b_h", s, i, f]
                        dve.wait_ge(s_ready, n + 1)
                        v.tensor_tensor(hb[:, f, :], G[2 * (n % 2)][:, :], sg[:, n % 2, :], ALU.mult).then_inc(g_read, 1)
                    dve.wait_ge(g_read, n + 1)
                    v.tensor_copy(gs[:, 0:1], rstd[:, 0, 0:1]).then_inc(hb_ready, 1)
                    for e in (0, 1):
                        v.tensor_tensor(xm[:, e], hb[:, :, :],
                                        mask[:, e, i * HALF:(i + 1) * HALF].unsqueeze(1).to_broadcast([P, KD, HALF]),
                                        ALU.mult).then_inc(hm_ready, 1)
                elif kind in ("b_y", "moe_y"):
                    for b in range(2):
                        n = at["Y"][s, 2 * i + b]
                        if kind == "b_y":
                            dve.wait_ge(y_full, n + 1)
                        else:
                            dve.wait_ge(w_used, (SHARED[s] + ROUTED) * (i + 1) + (w_all("C") if s == "F" and "C" in first else 0))
                        xb = x[:, NT * (2 * i + b):NT * (2 * i + b) + NT, :]
                        v.tensor_tensor(xb, xb, Y[b][:, :].rearrange("p (t d) -> p t d", t=NT), ALU.add).then_inc(y_read, 1)
                elif kind == "gate":
                    h = moe_half(s, i)
                    if h == 0:
                        dve.wait_ge(gate_in, 48)
                    dve.wait_ge(t_read, at["T"]["gate", s, i] + 1)
                    wide = [P, TH, NE]
                    link(v.tensor_reduce(gs[:, :], lg[:, :, :], AX.X, ALU.max))
                    v.tensor_tensor(g1[:, :, :], lg[:, :, :], gs[:, :].unsqueeze(2).to_broadcast(wide),
                                    ALU.subtract).then_inc(gsub_ready, 1)
                    dve.wait_ge(gexp_ready, h + 1)
                    link(v.tensor_reduce(gs[:, :], g2[:, :, :], AX.X, ALU.add))
                    link(v.reciprocal(gs[:, :], gs[:, :]))
                    link(v.tensor_tensor(g1[:, :, :], g2[:, :, :], gs[:, :].unsqueeze(2).to_broadcast(wide), ALU.mult))
                    for t in range(TH):
                        link(v.max(top[:, t, :], g1[:, t, :]))
                        link(v.max_index(topi[:, t, :], top[:, t, :], g1[:, t, :]))
                    link(v.tensor_copy(topf[:, :, :], topi[:, :, 0:2]))
                    io = iota[:, :].unsqueeze(1).to_broadcast(wide)
                    link(v.tensor_tensor(g2[:, :, :], io, topf[:, :, 0:1].to_broadcast(wide), ALU.is_equal))
                    link(v.tensor_tensor(lg[:, :, :], io, topf[:, :, 1:2].to_broadcast(wide), ALU.is_equal))
                    link(v.tensor_tensor(g2[:, :, :], g2[:, :, :], lg[:, :, :], ALU.add))
                    link(v.tensor_tensor(g1[:, :, :], g1[:, :, :], g2[:, :, :], ALU.mult))
                    if s == "C":
                        link(v.tensor_reduce(gs[:, :], g1[:, :, :], AX.X, ALU.add))
                        link(v.tensor_scalar(gs[:, :], gs[:, :], 1e-20, None, ALU.add))
                        link(v.reciprocal(gs[:, :], gs[:, :]))
                        link(v.tensor_tensor(g1[:, :, :], g1[:, :, :], gs[:, :].unsqueeze(2).to_broadcast(wide), ALU.mult))
                    link(v.tensor_copy(cwp[:, :, 0, :], g1[:, :, :]))
                    link(v.tensor_tensor(g2[:, :, :], g1[:, :, :], cwp[:, :, 0, :], ALU.subtract))
                    link(v.tensor_copy(cwp[:, :, 1, :], g2[:, :, :]))
                    v.tensor_tensor(cwp[:, :, 2, :], g2[:, :, :], cwp[:, :, 1, :], ALU.subtract).then_inc(cwp_ready, 1)
                elif kind == "moe" and i[1] < SHARED[s] + ROUTED:
                    hf, j = i
                    n = at["G"]["moe", s, hf, j]
                    w = n - g_other(s)
                    dve.wait_ge(u_full, w + 1)
                    dve.wait_ge(s_ready, n + 1)
                    if w >= NA:
                        dve.wait_ge(w_used, w - NA + 1)
                    v.tensor_tensor(act_[:, w % NA, :], G[2 * (n % 2) + 1][:, :], sg[:, n % 2, :], ALU.mult).then_inc(g_read, 1)
                    if j >= SHARED[s]:
                        m = at["W"]["moe", s, hf, j]
                        dve.wait_ge(cw_full, m + 1)
                        dve.wait_ge(g_read, n + 1)
                        v.tensor_tensor(act_[:, w % NA, :], act_[:, w % NA, :], CW[:, :], ALU.mult).then_inc(cw_read, 1)
                elif kind == "switch" and s == "D":
                    dve.wait_ge(mix_in, 96)
                    dve.wait_ge(raw_cleared, 1)
                elif kind == "din" and not on_pool(i[1]):
                    conv(dve, v, s, i, conv_dve)
                elif kind == "dz":
                    n = at["V"]["dz", s, i]
                    dve.wait_ge(v_full, n + 1)
                    if i:
                        dve.wait_ge(zs_ready, i)
                    v.tensor_tensor(zt[:, :], V[n % 2][:, :], zb[:, :], ALU.add).then_inc(v_read, 1)
                elif kind == "dt":
                    t = dtb[:, i % 2]
                    dve.wait_ge(w_ready, i + 1)
                    link(v.reciprocal(t[:, 7, :], t[:, 3, :]))
                    link(v.tensor_tensor(t[:, 4, :], t[:, 4, :], t[:, 7, :], ALU.mult))
                    dve.wait_ge(ln_ready, i + 1)
                    link(v.tensor_tensor(t[:, 4, :], t[:, 4, :], t[:, 5, :], ALU.add))
                    link(v.tensor_tensor(t[:, 6, :], t[:, 4, :], t[:, 6, :], ALU.add))
                    link(v.reciprocal(t[:, 7, :], t[:, 6, :]))
                    v.tensor_tensor(t[:, 7, :], t[:, 7, :], dskip[:, :], ALU.mult).then_inc(dt_ready, 1)
                elif kind == "acum":
                    c = i % 2
                    dve.wait_ge(t_read, at["T"]["acum", s, i] + 1)
                    if i:
                        dve.wait_ge(t_full, at["T"]["at", s, i - 1] + 1)
                    if i >= 2:
                        dve.wait_ge(yf_ready, i - 1)
                        if c == 0:
                            dve.wait_ge(xd_ready, i // 2)
                    cum, last = acs[:, c, 0, :], acs[:, c, 1, :]
                    if c == 0:
                        v.tensor_tensor(dec[:, c, :], last, cum, ALU.subtract).then_inc(decin_ready, 1)
                    else:
                        v.tensor_copy(dec[:, c, :], cum).then_inc(decin_ready, 1)
                    cum = cum.rearrange("p (j g) -> p j g", j=HG)
                    rest = dtb[:, c, 5, :].rearrange("p (j g) -> p j g", j=HG)
                    link(v.tensor_copy(ap_[:, :, 0, :], cum))
                    link(v.tensor_tensor(rest, cum, ap_[:, :, 0, :], ALU.subtract))
                    link(v.tensor_copy(ap_[:, :, 1, :], rest))
                    v.tensor_tensor(ap_[:, :, 2, :], rest, ap_[:, :, 1, :], ALU.subtract).then_inc(ap_ready, 1)
                elif kind == "cb":
                    if i >= 2:
                        dve.wait_ge(m_pool, m_value(i - 2, NHG - 1))
                    for par in range(2):
                        n = at["V"]["cb", s, i, par]
                        dve.wait_ge(v_full, n + 1)
                        v.tensor_copy(CBs[:, i % 2, par:NG:2, :], V[n % 2][:, :].rearrange("p (g s) -> p g s", g=NG // 2)
                                      ).then_inc(v_read, 1)
                elif kind == "ssd":
                    decayed(dve, v, s, i, False)
                elif kind == "state" and i % 2 == 1:
                    dve.wait_ge(dec_ready, i + 1)
                    for par in range(2):
                        n = at["V"]["state", s, i, par]
                        dve.wait_ge(v_full, n + 1)
                        o4 = yo.rearrange("p (g j h w) -> p g j h w", g=NG // 2, j=2, w=PV)[:, :, par]
                        e4 = dec[:, 1, :].rearrange("p (g j h) -> p g j h", g=NG // 2, j=2)[:, :, par]
                        for g_ in range(NG // 2):
                            ins = v.tensor_tensor(o4[:, g_], V[n % 2][:, g_ * NS:(g_ + 1) * NS].rearrange("p (h w) -> p h w", w=PV),
                                                  e4[:, g_].unsqueeze(2).to_broadcast([P, NG, PV]), ALU.mult)
                        ins.then_inc(v_read, 1)
                elif kind == "y_t":
                    b, c = divmod(i, NT)
                    n = at["V"]["y_t", s, i]
                    dve.wait_ge(v_full, n + 1)
                    dve.wait_ge(du_ready, i + 1)
                    dve.wait_ge(zs_ready, i + 1)
                    if i:
                        dve.wait_ge(t_full, at["T"]["dy_t", s, i - 1] + 1)

                    def quarters(a):
                        return a.rearrange("p (j g f) -> p g j f", j=HG, g=HG)

                    v.tensor_tensor(quarters(yf), V[n % 2][:, :].rearrange("p (g j f) -> p g j f", g=HG, j=HG),
                                    quarters(Du[:, c, :]), ALU.add).then_inc(v_read, 1)
                    dve.wait_ge(v_read, n + 1)
                    if c:
                        dve.wait_ge(v_read, at["V"]["state", s, i, 1] + 1)
                        link(v.tensor_tensor(yf, yf, yo, ALU.add))
                    v.tensor_tensor(yf, yf, zs[:, c, :], ALU.mult).then_inc(yf_ready, 1)
                elif kind == "dy":
                    n = at["V"]["dy", s, i]
                    dve.wait_ge(v_full, n + 1)
                    v.tensor_tensor(x[:, i, :], x[:, i, :], V[n % 2][:, 0:D], ALU.add).then_inc(v_read, 1)


def layouts(inp):

    bf = np.dtype("bfloat16")
    f = {k: np.asarray(v) for k, v in inp.items()}

    def rows(w):
        return np.ascontiguousarray(w.reshape(-1, P, w.shape[1]).transpose(1, 0, 2))

    arrays = {
        "x": f["x"], "ctx": f["ctx_2048"], "tok": f["itok_BxS_13_99985"].reshape(-1),
        "wqkv": rows(np.concatenate([f["L0_attn_Wq"].T, f["L0_attn_Wk"].T, f["L0_attn_Wv"].T], 1)),
        "wo": rows(f["L0_attn_Wo"].T),
        "bqkv": np.concatenate([f["L0_attn_bq"], f["L0_attn_bk"], f["L0_attn_bv"]]),
        "bo": f["L0_attn_bo"],
        "ctxT": np.ascontiguousarray(f["ctx_2048"].transpose(0, 2, 1).reshape(E0, KD, P, D).transpose(2, 0, 1, 3)),
        "gatew": np.ascontiguousarray(np.stack([rows(f["L0_ffn_gate_w"].T), rows(f["L1_ffn_gate_weight"].T)], 1)),
        "win": rows(f["L1_attn_in_proj_w"].T),
        "wout": rows(f["L1_attn_out_proj_w"].T),
        "zb": f["L1_attn_z_bias"], "dskip": f["L1_attn_D"],
        "convw": np.ascontiguousarray(np.concatenate([f["L1_attn_conv1d_weight"][:, 0, :], f["L1_attn_conv1d_bias"][:, None]],
                                                     1).reshape(CT, P, KS + 1).transpose(1, 0, 2)),
    }

    def tiles(gate, up, down, n):
        pad = n * P - gate.shape[1]
        gate, up = (np.pad(w, ((0, 0), (0, pad))).reshape(KD, P, n, P) for w in (gate, up))
        down = np.pad(down, ((0, pad), (0, 0))).reshape(n, P, D)
        gu = np.stack([gate, up], 3).transpose(2, 1, 0, 3, 4).reshape(n, P, 2 * KD * P)
        return np.concatenate([gu, down], 2)

    def cat(w):
        return w.transpose(1, 0, 2).reshape(D, NE * FE)

    w1 = f["L0_ffn_w1"]
    arrays["wC"] = np.ascontiguousarray(np.concatenate([
        tiles(f["L0_ffn_sw1"].T, f["L0_ffn_sw2"].T, f["L0_ffn_sw3"].T, SHARED["C"]),
        tiles(cat(w1[:, :, :FE]), cat(w1[:, :, FE:]), f["L0_ffn_w2"].reshape(NE * FE, D), ROUTED)]))
    gu, sgu = f["L1_ffn_gate_up_weights"], f["L1_ffn_shared_gate_up"]
    fs = sgu.shape[0] // 2
    arrays["wF"] = np.ascontiguousarray(np.concatenate([
        tiles(sgu[:fs].T, sgu[fs:].T, f["L1_ffn_shared_down"].T, SHARED["F"]),
        tiles(cat(gu[:, :FE].transpose(0, 2, 1)), cat(gu[:, FE:].transpose(0, 2, 1)),
              f["L1_ffn_down_weights"].transpose(0, 2, 1).reshape(NE * FE, D), ROUTED)]))

    i = np.arange(P)
    arrays["ident"] = np.eye(P, dtype=np.float32)
    arrays["identb"] = np.eye(P).astype(bf)
    later = np.where(i[None, :] > i[:, None], NEG, 0.0)
    arrays["masks"] = np.concatenate([np.zeros((P, P)), later], 1).astype(bf)
    arrays["maskt"] = later.T.astype(bf)
    inv = np.float32(10000.0) ** (np.float32(-2.0) * np.arange(HD // 2, dtype=np.float32) / np.float32(HD))
    theta = np.arange(L, dtype=np.float32)[:, None] * inv[None, :].astype(np.float32)
    turn = np.tile(np.cos(theta) + np.sin(theta), (1, 2)).astype(np.float32)
    arrays["rope"] = np.ascontiguousarray(np.concatenate([np.tile(turn * np.float32(QSCALE), (1, NH)), np.tile(turn, (1, NKV))],
                                                         1).reshape(NT, P, -1).transpose(1, 0, 2))
    expert = (np.arange(ROUTED * P) // FE).reshape(ROUTED, P)
    arrays["sel"] = np.tile(expert[None] == np.arange(NE)[:, None, None], (3, 1, 1)).astype(bf)
    arrays["iota"] = np.tile(np.arange(NE, dtype=np.float32), (P, 1))
    arrays["tri"] = np.stack([-(i[:, None] <= i[None, :]).astype(np.float32), -np.ones((P, P), np.float32)], 1)
    arrays["onehot"] = np.tile(np.repeat(np.eye(HG), 3, 0)[:, :, None, None], (1, 1, NHG, P)).astype(bf)
    arrays["ones3"] = np.ones((3, NHG, P)).astype(bf)
    return arrays


def kernel(**inputs):
    import concourse.bacc as bacc
    from concourse.bass_utils import run_bass_kernel_spmd

    nc = bacc.Bacc("TRN2", target_bir_lowering=False, num_devices=1)
    arrays = layouts(inputs)
    args = {n: nc.dram_tensor(f"in_{n}", a.shape, mybir.dt.from_np(a.dtype), kind="ExternalInput").ap()
            for n, a in arrays.items()}
    out = nc.dram_tensor("out_x", (B, L, D), F32, kind="ExternalOutput").ap()
    decoder(nc, args, out)
    r = run_bass_kernel_spmd(nc, [{f"in_{n}": a for n, a in arrays.items()}], core_ids=[0])
    return r.results[0]["out_x"]
```

```python
from contextlib import ExitStack

import numpy as np

import concourse.bass as bass
from concourse import mybir

ALU = mybir.AluOpType
ACT = mybir.ActivationFunctionType
AX = mybir.AxisListType
F32 = mybir.dt.float32
F32R = mybir.dt.float32r
BF16 = mybir.dt.bfloat16
I32 = mybir.dt.int32
U32 = mybir.dt.uint32

P = 128
B, L, D = 4, 256, 256
TOK = B * L
NT = L // P
KD = D // P
EPS = 1e-5
NH, HD = 16, 16
NKV = 4
QSCALE = HD ** -0.5
NEG = -1e30
SLOTS = 6
KQ = SLOTS * HD
VW = 32
VOCAB, E0 = 12500, 4
DVE_EXPERTS = 3
PER_EXPERT = VOCAB // E0
NE, FE = 8, 176
HALF = TOK // 2
TH = HALF // P
ROUTED = NE * FE // P
SHARED = {"C": 2, "F": 3}
EARLY = KD * (384 + D) + E0 * KD * D + E0 * TOK // 2
AHEAD = 2
DOWN_LAG = 2
WCOLS = KD * 2 * P + D
DI, NS, NG, NV = 512, 64, 8, 64
PV = DI // NV
CONV = DI + 2 * NG * NS
CT = CONV // P
KS = 4
NB = 12
HG = 4
NHG = NV // HG
PAIRS = CT // 2
BESIDE_C = 8
FIRST_PAIRS = 9
FIRST_SPLITS = (8, 11)
LATER_SPLITS = (4, 8)
REST = 1
SECOND_SPLITS = (6, 10)
LAST_UNIT = (3, "y_t"), (5, "dy_t"), (7, "dy")
NEXT_UNIT = (6, "at"), (8, "dz"), (10, "zs"), (12, "xt"), (13, "cb")
PAIR_AT = 1, 4, 9
LAG = 3
RR = 3 + 3 * HG
RA = HG // 2 * 3 * NHG


def schedule(stages):
    steps = []
    after = {s: stages[i + 1] if i + 1 < len(stages) else None for i, s in enumerate(stages)}

    def norm(s, b):
        if after[s] is not None:
            steps.append(("ln", after[s], b))

    def turn(s, b):
        if s is not None and s != "E":
            steps.append(("lt", s, b))

    for b in range(B):
        steps.append(("ln", stages[0], b))
        turn(stages[0], b)
    late, last_norm = [], []
    beside_c = BESIDE_C if "D" in stages and stages[stages.index("D") - 1:stages.index("D")] == "C" else 0
    if stages[0] == "B":
        steps.append(("tokens", "B", 0))
    def din(m):
        steps.append(("din", "D", divmod(m, PAIRS)))

    def taps(m):
        steps.extend(("tap", "D", (*divmod(m, PAIRS), k)) for k in range(1, KS))

    def silu(m):
        steps.append(("th", "D", divmod(m, PAIRS)))
        steps.append(("silu", "D", divmod(m, PAIRS)))

    for s in stages:
        steps.append(("switch", s, 0))
        nxt = after[s]
        if s in "AE":
            steps.extend(("qkv_mm", s, (0, t)) for t in range(NT))
            if s == "E" and after.get("D") == "E":
                steps.append(("v_copy", s, 0))
            else:
                steps.extend((kind, s, (0, t)) for t in range(NT) for kind in ("qkv_split", "q_rest"))
            while late:
                turn(*late.pop(0))
            steps.append(("stack_t", s, 0))
            steps.extend(("qkv_mm", s, (1, t)) for t in range(NT))
            split_at = (0, 0) if s == "A" else SECOND_SPLITS
            for k in range(NB):
                steps.extend((kind, s, (1, t)) for t in range(NT) if split_at[t] == k for kind in ("qkv_split", "q_rest"))
                steps.append(("s", s, (0, k)))
            steps.append(("m_split", s, 0))
            steps.append(("m_t", s, 0))
            steps.append(("stack_t", s, 1))
            if last_norm:
                steps.append(last_norm.pop())
            for b in range(B):
                for k in range(NB):
                    if b + 1 < B:
                        steps.append(("s", s, (b + 1, k)))
                        if k == NB - 1:
                            steps.append(("m_split", s, b + 1))
                    if k in LATER_SPLITS and b + 2 < B:
                        steps.append(("qkv_mm", s, (b + 2, LATER_SPLITS.index(k))))
                    steps.append(("pv", s, (b, k)))
                    if k in LATER_SPLITS and b + 2 < B:
                        steps.append(("qkv_split", s, (b + 2, LATER_SPLITS.index(k))))
                    if k - REST in LATER_SPLITS and b + 2 < B:
                        steps.append(("q_rest", s, (b + 2, LATER_SPLITS.index(k - REST))))
                    if k == 1 and b:
                        steps.append(("o_t", s, b - 1))
                    if k == 3 and b:
                        steps.append(("o", s, b - 1))
                        norm(s, b - 1)
                    if k == 2 and b == 0 and nxt == "B":
                        steps.append(("tokens", "B", 0))
                    if k == 6:
                        steps.append(("y_t", s, (b, 0)))
                    if k == 9 and b:
                        turn(nxt, b - 1)
                if b + 1 < B:
                    steps.append(("m_t", s, b + 1))
                steps.append(("y_t", s, (b, 1)))
                if b + 2 < B:
                    steps.append(("stack_t", s, b + 2))
            steps.append(("o_t", s, B - 1))
            steps.append(("o", s, B - 1))
            norm(s, B - 1)
            late.append((nxt, B - 1))
        elif s == "B":
            steps.append(("b_mask", s, 0))
            while late:
                turn(*late.pop(0))
            steps.append(("b_mask", s, 1))
            steps.append(("b_h", s, 0))
            steps.append(("b_h", s, 1))
            for b in range(B):
                steps.append(("b_y", s, b))
                if b >= 2:
                    turn(nxt, b - 2)
                if b == 2 and nxt == "C":
                    steps.extend(("w_split", nxt, j) for j in range(AHEAD))
                norm(s, b)
            late.extend((nxt, b) for b in (2, 3))
        elif s in "CF":
            for hf in range(2):
                n = SHARED[s] + ROUTED
                if hf == 0:
                    if s == "F" or stages[0] == "C":
                        steps.extend(("w_split", s, j) for j in range(AHEAD))
                    steps.append(("gate", s, 0))
                for j in range(n + DOWN_LAG):
                    if j == 1:
                        steps.append(("cw_t", s, hf))
                    if j == 3:
                        while late:
                            turn(*late.pop(0))
                    steps.append(("moe", s, (hf, j)))
                    if nxt == "D" and hf == 0 and j == 4:
                        steps.append(("d_init", nxt, 0))
                    if nxt == "D" and hf == 1:
                        if 0 < j - 4 <= beside_c:
                            taps(j - 5)
                        if 0 < j - 5 <= beside_c:
                            silu(j - 6)
                        if 0 <= j - 4 < beside_c:
                            din(j - 4)
                    if j == n - 3 and hf == 0:
                        steps.append(("gate", s, 1))
                    if j < n:
                        steps.append(("a_split", s, (hf, j)))
                        if hf * n + j + AHEAD < 2 * n:
                            steps.append(("w_split", s, hf * n + j + AHEAD))
                steps.append(("moe_y", s, hf))
                for b in (2 * hf, 2 * hf + 1):
                    norm(s, b)
                    late.append((nxt, b))
        elif s == "D":
            if not beside_c:
                steps.append(("d_init", s, 0))
            while late:
                turn(*late.pop(0))
            steps.append(("dt_in", s, 0))
            chain = ["dt", "acum", "at", "ddt"]
            for m in range(beside_c, FIRST_PAIRS):
                din(m)
                if m > beside_c:
                    silu(m - 1)
                if m == beside_c:
                    steps.append(("dz", s, 0))
                taps(m)
                if chain:
                    steps.append((chain.pop(0), s, 0))
            silu(FIRST_PAIRS - 1)
            if beside_c:
                steps.append(("cb", s, 0))
            steps.extend((kind, s, 0) for kind in chain)
            for kind in ("zs", "xt") + (() if beside_c else ("cb",)):
                steps.append((kind, s, 0))
            units = B * NT
            for u in range(units + 1):
                b, c = divmod(u, NT)
                beside = {}
                if u:
                    for hg, kind in LAST_UNIT:
                        beside[hg] = [(kind, s, u - 1)]
                if u < units:
                    beside.setdefault(0, []).append(("state", s, u))
                for n, hg in enumerate(PAIR_AT):
                    pair = divmod(FIRST_PAIRS + len(PAIR_AT) * u + n, PAIRS)
                    if pair[0] < B:
                        beside.setdefault(hg, []).append(("din", s, pair))
                        for k in range(1, KS):
                            beside.setdefault(hg + k, []).append(("tap", s, (*pair, k)))
                        beside.setdefault(hg + KS, []).append(("th", s, pair))
                        beside.setdefault(hg + KS + 1, []).append(("silu", s, pair))
                if u + 1 < units:
                    for hg, kind in NEXT_UNIT:
                        beside.setdefault(hg, []).append((kind, s, u + 1))
                for hg in range(NHG if u < units else LAST_UNIT[-1][0] + 1):
                    if u < units:
                        steps.append(("ssd", s, (u, hg)))
                    elif hg == 0:
                        steps.append(("ssd_end", s, units))
                    steps.extend(beside.get(hg, []))
                    if nxt == "E" and u == units - 1 and hg in FIRST_SPLITS:
                        steps.extend((kind, nxt, (0, FIRST_SPLITS.index(hg))) for kind in ("qkv_split", "q_rest"))
                if c == 0 and b:
                    if b == B and nxt == "E":
                        last_norm.append(("ln", nxt, b - 1))
                    else:
                        norm(s, b - 1)
                    if b > 1:
                        turn(nxt, b - 2)
            turn(nxt, B - 2)
            late.append((nxt, B - 1))
    return steps


def number(steps):
    at = {r: {} for r in "TVAOGWY"}

    def fill(ring, *key):
        at[ring][key] = len(at[ring])

    for place, (kind, s, i) in enumerate(steps):
        if kind in ("lt", "m_t", "gate", "cw_t", "dt_in", "at", "dy_t"):
            fill("T", kind, s, i)
        if kind == "dz":
            fill("V", kind, s, i)
        if kind == "acum":
            for k in range(2):
                fill("T", kind, s, k)
        if kind == "qkv_mm" and s == "A":
            fill("V", kind, s, *i)
        if kind == "s":
            fill("V", kind, s, *i)
        if kind == "stack_t":
            for t in range(NT):
                for k in range(3 if s == "A" else 4):
                    fill("AV"[k % 2], kind, s, i, t, k)
        if kind == "pv":
            fill("A", kind, s, *i)
            if i[1] in (0, 4):
                fill("O", kind, s, i[0], i[1] // 4)
        if kind == "y_t":
            fill("V", kind, s, i)
        if kind == "o_t" and s == "A":
            fill("T", kind, s, i)
        if kind == "o" and s == "A":
            fill("V", kind, s, i)
        if kind == "b_h":
            for f in range(KD):
                fill("G", kind, s, i, f)
        if kind == "moe" and i[1] < SHARED[s] + ROUTED:
            fill("G", kind, s, *i)
            if i[1] >= SHARED[s]:
                fill("W", kind, s, *i)
        if kind == "b_y":
            fill("Y", s, i)
        if kind == "moe_y":
            for b in (2 * i, 2 * i + 1):
                fill("Y", s, b)
        if kind == "din":
            fill("A" if ("switch", s, 0) in steps[:place] else "T", kind, s, *i)
        if kind == "xt":
            fill("A", kind, s, i, 0)
            if i % 2 == 0:
                fill("A", kind, s, i, 1)
        if kind == "cb":
            for par in range(2):
                fill("V", kind, s, i, par)
        if kind == "ssd":
            fill("A", kind, s, *i)
            if i[1] == 0:
                fill("O", kind, s, i[0])
        if kind == "state" and i % 2 == 0:
            fill("T", kind, s, i)
        if kind == "state" and i % 2 == 1:
            for par in range(2):
                fill("V", kind, s, i, par)
        if kind == "dy":
            fill("V", kind, s, i)
    return at


def decoder(nc, A, out, stages="ABCDEF"):
    steps = schedule(stages)
    at = number(steps)
    with ExitStack() as ctx:
        def sb(name, shape, dt=F32):
            return ctx.enter_context(nc.sbuf_tensor("s_" + name, shape, dt))

        def ps(name):
            return ctx.enter_context(nc.psum_tensor(name, [P, 512], F32))

        def sem(name):
            return ctx.enter_context(nc.semaphore(name))

        bank = [ps(f"bank{i}") for i in range(8)]
        V = bank[0:2]
        AR = [bank[2], bank[3], bank[6]]
        O = bank[4:6]
        T = bank[7]
        G = bank[0:4]
        CW = bank[4]
        Y = bank[5:7]

        x = sb("x", [P, B * NT, D])
        xn = sb("xn", [P, 2, NT, D])
        xnT = sb("xnT", [P, 2, KD, TOK])
        stats = sb("stats", [P, 2, NT, 6])
        mv = sb("mv", [P, 2, NT, 2])
        ve = sb("ve", [P, 2, NT])
        rstd = sb("rstd", [P, 2, NT])
        mhalf = sb("mhalf", [P, NT])
        ident = sb("ident", [P, P])
        identb = sb("identb", [P, P], BF16)
        masks = sb("masks", [P, 2 * P], BF16)
        maskt = sb("maskt", [P, P], BF16)
        ctxn = sb("ctxn", [P, B * NT, D])

        early = sb("early", [P, EARLY])
        wqkv = early[:, 0:KD * 384].rearrange("p (k n) -> p k n", k=KD)
        wo = early[:, KD * 384:KD * (384 + D)].rearrange("p (k n) -> p k n", k=KD)
        bqkv = sb("bqkv", [P, 384])
        bo = sb("bo", [P, D])
        rope = sb("rope", [P, NT, 320])

        ctxT = early[:, KD * (384 + D):KD * (384 + D) + E0 * KD * D].rearrange("p (e k d) -> p e k d", e=E0, k=KD)
        mask = early[:, EARLY - E0 * TOK // 2:].bitcast(BF16).rearrange("p (e t) -> p e t", e=E0)

        NW = 3
        wmoe = sb("wmoe", [P, NW, WCOLS])
        gatew = sb("gatew", [P, 2, KD, NE])
        iota = sb("iota", [P, NE])
        sel = sb("sel", [3 * NE, ROUTED, P], BF16)
        lg = sb("lg", [P, TH, NE])
        g1 = sb("g1", [P, TH, NE])
        g2 = sb("g2", [P, TH, NE])
        gs = sb("gs", [P, TH])
        top = sb("top", [P, TH, NE])
        topi = sb("topi", [P, TH, NE], U32)
        topf = sb("topf", [P, TH, 2])
        cwp = sb("cwp", [P, TH, 3, NE], BF16)
        cwT = sb("cwT", [3 * NE, HALF], BF16)

        win = sb("win", [P, KD, CONV + DI + NV])
        wout = sb("wout", [P, DI // P, D])
        convw = sb("convw", [P, CT, KS + 1])
        zb = sb("zb", [P, DI])
        dskip = sb("dskip", [P, NV])
        tri = sb("tri", [P, 2, P])

        ARENA = 27200
        with ExitStack() as lent:
            arena = lent.enter_context(nc.sbuf_tensor("s_arena", [P, ARENA], F32))
        NA, NS_ = 4, 4
        moe_words = 4 * HALF + 2 * NA * HALF + 2 * NS_ * WCOLS
        BEFORE = ARENA - 2 * KD * TOK - moe_words
        sb("before", [P, BEFORE])
        act_ = sb("act", [P, 2, HALF])
        sg_moe = sb("sg_moe", [P, 2, HALF])
        ah, al = (sb(n, [P, NA, HALF], F32R) for n in ("ah", "al"))
        wh, wl = (sb(n, [P, NS_, WCOLS], F32R) for n in ("wh", "wl"))
        xh, xl = (sb(n, [P, KD, TOK], F32R) for n in ("xh", "xl"))
        at_ = [0]

        def cut(words, dt=F32, parts=P):
            a = arena[0:parts, at_[0]:at_[0] + words]
            at_[0] += words
            assert at_[0] <= ARENA, at_
            return a if dt is F32 else a.bitcast(dt)

        qf = cut(2 * 512).rearrange("p (c n) -> p c n", c=2)
        stk = cut(2 * 32 * KQ // 2, BF16).rearrange("p (c h s d) -> p c h s d", c=2, h=32, s=SLOTS)
        QT = cut(2 * NH * L // 2, BF16).rearrange("p (c h q) -> p c h q", c=2, h=NH)
        KT = cut(2 * NH * L // 2, BF16).rearrange("p (c h q) -> p c h q", c=2, h=NH)
        r1 = cut(512)
        vaug = cut(3 * NT * NH * VW).rearrange("p (c t g w) -> p c t g w", c=3, t=NT, g=NH)
        nM = cut(NT * NH).rearrange("p (t h) -> p t h", t=NT)
        mp = cut(NT * 2 * NH // 2, BF16).rearrange("p (t m h) -> p t m h", t=NT, m=2)
        MT = cut(L // 2, BF16, 2 * NH)
        NPT = 4
        PT = cut(NPT * 512).rearrange("p (c n) -> p c n", c=NPT)
        rs = cut(NT * NH).rearrange("p (t h) -> p t h", t=NT)
        y = cut(2 * NT * D).rearrange("p (c t d) -> p c t d", c=2, t=NT)
        yT = cut(KD * L).rearrange("p (k q) -> p k q", k=KD)
        yp = cut(512)
        attn_words = at_[0]

        at_[0] = 0
        xm = cut(2 * E0 * KD * HALF).rearrange("p (c e k t) -> p c e k t", c=2, e=E0, k=KD)
        hb = cut(KD * HALF).rearrange("p (k t) -> p k t", k=KD)
        sg = cut(2 * HALF).rearrange("p (c t) -> p c t", c=2)
        assert attn_words <= ARENA - 2 * KD * TOK and at_[0] <= BEFORE
        tok32 = xnT[:, 1, 0, :].bitcast(I32)
        tokf = xnT[:, 1, 1, :]

        at_[0] = 0
        NRAW = 2
        raw = cut(NRAW * 2 * (KS - 1 + L)).rearrange("p (c i t) -> p c i t", c=NRAW, i=2)
        xs = cut(2 * CT * L).rearrange("p (c i t) -> p c i t", c=2, i=CT)
        zt = cut(DI)
        zs = cut(2 * DI).rearrange("p (c n) -> p c n", c=2)
        NU = B * NT
        ddt = cut(NU * NV)
        dec = cut(NU * NV)
        ap_ = cut(3 * NU * NV // 2, BF16).rearrange("p (u j m g) -> p u j m g", u=NU, j=HG, m=3)
        AT = cut(2 * P // 2, BF16, RA).rearrange("p (i s) -> p i s", i=2)
        nAT = cut(2 * P // 2, BF16, RA).rearrange("p (i s) -> p i s", i=2)
        RS, RZ = NHG * HG * P // 2, NHG * P // 2
        rows_s = [a.rearrange("p (j g s) -> p j g s", j=HG, g=NHG)
                  for a in (cut(RS, BF16, RR), early[0:RR, 0:RS].bitcast(BF16))]
        rows_z = [a.rearrange("p (g z) -> p g z", g=NHG)
                  for a in (cut(RZ, BF16, RR), early[0:RR, RS:RS + RZ].bitcast(BF16))]
        XS = NHG * P
        xsp = [a.rearrange("p (g h j q w) -> p g h j q w", g=HG, h=NHG // HG, j=HG, w=PV)
               for a in (cut(XS), wmoe[:, :, :].rearrange("p n w -> p (n w)")[:, 0:XS])]
        ys = cut(DI)
        Xt = cut(2 * DI).rearrange("p (c n) -> p c n", c=2)
        Bt = cut(DI)
        XD = cut(DI)
        Du = cut(2 * DI).rearrange("p (c n) -> p c n", c=2)
        CBs = cut(2 * NG * P).rearrange("p (c g s) -> p c g s", c=2, g=NG)
        NM = 4
        M = cut(NM * 512).rearrange("p (c n) -> p c n", c=NM)
        stt = cut(NG // 2 * NS).rearrange("p (g n) -> p g n", g=NG // 2)
        yo = cut(DI)
        yf = cut(DI)
        yfT = ys.rearrange("p (k q) -> p k q", k=DI // P)
        t_a, t_abs, t_u, t_1u = (M[:, k, :] for k in range(4))
        t_max, t_rest = yf, yo

        def sems(names):
            return [sem(n) for n in names.split()]

        x_in, const_in, attn_in, ctx_in, tok_in, gate_in, mix_in, hot_in = sems(
            "x_in const_in attn_in ctx_in tok_in gate_in mix_in hot_in")
        w_in = [sem(f"w_in{i}") for i in range(NW)]
        wh_ready, wl_ready, ah_ready, al_ready, x_split = sems("wh_ready wl_ready ah_ready al_ready x_split")
        w_used, stored, init = sems("w_used stored init")
        dv, ac, pl = sems("dv ac pl")
        t_full, t_read, v_full, v_read, a_full, a_read, o_read = sems(
            "t_full t_read v_full v_read a_full a_read o_read")
        g_full, u_full, g_read, cw_full, cw_read, y_full, y_read = sems("g_full u_full g_read cw_full cw_read y_full y_read")
        ve_ready, rstd_ready, xn_ready = sems("ve_ready rstd_ready xn_ready")
        qk_ready, v_copied, parts_ready, q_stacked, stack_ready = sems(
            "qk_ready v_copied parts_ready q_stacked stack_ready")
        mp_ready, m_landed, pv_used, attn_added = sems(
            "mp_ready m_landed pv_used attn_added")
        mask_ready, xm_dve, xm_pool, hm_dve, hm_pool, s_ready = sems("mask_ready xm_dve xm_pool hm_dve hm_pool s_ready")
        gsub_ready, gexp_ready, cwp_ready = sems("gsub_ready gexp_ready cwp_ready")
        raw_cleared, conv_done, tanh_ready, xs_ready = sems("raw_cleared conv_done tanh_ready xs_ready")
        z_tanh, halved = sems("z_tanh halved")
        zs_ready, nab_ready, u_ready, w_ready, ln_ready, dt_ready = sems(
            "zs_ready nab_ready u_ready w_ready ln_ready dt_ready")
        ap_ready, decin_ready, dec_ready, rows_landed = sems("ap_ready decin_ready dec_ready rows_landed")
        xsp_ready = sem("xsp_ready")
        du_ready, xd_ready, m_ready, m_used, yf_ready = sems("du_ready xd_ready m_ready m_used yf_ready")

        first = {s: i for i, s in enumerate(stages)}
        turned = [s for s in stages if s != "E"]
        attns = [s for s in stages if s in "AE"]
        beside_c = sum(k[0] == "din" for k in at["T"])
        begun_in_d = any(kind == "v_copy" for kind, _, _ in steps)

        def ln_index(s, b):
            return first[s] * B + b

        def attn_index(s, b):
            return attns.index(s) * B + b

        def xn_of(s, b):
            if s == "E":
                k = sum(t < s for t in turned) % 2
                return xnT[:, k].rearrange("p k t -> p (k t)").rearrange("p (n d) -> p n d", d=D)[:, NT * b:NT * b + NT, :]
            return xn[:, ln_index(s, b) % 2]

        def rounded_off(s, b):
            return xn[:, 0].rearrange("p t d -> p (t d)") if (s, b) == ("E", 0) and begun_in_d else r1

        def xnT_of(s):
            return xnT[:, turned.index(s) % 2]

        def added(s, b):
            if s in "AE":
                return attn_added, attn_index(s, b) + 1
            if s in "BCF":
                return y_read, at["Y"][s, b] + 1
            return v_read, at["V"]["dy", s, NT * b + 1] + 1

        def previous(s):
            return added(stages[first[s] - 1], B - 1)


        def before_d(engine):
            if beside_c and first["C"]:
                engine.wait_ge(*previous("C"))
            elif first["D"] and not beside_c:
                engine.wait_ge(*previous("D"))

        out_v = out.rearrange("b (t p) d -> p (b t) d", p=P)
        x_v = A["x"].rearrange("b (t p) d -> p (b t) d", p=P)
        ctx_v = A["ctx"].rearrange("b (t p) d -> p (b t) d", p=P)

        def row(name, n):
            return A[name].rearrange("(a n) -> a n", a=1).to_broadcast([P, n])

        block = ctx.enter_context(nc.Block())

        def g_other(s):
            return sum(k[0] == "b_h" for k in at["G"])

        def moe_half(s, hf):
            return 2 * (s == "F" and "C" in first) + hf

        def stage_of(ring, key):
            return key[0] if ring == "Y" else key[1]

        def w_all(s):
            return 2 * (SHARED[s] + ROUTED)

        def stack_end(k, t):
            return at["A"]["stack_t", attns[k // B], k % B, t, 2]

        @block.sync
        def _(sp):
            for b in range(B):
                sp.dma_start(x[:, NT * b:NT * b + NT, :], x_v[:, NT * b:NT * b + NT, :]).then_inc(x_in, 16)
            for dst, name in ((ident, "ident"), (identb, "identb"), (masks, "masks"), (maskt, "maskt")):
                sp.dma_start(dst[:, :], A[name]).then_inc(const_in, 16)
            for dst, name in ((wqkv, "wqkv"), (wo, "wo"), (rope, "rope")):
                sp.dma_start(dst[:, :, :], A[name]).then_inc(attn_in, 16)
            sp.dma_start(bqkv[:, :], row("bqkv", 384)).then_inc(attn_in, 16)
            sp.dma_start(bo[:, :], row("bo", D)).then_inc(attn_in, 16)
            sp.dma_start(tok32, row("tok", TOK)).then_inc(tok_in, 16)
            sp.dma_start(ctxT[:, :, :, :], A["ctxT"]).then_inc(ctx_in, 16)
            sp.dma_start(ctxn[:, :, :], ctx_v).then_inc(ctx_in, 16)
            sp.dma_start(gatew[:, :, :, :], A["gatew"]).then_inc(gate_in, 16)
            sp.dma_start(iota[:, :], A["iota"]).then_inc(gate_in, 16)
            sp.dma_start(sel[:, :, :], A["sel"]).then_inc(gate_in, 16)
            sp.dma_start(win[:, :, :], A["win"]).then_inc(mix_in, 16)
            sp.dma_start(wout[:, :, :], A["wout"]).then_inc(mix_in, 16)
            sp.dma_start(convw[:, :, :], A["convw"]).then_inc(mix_in, 16)
            sp.dma_start(zb[:, :], row("zb", DI)).then_inc(mix_in, 16)
            sp.dma_start(dskip[:, :], row("dskip", NV)).then_inc(mix_in, 16)
            sp.dma_start(tri[:, :, :], A["tri"]).then_inc(mix_in, 16)
            for kind, s, i in steps:
                if kind == "m_t":
                    k = attn_index(s, i)
                    sp.wait_ge(t_read, at["T"]["m_t", s, i] + 1)
                    if k >= 2:
                        sp.wait_ge(pv_used, 8 * (k - 1))
                    for m in range(2):
                        sp.dma_start(QT[KQ + m:KQ + m + 1, k % 2, :, :],
                                     MT[m * NH:(m + 1) * NH, :]).then_inc(m_landed, 16)
                elif kind == "switch" and s == "D":
                    if first[s]:
                        sp.wait_ge(*previous(s))
                    sp.wait_ge(attn_in, 80)
                    sp.wait_ge(ctx_in, 32)
                    for c in range(2):
                        sp.dma_start(rows_s[c][3:RR, :, :, :], A["onehot"]).then_inc(hot_in, 16)
                        sp.dma_start(rows_z[c][0:3, :, :], A["ones3"]).then_inc(hot_in, 16)
                elif kind == "moe" and i[1] < SHARED[s] + ROUTED:
                    k = at["G"]["moe", s, i[0], i[1]] - g_other(s)
                    if k >= NW:
                        sp.wait_ge(wl_ready, k - NW + 1)
                    sp.dma_start(wmoe[:, k % NW, :], A["w" + s][i[1]]).then_inc(w_in[k % NW], 16)
                elif kind == "at":
                    sp.wait_ge(t_read, at["T"]["at", s, i] + 1)
                    if i >= 2:
                        sp.wait_ge(a_full, at["A"]["ssd", s, i - 2, NHG - 1] + 1)
                    for j in range(HG):
                        h = 3 * NHG * (j % 2)
                        sp.dma_start(rows_s[i % 2][0:3, j, :, :], AT[h:h + 3 * NHG, j // 2, :]).then_inc(rows_landed, 16)
                    for h in range(2):
                        sp.dma_start(rows_z[i % 2][3 + 6 * h:9 + 6 * h, :, :], nAT[:, h, :]).then_inc(rows_landed, 16)
            for landed, loads in ((x_in, 4), (tok_in, 1), (const_in, 4), (attn_in, 5), (ctx_in, 2), (gate_in, 3), (mix_in, 6)):
                sp.wait_ge(landed, 16 * loads)
            for b in range(B):
                sp.wait_ge(*added(stages[-1], b))
                sp.dma_start(out_v[:, NT * b:NT * b + NT, :], x[:, NT * b:NT * b + NT, :]).then_inc(stored, 16)
            sp.wait_ge(stored, 16 * B)

        @block.gpsimd
        def _(pool):
            g = nc.gpsimd
            own = [0]

            def link(ins):
                own[0] += 1
                ins.then_inc(pl, 1)
                pool.wait_ge(pl, own[0])

            link(g.memset(mhalf[:, :], -0.5))
            for kind, s, i in steps:
                if kind == "ln":
                    n = ln_index(s, i)
                    pool.wait_ge(ve_ready, n + 1)
                    g.tensor_tensor(rstd[:, n % 2, :], ve[:, n % 2, :], mhalf[:, :], ALU.pow).then_inc(rstd_ready, 1)
                elif kind == "switch" and s in "AE":
                    if first[s]:
                        pool.wait_ge(*previous(s))
                    pool.wait_ge(rstd_ready, B * (first[s] + 1) - (s == "E" and "D" in first))
                    if s == "E" and begun_in_d:
                        pool.wait_ge(stack_ready, NT * (attn_index(s, 0) + 1))
                    link(g.memset(KT[KQ:P, :, :, :], 1.0))
                    g.memset(vaug[:, :, :, :, HD:HD + 1], 1.0)
                    g.memset(vaug[:, :, :, :, HD + 1:VW], 0.0).then_inc(init, 1)
                elif kind == "qkv_split":
                    i, t = i
                    k = attn_index(s, i)
                    nk = NKV if s == "A" else NH
                    if not (s == "E" and i == 0 and begun_in_d):
                        pool.wait_ge(qk_ready, NT * k + t + 1)
                        if k >= 3:
                            pool.wait_ge(pv_used, 8 * (k - 2))
                        src = qf[:, t, 320:384] if s == "A" else ctxn[:, NT * i + t, :]
                        g.tensor_copy(vaug[:, k % 3, t, 0:nk, 0:HD],
                                      src.rearrange("p (g w) -> p g w", g=nk)).then_inc(v_copied, 1)
                    pool.wait_ge(parts_ready, NT * k + t + 1)
                    st = stk[:, t]
                    g.tensor_copy(st[:, NH:NH + nk, 2:5:2, :],
                                  st[:, NH:NH + nk, 0, :].unsqueeze(2).to_broadcast([P, nk, 2, HD]))
                    g.tensor_copy(st[:, NH:NH + nk, 1, :], st[:, NH:NH + nk, 5, :]).then_inc(stack_ready, 1)
                elif kind == "v_copy":
                    k = attn_index(s, i)
                    pool.wait_ge(ctx_in, 32)
                    if k >= 3:
                        pool.wait_ge(pv_used, 8 * (k - 2))
                    for t in range(NT):
                        g.tensor_copy(vaug[:, k % 3, t, 0:NH, 0:HD],
                                      ctxn[:, NT * i + t, :].rearrange("p (g w) -> p g w", g=NH)).then_inc(v_copied, 1)
                elif kind == "lt" and s in "CF":
                    pool.wait_ge(t_read, at["T"]["lt", s, i] + 1)
                    if s == "F" and "C" in first:
                        pool.wait_ge(w_used, w_all("C"))
                    n = B * (s == "F" and "C" in first) + i
                    cols = slice(i * L, (i + 1) * L)
                    link(g.tensor_copy(xh[:, :, cols], xnT_of(s)[:, :, cols]))
                    g.tensor_tensor(xl[:, :, cols], xnT_of(s)[:, :, cols], xh[:, :, cols], ALU.subtract).then_inc(x_split, 1)
                elif kind == "w_split":
                    w = (w_all("C") if s == "F" and "C" in first else 0) + i
                    pool.wait_ge(wh_ready, w + 1)
                    g.tensor_tensor(wl[:, w % NS_, :], wmoe[:, w % NW, :], wh[:, w % NS_, :], ALU.subtract).then_inc(wl_ready, 1)
                elif kind == "b_mask":
                    pool.wait_ge(mask_ready, E0 - 2)
                    pool.wait_ge(t_read, at["T"]["lt", s, 2 * i + 1] + 1)
                    for e in range(DVE_EXPERTS, E0):
                        g.tensor_tensor(xm[:, i, e], xnT_of(s)[:, :, i * HALF:(i + 1) * HALF],
                                        mask[:, e, i * HALF:(i + 1) * HALF].unsqueeze(1).to_broadcast([P, KD, HALF]),
                                        ALU.mult).then_inc(xm_pool, 1)
                elif kind == "b_h":
                    pool.wait_ge(g_read, at["G"]["b_h", s, i, KD - 1] + 1)
                    for e in range(DVE_EXPERTS, E0):
                        g.tensor_tensor(xm[:, i, e], hb[:, :, :],
                                        mask[:, e, i * HALF:(i + 1) * HALF].unsqueeze(1).to_broadcast([P, KD, HALF]),
                                        ALU.mult).then_inc(hm_pool, 1)
                elif kind == "d_init":
                    before_d(pool)
                    g.memset(raw[:, :, :, 0:KS - 1], 0.0).then_inc(raw_cleared, 1)
                    pool.wait_ge(raw_cleared, 1)
                elif kind == "switch" and s == "D":
                    if first[s]:
                        pool.wait_ge(*previous(s))
                elif kind == "dt":
                    pool.wait_ge(t_read, at["T"]["dt_in", s, i] + 1)
                    link(g.tensor_scalar(t_max, t_a, 0.0, None, ALU.max))
                    link(g.tensor_tensor(t_abs, t_max, t_max, ALU.add))
                    g.tensor_tensor(t_abs, t_abs, t_a, ALU.subtract).then_inc(nab_ready, 1)
                    pool.wait_ge(u_ready, 1)
                    g.tensor_scalar(t_1u, t_u, 1.0, None, ALU.add).then_inc(w_ready, 1)
                    pool.wait_ge(w_ready, 1)
                    link(g.tensor_scalar(t_rest, t_1u, -1.0, None, ALU.add))
                    g.tensor_tensor(t_u, t_u, t_rest, ALU.subtract).then_inc(w_ready, 1)
                    g.memset(xsp[0], 0.0)
                    link(g.memset(xsp[1], 0.0))
                elif kind == "xt":
                    c = i % 2
                    pool.wait_ge(a_read, at["A"]["xt", s, i, 0] + 1)
                    pool.wait_ge(dt_ready, 2)
                    if i >= 2:
                        pool.wait_ge(yf_ready, i - 1)
                    if i >= 2:
                        pool.wait_ge(m_used, NHG * (i - 1))
                    x5 = Xt[:, c, :].rearrange("p (j g q w) -> p g j q w", j=HG, g=HG, w=PV)
                    for h in range(HG):
                        ins = g.tensor_copy(xsp[c][:, :, h, :, h, :], x5[:, :, :, h, :])
                    ins.then_inc(xsp_ready, 1)
                    g.tensor_tensor(Du[:, c, :].rearrange("p (h w) -> p h w", w=PV),
                                    Xt[:, c, :].rearrange("p (h w) -> p h w", w=PV),
                                    ddt[:, i * NV:(i + 1) * NV].unsqueeze(2).to_broadcast([P, NV, PV]), ALU.mult).then_inc(du_ready, 1)
                    if c == 0:
                        pool.wait_ge(dec_ready, 1)
                        if i:
                            pool.wait_ge(t_full, at["T"]["state", s, i - 2] + 1)
                        g.tensor_tensor(XD.rearrange("p (h w) -> p h w", w=PV),
                                        Xt[:, c, :].rearrange("p (h w) -> p h w", w=PV),
                                        dec[:, i * NV:(i + 1) * NV].unsqueeze(2).to_broadcast([P, NV, PV]), ALU.mult).then_inc(xd_ready, 1)

        @block.scalar
        def _(act):
            a = nc.scalar
            own = [0]

            def link(ins):
                own[0] += 1
                ins.then_inc(ac, 1)
                act.wait_ge(ac, own[0])

            def start(s):
                if first[s] and s != "C":
                    act.wait_ge(*previous(s))

            for kind, s, i in steps:
                if kind == "switch":
                    start(s)
                elif kind == "lt":
                    act.wait_ge(t_full, at["T"]["lt", s, i] + 1)
                    a.copy(xnT_of(s)[:, :, i * L:(i + 1) * L], T[:, :].rearrange("p (k q) -> p k q", k=KD)
                           ).then_inc(t_read, 1)
                elif kind == "stack_t":
                    k = attn_index(s, i)
                    if k >= 2:
                        act.wait_ge(pv_used, 8 * (k - 1))
                    for t in range(NT):
                        for j in (0, 2):
                            n = at["A"]["stack_t", s, i, t, j]
                            act.wait_ge(a_full, n + 1)
                            heads = 4 if j == 2 and s == "A" else 8
                            src = AR[n % 3][:, :].bitcast(BF16)[0:KQ, 0:heads * P].rearrange("p (h q) -> p h q", h=heads)
                            to = QT if j < 2 else KT
                            a.copy(to[0:KQ, k % 2, 0:heads, t * P:(t + 1) * P], src).then_inc(a_read, 1)
                elif kind == "m_t":
                    k = attn_index(s, i)
                    act.wait_ge(t_full, at["T"]["m_t", s, i] + 1)
                    if k:
                        act.wait_ge(m_landed, 32 * k)
                    a.copy(MT[:, :], T[:, :].bitcast(BF16)[0:2 * NH, 0:L]).then_inc(t_read, 1)
                elif kind == "pv":
                    b, j = i
                    n = at["A"]["pv", s, b, j]
                    p = NB * attn_index(s, b) + j
                    act.wait_ge(a_full, n + 1)
                    if p >= NPT:
                        kk, jj = divmod(p - NPT, NB)
                        act.wait_ge(pv_used, 8 * kk + 1 + (jj if jj < 4 else 4 + (jj - 4) // 2))
                    a.activation(PT[:, p % NPT, :], AR[n % 3][:, :], ACT.Exp).then_inc(a_read, 1)
                elif kind == "y_t" and s != "D":
                    b, q = i
                    act.wait_ge(pv_used, 8 * attn_index(s, b) + 4 * (q + 1))
                    if (b, q) > (0, 0):
                        act.wait_ge(v_full, at["V"]["y_t", s, (b - 1 + q, 1 - q)] + 1)
                    a.copy(yp[:, :], O[at["O"]["pv", s, b, q] % 2][:, :]).then_inc(o_read, 1)
                elif kind == "o_t" and s == "A":
                    act.wait_ge(t_full, at["T"]["o_t", s, i] + 1)
                    if i:
                        act.wait_ge(v_full, at["V"]["o", s, i - 1] + 1)
                    a.copy(yT[:, :, :], T[:, :].rearrange("p (k q) -> p k q", k=KD)).then_inc(t_read, 1)
                elif kind == "b_h":
                    for f in range(KD):
                        n = at["G"]["b_h", s, i, f]
                        act.wait_ge(g_full, n + 1)
                        if n >= 2:
                            act.wait_ge(g_read, n - 1)
                        a.activation(sg[:, n % 2, :], G[2 * (n % 2)][:, :], ACT.Silu).then_inc(s_ready, 1)
                elif kind == "gate":
                    act.wait_ge(t_full, at["T"]["gate", s, i] + 1)
                    h = 2 * (s == "F" and "C" in first) + i
                    if h:
                        act.wait_ge(cwp_ready, h)
                    a.copy(lg[:, :, :], T[:, 0:TH * NE].rearrange("p (t e) -> p t e", t=TH)).then_inc(t_read, 1)
                    act.wait_ge(gsub_ready, h + 1)
                    a.activation(g2[:, :, :], g1[:, :, :], ACT.Exp).then_inc(gexp_ready, 1)
                elif kind == "cw_t":
                    act.wait_ge(t_full, at["T"]["cw_t", s, i] + 1)
                    m = [v for (kk, ss, hh, jj), v in at["W"].items() if (ss, hh) < (s, i)]
                    if m:
                        act.wait_ge(cw_full, max(m) + 1)
                    a.copy(cwT[:, :], T[:, :].bitcast(BF16)[0:3 * NE, 0:HALF]).then_inc(t_read, 1)
                elif kind == "moe" and i[1] < SHARED[s] + ROUTED:
                    n = at["G"]["moe", s, i[0], i[1]]
                    act.wait_ge(g_full, n + 1)
                    if n >= 2:
                        act.wait_ge(g_read, n - 1)
                    a.activation(sg_moe[:, n % 2, :], G[2 * (n % 2)][:, :], ACT.Silu).then_inc(s_ready, 1)
                elif kind == "w_split":
                    w = (w_all("C") if s == "F" and "C" in first else 0) + i
                    act.wait_ge(w_in[w % NW], 16 * (w // NW + 1))
                    if w >= NS_:
                        act.wait_ge(w_used, w - NS_ + 1)
                    a.copy(wh[:, w % NS_, :], wmoe[:, w % NW, :]).then_inc(wh_ready, 1)
                elif kind == "a_split":
                    hf, j = i
                    n = at["G"]["moe", s, hf, j]
                    w = n - g_other(s)
                    if j < SHARED[s]:
                        act.wait_ge(g_read, n + 1)
                    else:
                        act.wait_ge(cw_read, at["W"]["moe", s, hf, j] + 1)
                    if w >= NA:
                        act.wait_ge(w_used, w - NA + 1)
                    a.copy(ah[:, w % NA, :], act_[:, w % 2, :]).then_inc(ah_ready, 1)
                elif kind == "din":
                    b, j = i
                    m = b * (CT // 2) + j
                    if m < beside_c:
                        act.wait_ge(t_full, at["T"]["din", s, b, j] + 1)
                        bk, read = T, t_read
                    else:
                        n = at["A"]["din", s, b, j]
                        act.wait_ge(a_full, n + 1)
                        bk, read = AR[n % 3], a_read
                    if m >= NRAW:
                        act.wait_ge(xs_ready, m - NRAW + 1)
                    act.wait_ge(halved, 1)
                    if b >= 2:
                        act.wait_ge(v_read, at["V"]["state", s, NT * (b - 2) + 1, 1] + 1)
                    pair = bk[:, :].rearrange("p (i t) -> p i t", i=2)
                    for h in range(2):
                        ct = 2 * j + h
                        a.activation(xs[:, b % 2, ct, :], pair[:, h, :], ACT.Identity,
                                     bias=convw[:, ct, KS:KS + 1], scale=convw[:, ct, KS - 1:KS])
                    a.copy(raw[:, m % NRAW, :, KS - 1:], pair).then_inc(read, 1)
                elif kind == "th":
                    b, j = i
                    m = b * (CT // 2) + j
                    act.wait_ge(conv_done, (KS - 1) * (m + 1))
                    if m < beside_c:
                        half = xs[:, b % 2, 2 * j:2 * j + 2, :]
                        a.activation(half, half, ACT.Silu, scale=2.0).then_inc(xs_ready, 1)
                        continue
                    a.activation(raw[:, m % NRAW, :, KS - 1:], xs[:, b % 2, 2 * j:2 * j + 2, :], ACT.Tanh
                                 ).then_inc(tanh_ready, 1)
                elif kind == "dt_in":
                    act.wait_ge(t_full, at["T"]["dt_in", s, i] + 1)
                    a.copy(t_a, T[:, :]).then_inc(t_read, 1)
                elif kind == "zs":
                    act.wait_ge(v_read, at["V"]["dz", s, i] + 1)
                    if i >= 2:
                        act.wait_ge(yf_ready, i - 1)
                    a.activation(zs[:, i % 2, :], zt[:, :], ACT.Tanh).then_inc(z_tanh, 1)
                elif kind == "dt":
                    act.wait_ge(nab_ready, 1)
                    a.activation(t_u, t_abs, ACT.Exp, scale=-1.0).then_inc(u_ready, 1)
                    act.wait_ge(w_ready, 1)
                    a.activation(t_abs, t_1u, ACT.Ln).then_inc(ln_ready, 1)
                    act.wait_ge(ln_ready, 1)
                    act.wait_ge(w_ready, 2)
                    a.activation(t_1u, t_abs, ACT.Exp, scale=-1.0).then_inc(ln_ready, 1)
                elif kind == "acum":
                    for k, t in ((0, t_a), (1, t_u)):
                        act.wait_ge(t_full, at["T"]["acum", s, k] + 1)
                        a.copy(t, T[:, :]).then_inc(t_read, 1)
                    act.wait_ge(decin_ready, 1)
                    a.activation(dec, dec, ACT.Exp).then_inc(dec_ready, 1)
                elif kind == "at":
                    act.wait_ge(t_full, at["T"]["at", s, i] + 1)
                    if i:
                        act.wait_ge(rows_landed, 16 * 6 * i)
                    src = T[:, :].bitcast(BF16)[0:RA, 0:2 * P].rearrange("p (i s) -> p i s", i=2)
                    a.copy(AT[:, :, :], src)
                    a.activation(nAT[:, :, :], src, ACT.Copy, scale=-1.0).then_inc(t_read, 1)
                elif kind == "xt":
                    n = at["A"]["xt", s, i, 0]
                    act.wait_ge(a_full, n + 1)
                    if i >= 2:
                        act.wait_ge(xsp_ready, i - 1)
                        act.wait_ge(du_ready, i - 1)
                        act.wait_ge(xd_ready, (i - 2) // 2 + 1)
                    a.copy(Xt[:, i % 2, :], AR[n % 3][:, :]).then_inc(a_read, 1)
                    if i % 2 == 0:
                        n = at["A"]["xt", s, i, 1]
                        act.wait_ge(a_full, n + 1)
                        if i:
                            act.wait_ge(t_full, at["T"]["state", s, i - 2] + 1)
                        a.copy(Bt, AR[n % 3][:, :]).then_inc(a_read, 1)
                elif kind == "ssd":
                    u, hg = i
                    n = at["A"]["ssd", s, u, hg]
                    k = NHG * u + hg
                    act.wait_ge(a_full, n + 1)
                    if k >= NM:
                        act.wait_ge(m_used, k - NM + 1)
                    a.activation(M[:, k % NM, :], AR[n % 3][:, :], ACT.Exp).then_inc(a_read, 1)
                elif kind == "state" and i % 2 == 0:
                    act.wait_ge(t_full, at["T"]["state", s, i] + 1)
                    if i:
                        act.wait_ge(v_full, at["V"]["state", s, i - 1, 1] + 1)
                    a.copy(stt[:, :, :], T[:, 0:NG // 2 * NS].rearrange("p (g n) -> p g n", g=NG // 2)).then_inc(t_read, 1)
                elif kind == "y_t" and s == "D":
                    act.wait_ge(m_used, NHG * (i + 1))
                    if i:
                        act.wait_ge(v_full, at["V"]["dy", s, i - 1] + 1)
                    a.copy(ys, O[at["O"]["ssd", s, i] % 2][:, :]).then_inc(o_read, 1)
                elif kind == "dy_t":
                    act.wait_ge(t_full, at["T"]["dy_t", s, i] + 1)
                    if i:
                        act.wait_ge(v_full, at["V"]["dy", s, i - 1] + 1)
                    a.copy(yfT[:, :, :], T[:, :].rearrange("p (k q) -> p k q", k=DI // P)).then_inc(t_read, 1)

        @block.tensor
        def _(pe):
            mm = nc.tensor.matmul
            tr = nc.tensor.transpose

            def t_bank(*key):
                if at["T"][key]:
                    pe.wait_ge(t_read, at["T"][key])
                return T

            def v_bank(*key):
                n = at["V"][key]
                if n >= 2:
                    pe.wait_ge(v_read, n - 1)
                return V[n % 2]

            def a_bank(*key):
                n = at["A"][key]
                if n >= 3:
                    pe.wait_ge(a_read, n - 2)
                return AR[n % 3]

            def o_bank(*key):
                n = at["O"][key]
                if n >= 2:
                    pe.wait_ge(o_read, n - 1)
                return O[n % 2]

            def scan(s, u, hg):
                k = NHG * u + hg
                if hg == 0:
                    bk = o_bank("ssd", s, u)
                    pe.wait_ge(xsp_ready, u + 1)
                pe.wait_ge(m_ready, k + 1)
                bk = O[at["O"]["ssd", s, u] % 2]
                quarter, h = divmod(hg, HG)
                for j in range(HG):
                    ins = mm(bk[j * 32:(j + 1) * 32, quarter * P:(quarter + 1) * P],
                             xsp[u % 2][:, quarter, h, j, :, :].rearrange("p q w -> p (q w)"),
                             M[:, k % NM, j * P:(j + 1) * P], start=(h == 0), stop=(h == HG - 1), skip_group_check=True)
                ins.then_inc(m_used, 1)

            pe.wait_ge(const_in, 64)
            for kind, s, i in steps:
                if kind == "switch":
                    if first[s] and s != "C":
                        pe.wait_ge(*previous(s))
                        for ring, read in (("V", v_read), ("A", a_read), ("O", o_read), ("G", g_read),
                                           ("W", cw_read), ("Y", y_read)):
                            done = sum(1 for key in at[ring] if stage_of(ring, key) in first
                                       and first[stage_of(ring, key)] < first[s])
                            if done:
                                pe.wait_ge(read, done)
                    if s == "A":
                        pe.wait_ge(attn_in, 80)
                    if s == "B":
                        pe.wait_ge(ctx_in, 32)
                    if s in "CF":
                        pe.wait_ge(gate_in, 48)
                    if s == "D":
                        pe.wait_ge(mix_in, 96)
                elif kind == "lt":
                    n = ln_index(s, i)
                    bk = t_bank("lt", s, i)
                    pe.wait_ge(xn_ready, n + 1)
                    for k in range(KD):
                        for t in range(NT):
                            ins = tr(bk[:, (k * NT + t) * P:(k * NT + t + 1) * P], xn_of(s, i)[:, t, k * P:(k + 1) * P],
                                     ident[:, :])
                    ins.then_inc(t_full, 1)
                elif kind == "qkv_mm" and s == "A":
                    i, t = i
                    pe.wait_ge(t_read, at["T"]["lt", s, i] + 1)
                    bk = v_bank("qkv_mm", s, i, t)
                    for k in range(KD):
                        ins = mm(bk[:, 0:384], xnT_of(s)[:, k, i * L + t * P:i * L + (t + 1) * P], wqkv[:, k, :],
                                 start=(k == 0), stop=(k == KD - 1))
                    ins.then_inc(v_full, 1)
                elif kind == "stack_t":
                    kk = attn_index(s, i)
                    for t in range(NT):
                        pe.wait_ge(q_stacked, NT * kk + t + 1)
                        pe.wait_ge(stack_ready, NT * kk + t + 1)
                        for j in range(3 if s == "A" else 4):
                            heads = 4 if j == 2 and s == "A" else 8
                            bank_of, full = ((a_bank, a_full), (v_bank, v_full))[j % 2]
                            bk = bank_of("stack_t", s, i, t, j)
                            for h in range(heads):
                                ins = tr(bk[:, :].bitcast(BF16)[0:KQ, h * P:(h + 1) * P],
                                         stk[:, t, 8 * j + h, :, :].rearrange("p s d -> p (s d)"), identb[:, :])
                            ins.then_inc(full, 1)
                elif kind == "s":
                    b, j = i
                    c = attn_index(s, b) % 2
                    pe.wait_ge(a_read, at["A"]["stack_t", s, b, NT - 1, 2] + 1)
                    pe.wait_ge(v_read, at["V"]["stack_t", s, b, NT - 1, 1 if s == "A" else 3] + 1)
                    bk = v_bank("s", s, b, j)
                    if j < 4:
                        mm(bk[:, :], identb[:, :], masks[:, P:2 * P].unsqueeze(1).to_broadcast([P, 4, P]),
                           start=True, stop=False, skip_group_check=True)
                        for h in range(4 * j, 4 * j + 4):
                            g = h // (NH // NKV) if s == "A" else h
                            ins = mm(bk[:, (h % 4) * P:(h % 4 + 1) * P], QT[0:KQ, c, h, 0:P], KT[0:KQ, c, g, 0:P],
                                     start=False, stop=(h % 4 == 3), skip_group_check=True)
                    else:
                        mm(bk[:, :], identb[:, :], masks[:, :].unsqueeze(1).to_broadcast([P, 2, 2 * P]),
                           start=True, stop=False, skip_group_check=True)
                        for h in range(2 * (j - 4), 2 * (j - 4) + 2):
                            g = h // (NH // NKV) if s == "A" else h
                            ins = mm(bk[:, (h % 2) * L:(h % 2 + 1) * L], QT[0:KQ, c, h, P:L], KT[0:KQ, c, g, :],
                                     start=False, stop=(h % 2 == 1), skip_group_check=True)
                    ins.then_inc(v_full, 1)
                elif kind == "m_t":
                    k = attn_index(s, i)
                    bk = t_bank("m_t", s, i)
                    pe.wait_ge(mp_ready, k + 1)
                    for q in range(NT):
                        ins = tr(bk[:, :].bitcast(BF16)[0:2 * NH, q * P:(q + 1) * P],
                                 mp[:, q, :, :].rearrange("p m h -> p (m h)"), identb[:, :])
                    ins.then_inc(t_full, 1)
                elif kind == "pv":
                    i, step = i
                    ka = attn_index(s, i)
                    c = ka % 2
                    if step == 0:
                        pe.wait_ge(m_landed, 32 * (ka + 1))
                        pe.wait_ge(v_copied, NT * (ka + 1))
                        pe.wait_ge(init, attns.index(s) + 1)
                    def scores(j):
                        q, kt, h4 = (0, 0, j) if j < 4 else (1, (j - 4) % 2, (j - 4) // 2)
                        bk = a_bank("pv", s, i, j)
                        diag = q == kt
                        if diag:
                            mm(bk[:, :], identb[:, :], maskt[:, :].unsqueeze(1).to_broadcast([P, 4, P]),
                               start=True, stop=False, skip_group_check=True)
                        if s == "A":
                            ins = mm(bk[:, :], KT[0:KQ + 2, c, h4, kt * P:(kt + 1) * P],
                                     QT[0:KQ + 2, c, 4 * h4:4 * h4 + 4, q * P:(q + 1) * P],
                                     start=not diag, stop=True, skip_group_check=True)
                        else:
                            for h in range(4 * h4, 4 * h4 + 4):
                                ins = mm(bk[:, (h % 4) * P:(h % 4 + 1) * P], KT[0:KQ + 2, c, h, kt * P:(kt + 1) * P],
                                         QT[0:KQ + 2, c, h, q * P:(q + 1) * P],
                                         start=not diag, stop=True, skip_group_check=True)
                        ins.then_inc(a_full, 1)

                    def values(j):
                        q, h4 = (0, j) if j < 4 else (1, j - 4)
                        kept = [12 * ka + j] if q == 0 else [12 * ka + 4 + 2 * h4, 12 * ka + 5 + 2 * h4]
                        bk = O[at["O"]["pv", s, i, q] % 2]
                        if h4 == 0:
                            o_bank("pv", s, i, q)
                        pe.wait_ge(a_read, at["A"]["pv", s, i, j if q == 0 else 5 + 2 * h4] + 1)
                        for kt in range(q + 1):
                            for h in range(4 * h4, 4 * h4 + 4):
                                g = h // (NH // NKV) if s == "A" else h
                                c32 = slice(VW * (h % 4), VW * (h % 4) + VW)
                                ins = mm(bk[c32, h4 * P:(h4 + 1) * P], vaug[:, ka % 3, kt, g, :],
                                         PT[:, kept[kt] % NPT, (h % 4) * P:(h % 4 + 1) * P],
                                         start=(kt == 0), stop=(kt == q), skip_group_check=True)
                        ins.then_inc(pv_used, 1)

                    scores(step)
                    if 1 <= step <= 4:
                        values(step - 1)
                    elif step in (7, 9, 11):
                        values(4 + (step - 7) // 2)
                    if step == NB - 1:
                        values(7)
                elif kind == "y_t" and s == "D":
                    bk = v_bank("y_t", s, i)
                    pe.wait_ge(o_read, at["O"]["ssd", s, i] + 1)
                    for q in range(HG):
                        ins = tr(bk[:, q * P:(q + 1) * P], ys[:, q * P:(q + 1) * P], ident[:, :])
                    ins.then_inc(v_full, 1)
                elif kind == "y_t":
                    b, q = i
                    bk = v_bank("y_t", s, i)
                    pe.wait_ge(o_read, at["O"]["pv", s, b, q] + 1)
                    for h4 in range(4):
                        ins = tr(bk[:, h4 * P:(h4 + 1) * P], yp[:, h4 * P:(h4 + 1) * P], ident[:, :])
                    ins.then_inc(v_full, 1)
                elif kind == "o_t" and s == "A":
                    k = attn_index(s, i)
                    bk = t_bank("o_t", s, i)
                    pe.wait_ge(v_read, at["V"]["y_t", s, (i, 1)] + 1)
                    for d in range(KD):
                        for t in range(NT):
                            ins = tr(bk[:, (d * NT + t) * P:(d * NT + t + 1) * P], y[:, k % 2, t, d * P:(d + 1) * P],
                                     ident[:, :])
                    ins.then_inc(t_full, 1)
                elif kind == "o" and s == "A":
                    bk = v_bank("o", s, i)
                    pe.wait_ge(t_read, at["T"]["o_t", s, i] + 1)
                    for t in range(NT):
                        for d in range(KD):
                            ins = mm(bk[:, t * D:(t + 1) * D], yT[:, d, t * P:(t + 1) * P], wo[:, d, :],
                                     start=(d == 0), stop=(d == KD - 1))
                    ins.then_inc(v_full, 1)
                elif kind == "b_h":
                    pe.wait_ge(xm_dve, DVE_EXPERTS * (i + 1))
                    pe.wait_ge(xm_pool, (E0 - DVE_EXPERTS) * (i + 1))
                    for f in range(KD):
                        n = at["G"]["b_h", s, i, f]
                        if n >= 2:
                            pe.wait_ge(g_read, n - 1)
                        bk = G[2 * (n % 2)]
                        for e in range(E0):
                            for k in range(KD):
                                ins = mm(bk[:, :], ctxT[:, e, k, f * P:(f + 1) * P], xm[:, i, e, k, :],
                                         start=(e == 0 and k == 0), stop=(e == E0 - 1 and k == KD - 1))
                        ins.then_inc(g_full, 1)
                elif kind == "b_y":
                    hf, b = divmod(i, 2)
                    pe.wait_ge(hm_dve, DVE_EXPERTS * (hf + 1))
                    pe.wait_ge(hm_pool, (E0 - DVE_EXPERTS) * (hf + 1))
                    n = at["Y"][s, i]
                    if n >= 2:
                        pe.wait_ge(y_read, n - 1)
                    for t in range(NT):
                        for e in range(E0):
                            for k in range(KD):
                                ins = mm(Y[b][:, t * D:(t + 1) * D], xm[:, hf, e, k, (b * NT + t) * P:(b * NT + t + 1) * P],
                                         ctxT[:, e, k, :], start=(e == 0 and k == 0), stop=(e == E0 - 1 and k == KD - 1))
                    ins.then_inc(y_full, 1)
                elif kind == "gate":
                    bk = t_bank("gate", s, i)
                    pe.wait_ge(t_read, at["T"]["lt", s, 2 * i + 1] + 1)
                    for t in range(TH):
                        for k in range(KD):
                            ins = mm(bk[:, t * NE:(t + 1) * NE], xnT_of(s)[:, k, (TH * i + t) * P:(TH * i + t + 1) * P],
                                     gatew[:, int(s == "F"), k, :], start=(k == 0), stop=(k == KD - 1))
                    ins.then_inc(t_full, 1)
                elif kind == "cw_t":
                    bk = t_bank("cw_t", s, i)
                    pe.wait_ge(cwp_ready, moe_half(s, i) + 1)
                    for t in range(TH):
                        ins = tr(bk[:, :].bitcast(BF16)[0:3 * NE, t * P:(t + 1) * P],
                                 cwp[:, t, :, :].rearrange("p m e -> p (m e)"), identb[:, :])
                    ins.then_inc(t_full, 1)
                elif kind == "moe":
                    hf, j = i
                    last = SHARED[s] + ROUTED
                    toks = slice(hf * HALF, (hf + 1) * HALF)
                    if j < last:
                        n = at["G"]["moe", s, hf, j]
                        w = n - g_other(s)
                        wth, wtl = (a_[:, w % NS_, 0:2 * KD * P].rearrange("p (k g f) -> p k g f", k=KD, g=2)
                                    for a_ in (wh, wl))
                        if n >= 2:
                            pe.wait_ge(g_read, n - 1)
                        if j == 0:
                            pe.wait_ge(x_split, B * (s == "F" and "C" in first) + 2 * hf + 2)
                        pe.wait_ge(wl_ready, w + 1)
                        parts = [(a_, b_, k) for a_, b_ in ((wth, xh), (wth, xl), (wtl, xh)) for k in range(KD)]
                        for half, full in ((0, g_full), (1, u_full)):
                            for p_, (a_, b_, k) in enumerate(parts):
                                ins = mm(G[2 * (n % 2) + half][:, :], a_[:, k, half, :], b_[:, k, toks],
                                         start=(p_ == 0), stop=(p_ == len(parts) - 1))
                            ins.then_inc(full, 1)
                        if j >= SHARED[s]:
                            m = at["W"]["moe", s, hf, j]
                            if m:
                                pe.wait_ge(cw_read, m)
                            if j == SHARED[s]:
                                pe.wait_ge(t_read, at["T"]["cw_t", s, hf] + 1)
                            mm(CW[:, :], sel[:, j - SHARED[s], :], cwT[:, :], start=True, stop=True).then_inc(cw_full, 1)
                    if j >= DOWN_LAG:
                        j -= DOWN_LAG
                        n = at["G"]["moe", s, hf, j]
                        w = n - g_other(s)
                        pe.wait_ge(al_ready, w + 1)
                        if j == 0:
                            m = at["Y"][s, 2 * hf]
                            if m:
                                pe.wait_ge(y_read, m)
                        for t in range(TH):
                            for p_, (a_, b_) in enumerate(((ah, wh), (al, wh), (ah, wl))):
                                ins = mm(Y[t // NT][:, (t % NT) * D:(t % NT + 1) * D], a_[:, w % NA, t * P:(t + 1) * P],
                                         b_[:, w % NS_, 2 * KD * P:], start=(j == 0 and t % NT == 0 and p_ == 0),
                                         stop=(j == last - 1 and p_ == 2), skip_group_check=True)
                        ins.then_inc(w_used, 1)
                elif kind == "din":
                    b, j = i
                    if PAIRS * b + j < beside_c:
                        pe.wait_ge(mix_in, 96)
                        bk, full = t_bank("din", s, b, j), t_full
                    else:
                        bk, full = a_bank("din", s, b, j), a_full
                    pe.wait_ge(t_read, at["T"]["lt", s, b] + 1)
                    for h in range(2):
                        ct = 2 * j + h
                        for k in range(KD):
                            ins = mm(bk[:, h * L:(h + 1) * L], win[:, k, ct * P:(ct + 1) * P],
                                     xnT_of(s)[:, k, b * L:(b + 1) * L], start=(k == 0), stop=(k == KD - 1))
                    ins.then_inc(full, 1)
                elif kind == "dz":
                    bk = v_bank("dz", s, i)
                    for k in range(KD):
                        ins = mm(bk[:, :], xnT_of(s)[:, k, i * P:(i + 1) * P], win[:, k, CONV:CONV + DI],
                                 start=(k == 0), stop=(k == KD - 1))
                    ins.then_inc(v_full, 1)
                elif kind == "dt_in":
                    bk = t_bank("dt_in", s, i)
                    pe.wait_ge(t_read, at["T"]["lt", s, B - 1] + 1)
                    for u in range(NU):
                        for k in range(KD):
                            ins = mm(bk[:, u * NV:(u + 1) * NV], xnT_of(s)[:, k, u * P:(u + 1) * P],
                                     win[:, k, CONV + DI:], start=(k == 0), stop=(k == KD - 1))
                    ins.then_inc(t_full, 1)
                elif kind == "acum":
                    pe.wait_ge(dt_ready, 1)
                    for k in range(2):
                        bk = t_bank("acum", s, k)
                        mm(bk[:, :], tri[:, k, :], t_max, start=True, stop=True).then_inc(t_full, 1)
                elif kind == "at":
                    bk = t_bank("at", s, i)
                    pe.wait_ge(ap_ready, 1)
                    for h in range(2):
                        ins = tr(bk[:, :].bitcast(BF16)[0:RA, h * P:(h + 1) * P],
                                 ap_[:, i, 2 * h:2 * h + 2, :, :].rearrange("p j m g -> p (j m g)"), identb[:, :])
                    ins.then_inc(t_full, 1)
                elif kind == "xt":
                    b, c = divmod(i, NT)
                    pe.wait_ge(xs_ready, (CT // 2) * (b + 1))
                    for part in range(2 if c == 0 else 1):
                        bk = a_bank("xt", s, i, part)
                        for k in range(4):
                            ins = tr(bk[:, k * P:(k + 1) * P], xs[:, b % 2, 4 * part + k, c * P:(c + 1) * P], ident[:, :])
                        ins.then_inc(a_full, 1)
                elif kind == "cb":
                    b, c = divmod(i, NT)
                    banks = [v_bank("cb", s, i, par) for par in range(2)]
                    for g2_ in range(NG // 2):
                        for par in range(2):
                            rows = slice(NS * par, NS * par + NS)
                            ins = mm(banks[par][:, g2_ * P:(g2_ + 1) * P], xs[rows, b % 2, 4 + g2_, c * P:(c + 1) * P],
                                     xs[rows, b % 2, 8 + g2_, c * P:(c + 1) * P], start=True, stop=True)
                            if g2_ == NG // 2 - 1:
                                ins.then_inc(v_full, 1)
                elif kind == "ssd":
                    u, hg = i
                    if hg == 0:
                        if u == 0:
                            pe.wait_ge(hot_in, 64)
                        pe.wait_ge(rows_landed, 16 * 6 * (u + 1))
                    bk = a_bank("ssd", s, u, hg)
                    mm(bk[:, :], identb[:, :], maskt[:, :].unsqueeze(1).to_broadcast([P, HG, P]),
                       start=True, stop=False, skip_group_check=True)
                    mm(bk[:, :], rows_z[u % 2][:, hg, :], rows_s[u % 2][:, :, hg, :], start=False, stop=True,
                       skip_group_check=True).then_inc(a_full, 1)
                    k = NHG * u + hg - LAG
                    if k >= 0:
                        scan(s, *divmod(k, NHG))
                elif kind == "ssd_end":
                    for k in range(NHG * i - LAG, NHG * i):
                        scan(s, *divmod(k, NHG))
                elif kind == "state" and i % 2 == 0:
                    bk = t_bank("state", s, i)
                    pe.wait_ge(xd_ready, i // 2 + 1)
                    pe.wait_ge(a_read, at["A"]["xt", s, i, 1] + 1)
                    for g_ in range(NG):
                        lo = NS * (g_ % 2)
                        ins = mm(bk[lo:lo + NS, (g_ // 2) * NS:(g_ // 2 + 1) * NS], Bt[:, g_ * NS:(g_ + 1) * NS],
                                 XD[:, g_ * NS:(g_ + 1) * NS], start=True, stop=True)
                    ins.then_inc(t_full, 1)
                elif kind == "state":
                    b = i // NT
                    pe.wait_ge(t_read, at["T"]["state", s, i - 1] + 1)
                    banks = [v_bank("state", s, i, par) for par in range(2)]
                    for g2_ in range(NG // 2):
                        for par in range(2):
                            rows = slice(NS * par, NS * par + NS)
                            ins = mm(banks[par][:, g2_ * NS:(g2_ + 1) * NS], xs[rows, b % 2, 8 + g2_, P:L],
                                     stt[rows, g2_, :], start=True, stop=True)
                            if g2_ == NG // 2 - 1:
                                ins.then_inc(v_full, 1)
                elif kind == "dy_t":
                    bk = t_bank("dy_t", s, i)
                    pe.wait_ge(yf_ready, i + 1)
                    for k in range(DI // P):
                        ins = tr(bk[:, k * P:(k + 1) * P], yf[:, k * P:(k + 1) * P], ident[:, :])
                    ins.then_inc(t_full, 1)
                elif kind == "dy":
                    bk = v_bank("dy", s, i)
                    pe.wait_ge(t_read, at["T"]["dy_t", s, i] + 1)
                    for k in range(DI // P):
                        ins = mm(bk[:, 0:D], yfT[:, k, :], wout[:, k, :], start=(k == 0), stop=(k == DI // P - 1))
                    ins.then_inc(v_full, 1)

        @block.vector
        def _(dve):
            v = nc.vector
            own = [0]

            def link(ins):
                own[0] += 1
                ins.then_inc(dv, 1)
                dve.wait_ge(dv, own[0])

            dve.wait_ge(x_in, 64)
            for kind, s, i in steps:
                if kind == "ln":
                    n = ln_index(s, i)
                    c = n % 2
                    if first[s]:
                        dve.wait_ge(*added(stages[first[s] - 1], i))
                    for t in range(NT):
                        link(v.bn_stats(stats[:, c, t, :], x[:, NT * i + t, :]))
                    for t in range(NT):
                        link(v.bn_aggr(mv[:, c, t, :], stats[:, c, t, :]))
                    v.tensor_scalar(ve[:, c, :], mv[:, c, :, 1], EPS, None, ALU.add).then_inc(ve_ready, 1)
                    dve.wait_ge(rstd_ready, n + 1)
                    if s != "E":
                        m = n - 2
                        if m >= 0 and stages[m // B] != "E":
                            dve.wait_ge(t_full, at["T"]["lt", stages[m // B], m % B] + 1)
                    for t in range(NT):
                        ins = v.tensor_scalar(xn_of(s, i)[:, t, :], x[:, NT * i + t, :], mv[:, c, t, 0:1], rstd[:, c, t:t + 1],
                                              ALU.subtract, ALU.mult)
                    ins.then_inc(xn_ready, 1)
                elif kind == "qkv_split":
                    i, t = i
                    k = attn_index(s, i)
                    nk = NKV if s == "A" else NH
                    wide = NH * HD + nk * HD
                    if k:
                        dve.wait_ge(v_copied, NT * (k - 1) + t + 1)
                    q_ = qf[:, t, 0:wide]
                    if s == "A":
                        if k == 0:
                            dve.wait_ge(attn_in, 80)
                        n = at["V"]["qkv_mm", s, i, t]
                        dve.wait_ge(v_full, n + 1)
                        v.tensor_tensor(qf[:, t, 0:384], V[n % 2][:, 0:384], bqkv[:, :], ALU.add).then_inc(v_read, 1)
                        dve.wait_ge(v_read, n + 1)
                        v.tensor_tensor(q_, q_, rope[:, t, :], ALU.mult).then_inc(qk_ready, 1)
                    else:
                        if k % B == 0:
                            dve.wait_ge(ctx_in, 32)
                        if i == 0 and begun_in_d:
                            dve.wait_ge(xs_ready, PAIRS * B)
                            dve.wait_ge(v_read, at["V"]["state", "D", NT * (B - 1) - 1, 1] + 1)
                            dve.wait_ge(t_full, at["T"]["lt", "D", B - 1] + 1)
                        dve.wait_ge(xn_ready, ln_index(s, i) + 1)
                        v.tensor_scalar(qf[:, t, 0:D], xn_of(s, i)[:, t, :], QSCALE, None, ALU.mult)
                        v.tensor_copy(qf[:, t, D:2 * D], ctxn[:, NT * i + t, :]).then_inc(qk_ready, 1)
                    dve.wait_ge(qk_ready, NT * k + t + 1)
                    if k:
                        dve.wait_ge(a_full, stack_end(k - 1, t) + 1)
                    st = stk[:, t]
                    heads = NH + nk
                    q3 = q_.rearrange("p (h w) -> p h w", w=HD)
                    r3 = rounded_off(s, i)[:, 0:wide].rearrange("p (h w) -> p h w", w=HD)
                    link(v.tensor_copy(st[:, 0:heads, 0, :], q3))
                    link(v.tensor_tensor(r3, q3, st[:, 0:heads, 0, :], ALU.subtract))
                    link(v.tensor_copy(st[:, 0:heads, 5, :], r3))
                    v.tensor_tensor(st[:, NH:heads, 3, :], r3[:, NH:heads], st[:, NH:heads, 5, :],
                                    ALU.subtract).then_inc(parts_ready, 1)
                elif kind == "q_rest":
                    i, t = i
                    st = stk[:, t]
                    r3 = rounded_off(s, i)[:, 0:NH * HD].rearrange("p (h w) -> p h w", w=HD)
                    v.tensor_tensor(st[:, 0:NH, 4, :], r3[:, 0:NH], st[:, 0:NH, 5, :], ALU.subtract)
                    v.tensor_copy(st[:, 0:NH, 1:4:2, :], st[:, 0:NH, 0, :].unsqueeze(2).to_broadcast([P, NH, 2, HD]))
                    v.tensor_copy(st[:, 0:NH, 2, :], st[:, 0:NH, 5, :]).then_inc(q_stacked, 1)
                elif kind == "stack_t":
                    k = attn_index(s, i)
                    if k >= 2:
                        dve.wait_ge(pv_used, 8 * (k - 1))
                    for t in range(NT):
                        for j in (1,) if s == "A" else (1, 3):
                            n = at["V"]["stack_t", s, i, t, j]
                            dve.wait_ge(v_full, n + 1)
                            v.tensor_copy((QT if j < 2 else KT)[0:KQ, k % 2, NH // 2:, t * P:(t + 1) * P],
                                          V[n % 2][:, :].bitcast(BF16)[0:KQ, :].rearrange("p (h q) -> p h q", h=NH // 2)
                                          ).then_inc(v_read, 1)
                elif kind == "s":
                    b, j = i
                    n = at["V"]["s", s, b, j]
                    dve.wait_ge(v_full, n + 1)
                    q, h0, heads = (0, 4 * j, 4) if j < 4 else (1, 2 * (j - 4), 2)
                    v.tensor_reduce(nM[:, q, h0:h0 + heads], V[n % 2][:, :].rearrange("p (h k) -> p h k", h=heads),
                                    AX.X, ALU.max, negate=True).then_inc(v_read, 1)
                elif kind == "m_split":
                    k = attn_index(s, i)
                    dve.wait_ge(v_read, at["V"]["s", s, i, NB - 1] + 1)
                    if k:
                        dve.wait_ge(t_full, at["T"]["m_t", attns[(k - 1) // B], (k - 1) % B] + 1)
                    link(v.tensor_copy(mp[:, :, 0, :], nM))
                    v.tensor_tensor(mp[:, :, 1, :], nM, mp[:, :, 0, :], ALU.subtract).then_inc(mp_ready, 1)
                elif kind == "y_t" and s != "D":
                    b, q = i
                    k = attn_index(s, b)
                    n = at["V"]["y_t", s, i]
                    dve.wait_ge(v_full, n + 1)
                    o3 = V[n % 2][:, :].rearrange("p (h w) -> p h w", w=VW)
                    link(v.reciprocal(rs[:, q, :].unsqueeze(2), o3[:, :, HD:HD + 1]))
                    if s == "A" and q == 0 and b >= 2:
                        dve.wait_ge(t_full, at["T"]["o_t", s, b - 2] + 1)
                    v.tensor_tensor(y[:, k % 2, q, :].rearrange("p (h w) -> p h w", w=HD), o3[:, :, 0:HD],
                                    rs[:, q, :].unsqueeze(2).to_broadcast([P, NH, HD]), ALU.mult).then_inc(v_read, 1)
                elif kind == "o":
                    k = attn_index(s, i)
                    xb = x[:, NT * i:NT * i + NT, :]
                    if s == "A":
                        n = at["V"]["o", s, i]
                        dve.wait_ge(v_full, n + 1)
                        tmp = y[:, k % 2]
                        v.tensor_tensor(tmp, V[n % 2][:, :].rearrange("p (t d) -> p t d", t=NT),
                                        bo[:, :].unsqueeze(1).to_broadcast([P, NT, D]), ALU.add).then_inc(v_read, 1)
                        dve.wait_ge(v_read, n + 1)
                    else:
                        dve.wait_ge(v_read, at["V"]["y_t", s, (i, 1)] + 1)
                    v.tensor_tensor(xb, xb, y[:, k % 2], ALU.add).then_inc(attn_added, 1)
                elif kind == "tokens":
                    dve.wait_ge(tok_in, 16)
                    link(v.tensor_copy(tokf, tok32))
                    for e in range(1, E0):
                        ins = v.tensor_scalar(mask[:, e, :], tokf, float(PER_EXPERT * e), None, ALU.is_ge)
                    link(ins)
                    link(v.tensor_scalar(mask[:, 0, :], mask[:, 1, :], -1.0, 1.0, ALU.mult, ALU.add))
                    for e in range(1, E0 - 1):
                        ins = v.tensor_tensor(mask[:, e, :], mask[:, e, :], mask[:, e + 1, :], ALU.subtract)
                        ins.then_inc(mask_ready, 1)
                        dve.wait_ge(mask_ready, e)
                elif kind == "b_mask":
                    dve.wait_ge(t_read, at["T"]["lt", s, 2 * i + 1] + 1)
                    for e in range(DVE_EXPERTS):
                        v.tensor_tensor(xm[:, i, e], xnT_of(s)[:, :, i * HALF:(i + 1) * HALF],
                                        mask[:, e, i * HALF:(i + 1) * HALF].unsqueeze(1).to_broadcast([P, KD, HALF]),
                                        ALU.mult).then_inc(xm_dve, 1)
                elif kind == "b_h":
                    if i:
                        dve.wait_ge(hm_dve, DVE_EXPERTS * i)
                        dve.wait_ge(hm_pool, (E0 - DVE_EXPERTS) * i)
                    for f in range(KD):
                        n = at["G"]["b_h", s, i, f]
                        dve.wait_ge(s_ready, n + 1)
                        v.tensor_tensor(hb[:, f, :], G[2 * (n % 2)][:, :], sg[:, n % 2, :], ALU.mult).then_inc(g_read, 1)
                    dve.wait_ge(g_read, n + 1)
                    for e in range(DVE_EXPERTS):
                        v.tensor_tensor(xm[:, i, e], hb[:, :, :],
                                        mask[:, e, i * HALF:(i + 1) * HALF].unsqueeze(1).to_broadcast([P, KD, HALF]),
                                        ALU.mult).then_inc(hm_dve, 1)
                elif kind == "b_y":
                    dve.wait_ge(y_full, at["Y"][s, i] + 1)
                    xb = x[:, NT * i:NT * i + NT, :]
                    v.tensor_tensor(xb, xb, Y[i % 2][:, :].rearrange("p (t d) -> p t d", t=NT), ALU.add).then_inc(y_read, 1)
                elif kind == "moe_y":
                    for b in range(2):
                        dve.wait_ge(w_used, (SHARED[s] + ROUTED) * (i + 1) + (w_all("C") if s == "F" and "C" in first else 0))
                        xb = x[:, NT * (2 * i + b):NT * (2 * i + b) + NT, :]
                        v.tensor_tensor(xb, xb, Y[b][:, :].rearrange("p (t d) -> p t d", t=NT), ALU.add).then_inc(y_read, 1)
                elif kind == "gate":
                    h = moe_half(s, i)
                    if h == 0:
                        dve.wait_ge(gate_in, 48)
                    dve.wait_ge(t_read, at["T"]["gate", s, i] + 1)
                    wide = [P, TH, NE]
                    link(v.tensor_reduce(gs[:, :], lg[:, :, :], AX.X, ALU.max))
                    v.tensor_tensor(g1[:, :, :], lg[:, :, :], gs[:, :].unsqueeze(2).to_broadcast(wide),
                                    ALU.subtract).then_inc(gsub_ready, 1)
                    dve.wait_ge(gexp_ready, h + 1)
                    link(v.tensor_reduce(gs[:, :], g2[:, :, :], AX.X, ALU.add))
                    link(v.reciprocal(gs[:, :], gs[:, :]))
                    link(v.tensor_tensor(g1[:, :, :], g2[:, :, :], gs[:, :].unsqueeze(2).to_broadcast(wide), ALU.mult))
                    for t in range(TH):
                        link(v.max(top[:, t, :], g1[:, t, :]))
                        link(v.max_index(topi[:, t, :], top[:, t, :], g1[:, t, :]))
                    link(v.tensor_copy(topf[:, :, :], topi[:, :, 0:2]))
                    io = iota[:, :].unsqueeze(1).to_broadcast(wide)
                    link(v.tensor_tensor(g2[:, :, :], io, topf[:, :, 0:1].to_broadcast(wide), ALU.is_equal))
                    link(v.tensor_tensor(lg[:, :, :], io, topf[:, :, 1:2].to_broadcast(wide), ALU.is_equal))
                    link(v.tensor_tensor(g2[:, :, :], g2[:, :, :], lg[:, :, :], ALU.add))
                    link(v.tensor_tensor(g1[:, :, :], g1[:, :, :], g2[:, :, :], ALU.mult))
                    if s == "C":
                        link(v.tensor_reduce(gs[:, :], g1[:, :, :], AX.X, ALU.add))
                        link(v.tensor_scalar(gs[:, :], gs[:, :], 1e-20, None, ALU.add))
                        link(v.reciprocal(gs[:, :], gs[:, :]))
                        link(v.tensor_tensor(g1[:, :, :], g1[:, :, :], gs[:, :].unsqueeze(2).to_broadcast(wide), ALU.mult))
                    link(v.tensor_copy(cwp[:, :, 0, :], g1[:, :, :]))
                    link(v.tensor_tensor(g2[:, :, :], g1[:, :, :], cwp[:, :, 0, :], ALU.subtract))
                    link(v.tensor_copy(cwp[:, :, 1, :], g2[:, :, :]))
                    v.tensor_tensor(cwp[:, :, 2, :], g2[:, :, :], cwp[:, :, 1, :], ALU.subtract).then_inc(cwp_ready, 1)
                elif kind == "moe" and i[1] < SHARED[s] + ROUTED:
                    hf, j = i
                    n = at["G"]["moe", s, hf, j]
                    w = n - g_other(s)
                    dve.wait_ge(u_full, w + 1)
                    dve.wait_ge(s_ready, n + 1)
                    v.tensor_tensor(act_[:, w % 2, :], G[2 * (n % 2) + 1][:, :], sg_moe[:, n % 2, :], ALU.mult).then_inc(g_read, 1)
                    if j >= SHARED[s]:
                        m = at["W"]["moe", s, hf, j]
                        dve.wait_ge(cw_full, m + 1)
                        dve.wait_ge(g_read, n + 1)
                        v.tensor_tensor(act_[:, w % 2, :], act_[:, w % 2, :], CW[:, :], ALU.mult).then_inc(cw_read, 1)
                elif kind == "a_split":
                    hf, j = i
                    w = at["G"]["moe", s, hf, j] - g_other(s)
                    dve.wait_ge(ah_ready, w + 1)
                    v.tensor_tensor(al[:, w % NA, :], act_[:, w % 2, :], ah[:, w % NA, :], ALU.subtract).then_inc(al_ready, 1)
                elif kind == "d_init":
                    before_d(dve)
                    dve.wait_ge(mix_in, 96)
                    dve.wait_ge(raw_cleared, 1)
                    link(v.tensor_scalar(convw[:, :, :], convw[:, :, :], 0.5, None, ALU.mult))
                    v.tensor_scalar(zb[:, :], zb[:, :], 0.5, None, ALU.mult).then_inc(halved, 1)
                elif kind == "tap":
                    b, j, k = i
                    m = b * (CT // 2) + j
                    if k == 1:
                        if m < beside_c:
                            dve.wait_ge(t_read, at["T"]["din", s, b, j] + 1)
                        else:
                            dve.wait_ge(a_read, at["A"]["din", s, b, j] + 1)
                    else:
                        dve.wait_ge(conv_done, (KS - 1) * m + k - 1)
                    for h in range(2):
                        ct = 2 * j + h
                        o = xs[:, b % 2, ct, :]
                        ins = v.scalar_tensor_tensor(o, raw[:, m % NRAW, h, KS - 1 - k:KS - 1 - k + L],
                                                     convw[:, ct, KS - 1 - k:KS - k], o, ALU.mult, ALU.add)
                    ins.then_inc(conv_done, 1)
                elif kind == "silu":
                    b, j = i
                    m = b * (CT // 2) + j
                    if m < beside_c:
                        continue
                    dve.wait_ge(tanh_ready, m - beside_c + 1)
                    half = xs[:, b % 2, 2 * j:2 * j + 2, :]
                    v.scalar_tensor_tensor(half, raw[:, m % NRAW, :, KS - 1:], 1.0, half, ALU.add, ALU.mult
                                           ).then_inc(xs_ready, 1)
                elif kind == "dz":
                    n = at["V"]["dz", s, i]
                    dve.wait_ge(v_full, n + 1)
                    v.scalar_tensor_tensor(zt[:, :], V[n % 2][:, :], 0.5, zb[:, :], ALU.mult, ALU.add).then_inc(v_read, 1)
                elif kind == "zs":
                    dve.wait_ge(z_tanh, i + 1)
                    v.scalar_tensor_tensor(zs[:, i % 2, :], zs[:, i % 2, :], 1.0, zt[:, :], ALU.add, ALU.mult
                                           ).then_inc(zs_ready, 1)
                elif kind == "dt":
                    dve.wait_ge(w_ready, 2)
                    dve.wait_ge(ln_ready, 2)
                    link(v.tensor_tensor(t_rest, t_u, t_1u, ALU.mult))
                    link(v.tensor_tensor(t_rest, t_rest, t_abs, ALU.add))
                    v.tensor_tensor(t_max, t_rest, t_max, ALU.add).then_inc(dt_ready, 1)
                elif kind == "ddt":
                    dve.wait_ge(dt_ready, 1)
                    link(v.reciprocal(ddt, t_max))
                    v.tensor_tensor(ddt.rearrange("p (u h) -> p u h", h=NV), ddt.rearrange("p (u h) -> p u h", h=NV),
                                    dskip[:, :].unsqueeze(1).to_broadcast([P, NU, NV]), ALU.mult).then_inc(dt_ready, 1)
                elif kind == "acum":
                    dve.wait_ge(t_read, at["T"]["acum", s, 1] + 1)
                    cum, last, d3 = (a.rearrange("p (b c h) -> p b c h", c=NT, h=NV) for a in (t_a, t_u, dec))
                    v.tensor_tensor(d3[:, :, 0], last[:, :, 0], cum[:, :, 0], ALU.subtract)
                    v.tensor_copy(d3[:, :, 1], cum[:, :, 1]).then_inc(decin_ready, 1)
                    cum, rest = (a.rearrange("p (u j g) -> p u j g", j=HG, g=NHG) for a in (t_a, t_rest))
                    link(v.tensor_copy(ap_[:, :, :, 0, :], cum))
                    link(v.tensor_tensor(rest, cum, ap_[:, :, :, 0, :], ALU.subtract))
                    link(v.tensor_copy(ap_[:, :, :, 1, :], rest))
                    v.tensor_tensor(ap_[:, :, :, 2, :], rest, ap_[:, :, :, 1, :], ALU.subtract).then_inc(ap_ready, 1)
                elif kind == "cb":
                    for par in range(2):
                        n = at["V"]["cb", s, i, par]
                        dve.wait_ge(v_full, n + 1)
                        v.tensor_copy(CBs[:, i % 2, par:NG:2, :], V[n % 2][:, :].rearrange("p (g s) -> p g s", g=NG // 2)
                                      ).then_inc(v_read, 1)
                elif kind == "ssd":
                    u, hg = i
                    if hg == 0:
                        dve.wait_ge(v_read, at["V"]["cb", s, u, 1] + 1)
                    dve.wait_ge(a_read, at["A"]["ssd", s, u, hg] + 1)
                    m = M[:, (NHG * u + hg) % NM, :].rearrange("p (h z) -> p h z", h=HG)
                    v.tensor_tensor(m, m, CBs[:, u % 2, hg // (NV // NG):NG:NG // HG, :], ALU.mult).then_inc(m_ready, 1)
                elif kind == "state" and i % 2 == 1:
                    dve.wait_ge(dec_ready, 1)
                    for par in range(2):
                        n = at["V"]["state", s, i, par]
                        dve.wait_ge(v_full, n + 1)
                        o4 = yo.rearrange("p (g j h w) -> p g j h w", g=NG // 2, j=2, w=PV)[:, :, par]
                        e4 = dec[:, i * NV:(i + 1) * NV].rearrange("p (g j h) -> p g j h", g=NG // 2, j=2)[:, :, par]
                        for g_ in range(NG // 2):
                            ins = v.tensor_tensor(o4[:, g_], V[n % 2][:, g_ * NS:(g_ + 1) * NS].rearrange("p (h w) -> p h w", w=PV),
                                                  e4[:, g_].unsqueeze(2).to_broadcast([P, NG, PV]), ALU.mult)
                        ins.then_inc(v_read, 1)
                elif kind == "y_t":
                    b, c = divmod(i, NT)
                    n = at["V"]["y_t", s, i]
                    dve.wait_ge(v_full, n + 1)
                    dve.wait_ge(du_ready, i + 1)
                    dve.wait_ge(zs_ready, i + 1)
                    if i:
                        dve.wait_ge(t_full, at["T"]["dy_t", s, i - 1] + 1)

                    def quarters(a):
                        return a.rearrange("p (j g f) -> p g j f", j=HG, g=HG)

                    v.tensor_tensor(quarters(yf), V[n % 2][:, :].rearrange("p (g j f) -> p g j f", g=HG, j=HG),
                                    quarters(Du[:, c, :]), ALU.add).then_inc(v_read, 1)
                    dve.wait_ge(v_read, n + 1)
                    if c:
                        dve.wait_ge(v_read, at["V"]["state", s, i, 1] + 1)
                        link(v.tensor_tensor(yf, yf, yo, ALU.add))
                    v.tensor_tensor(yf, yf, zs[:, c, :], ALU.mult).then_inc(yf_ready, 1)
                elif kind == "dy":
                    n = at["V"]["dy", s, i]
                    dve.wait_ge(v_full, n + 1)
                    v.tensor_tensor(x[:, i, :], x[:, i, :], V[n % 2][:, 0:D], ALU.add).then_inc(v_read, 1)


def layouts(inp):

    bf = np.dtype("bfloat16")
    f = {k: np.asarray(v) for k, v in inp.items()}

    def rows(w):
        return np.ascontiguousarray(w.reshape(-1, P, w.shape[1]).transpose(1, 0, 2))

    arrays = {
        "x": f["x"], "ctx": f["ctx_2048"], "tok": f["itok_BxS_13_99985"].reshape(-1),
        "wqkv": rows(np.concatenate([f["L0_attn_Wq"].T, f["L0_attn_Wk"].T, f["L0_attn_Wv"].T], 1)),
        "wo": rows(f["L0_attn_Wo"].T),
        "bqkv": np.concatenate([f["L0_attn_bq"], f["L0_attn_bk"], f["L0_attn_bv"]]),
        "bo": f["L0_attn_bo"],
        "ctxT": np.ascontiguousarray(f["ctx_2048"].transpose(0, 2, 1).reshape(E0, KD, P, D).transpose(2, 0, 1, 3)),
        "gatew": np.ascontiguousarray(np.stack([rows(f["L0_ffn_gate_w"].T), rows(f["L1_ffn_gate_weight"].T)], 1)),
        "win": rows(f["L1_attn_in_proj_w"].T),
        "wout": rows(f["L1_attn_out_proj_w"].T),
        "zb": f["L1_attn_z_bias"], "dskip": f["L1_attn_D"],
        "convw": np.ascontiguousarray(np.concatenate([f["L1_attn_conv1d_weight"][:, 0, :], f["L1_attn_conv1d_bias"][:, None]],
                                                     1).reshape(CT, P, KS + 1).transpose(1, 0, 2)),
    }

    def tiles(gate, up, down, n):
        pad = n * P - gate.shape[1]
        gate, up = (np.pad(w, ((0, 0), (0, pad))).reshape(KD, P, n, P) for w in (gate, up))
        down = np.pad(down, ((0, pad), (0, 0))).reshape(n, P, D)
        gu = np.stack([gate, up], 3).transpose(2, 1, 0, 3, 4).reshape(n, P, 2 * KD * P)
        return np.concatenate([gu, down], 2)

    def cat(w):
        return w.transpose(1, 0, 2).reshape(D, NE * FE)

    w1 = f["L0_ffn_w1"]
    arrays["wC"] = np.ascontiguousarray(np.concatenate([
        tiles(f["L0_ffn_sw1"].T, f["L0_ffn_sw2"].T, f["L0_ffn_sw3"].T, SHARED["C"]),
        tiles(cat(w1[:, :, :FE]), cat(w1[:, :, FE:]), f["L0_ffn_w2"].reshape(NE * FE, D), ROUTED)]))
    gu, sgu = f["L1_ffn_gate_up_weights"], f["L1_ffn_shared_gate_up"]
    fs = sgu.shape[0] // 2
    arrays["wF"] = np.ascontiguousarray(np.concatenate([
        tiles(sgu[:fs].T, sgu[fs:].T, f["L1_ffn_shared_down"].T, SHARED["F"]),
        tiles(cat(gu[:, :FE].transpose(0, 2, 1)), cat(gu[:, FE:].transpose(0, 2, 1)),
              f["L1_ffn_down_weights"].transpose(0, 2, 1).reshape(NE * FE, D), ROUTED)]))

    i = np.arange(P)
    arrays["ident"] = np.eye(P, dtype=np.float32)
    arrays["identb"] = np.eye(P).astype(bf)
    later = np.where(i[None, :] > i[:, None], NEG, 0.0)
    arrays["masks"] = np.concatenate([np.zeros((P, P)), later], 1).astype(bf)
    arrays["maskt"] = later.T.astype(bf)
    inv = np.float32(10000.0) ** (np.float32(-2.0) * np.arange(HD // 2, dtype=np.float32) / np.float32(HD))
    theta = np.arange(L, dtype=np.float32)[:, None] * inv[None, :].astype(np.float32)
    turn = np.tile(np.cos(theta) + np.sin(theta), (1, 2)).astype(np.float32)
    arrays["rope"] = np.ascontiguousarray(np.concatenate([np.tile(turn * np.float32(QSCALE), (1, NH)), np.tile(turn, (1, NKV))],
                                                         1).reshape(NT, P, -1).transpose(1, 0, 2))
    expert = (np.arange(ROUTED * P) // FE).reshape(ROUTED, P)
    arrays["sel"] = np.tile(expert[None] == np.arange(NE)[:, None, None], (3, 1, 1)).astype(bf)
    arrays["iota"] = np.tile(np.arange(NE, dtype=np.float32), (P, 1))
    arrays["tri"] = np.stack([-(i[:, None] <= i[None, :]).astype(np.float32), -np.ones((P, P), np.float32)], 1)
    arrays["onehot"] = np.tile(np.repeat(np.eye(HG), 3, 0)[:, :, None, None], (1, 1, NHG, P)).astype(bf)
    arrays["ones3"] = np.ones((3, NHG, P)).astype(bf)
    return arrays


def kernel(**inputs):
    import concourse.bacc as bacc
    from concourse.bass_utils import run_bass_kernel_spmd

    nc = bacc.Bacc("TRN2", target_bir_lowering=False, num_devices=1)
    arrays = layouts(inputs)
    args = {n: nc.dram_tensor(f"in_{n}", a.shape, mybir.dt.from_np(a.dtype), kind="ExternalInput").ap()
            for n, a in arrays.items()}
    out = nc.dram_tensor("out_x", (B, L, D), F32, kind="ExternalOutput").ap()
    decoder(nc, args, out)
    r = run_bass_kernel_spmd(nc, [{f"in_{n}": a for n, a in arrays.items()}], core_ids=[0])
    return r.results[0]["out_x"]
```
